# Optimizing a Trainium2 kernel written in Bass

```python
import numpy as np
import jax
import jax.numpy as jnp

def _softmax(x, axis=-1):
    return jax.nn.softmax(x, axis=axis)

def _gelu(x):
    return jax.nn.gelu(x, approximate=True)

def _silu(x):
    return jax.nn.silu(x)

def _sigmoid(x):
    return jax.nn.sigmoid(x)

def _layernorm(x, axis=-1, eps=1e-05):
    m = jnp.mean(x, axis=axis, keepdims=True)
    v = jnp.var(x, axis=axis, keepdims=True)
    return (x - m) / jnp.sqrt(v + eps)

def _scatter_add(tgt, idx, src, axis=0):
    return tgt.at[idx].add(src)

def _segment_sum(src, seg, n):
    return jax.ops.segment_sum(src, seg, n)
kernel_name = 'mk_xattn_seq_d4_seqx_r8_ce85ab'

def setup_inputs(seed: int=0):
    np.random.seed(seed)
    _w = jnp.asarray

    def _rec_inputs():
        import jax
        import jax.numpy as jnp
        _rk = jax.random.key(seed)
        x = 7.22e-05 + 1 * jax.random.normal(jax.random.fold_in(_rk, 1), (8, 128, 256), jnp.float32)
        _lenS = 128 - jax.random.randint(jax.random.fold_in(_rk, 7), (8,), 0, max(1, 128 // 4) + 1, jnp.int32)
        _lenS2 = 128 - jax.random.randint(jax.random.fold_in(_rk, 8), (8,), 0, max(1, 128 // 4) + 1, jnp.int32)
        _ctx_2048P = jax.random.normal(jax.random.fold_in(_rk, 11), (8, 16, 256), jnp.float32)
        _ctx_2048c = jax.random.dirichlet(jax.random.fold_in(_rk, 511), 0.3 * jnp.ones((16,), jnp.float32), (8, 128))
        _ctx_2048t = jnp.einsum('bsk,bkd->bsd', _ctx_2048c, _ctx_2048P)
        _ctx_2048t = _ctx_2048t * jax.lax.rsqrt(jnp.mean(jnp.square(_ctx_2048t)) + 1e-12) * 0.953939
        ctx_2048 = 4.13588e-05 + 0.999923 * (_ctx_2048t + 0.3 * jax.random.normal(jax.random.fold_in(_rk, 611), (8, 128, 256), jnp.float32))
        _validS = jnp.arange(128)[None, :] < _lenS[:, None]
        _validS2 = jnp.arange(128)[None, :] < _lenS2[:, None]
        _causal = jnp.tril(jnp.ones((128, 128), dtype=bool))
        mask_Bx1xSxS2_ff0 = jnp.where(jnp.ones((8, 1, 128, 128), dtype=bool), 0.0, -1000000000.0).astype(jnp.float32)
        mask_1x1xSxS2_fc1 = jnp.where(jnp.broadcast_to(_validS2[0:1, None, None, :], (1, 1, 128, 128)), 1.0, 0.0).astype(jnp.float32)
        mask_Bx1xSxS2_ff1 = jnp.where(jnp.ones((8, 1, 128, 128), dtype=bool), 1.0, 0.0).astype(jnp.float32)
        return (x, ctx_2048, mask_Bx1xSxS2_ff0, mask_1x1xSxS2_fc1, mask_Bx1xSxS2_ff1)
    x, ctx_2048, mask_Bx1xSxS2_ff0, mask_1x1xSxS2_fc1, mask_Bx1xSxS2_ff1 = _rec_inputs()

    def _L0_xattn_setup():
        import jax, jax.numpy as jnp
        import numpy as np
        H = 256
        NH = 32
        KVH = 8
        HD = H // NH
        GROUPS = NH // KVH
        EPS = 1e-06
        B, L, S = (4, 128, 128)

        def _gqa_forward(hidden_state, encoder_hidden_state, encoder_attention_mask, Wq, bq, Wk, bk, Wv, bv, Wo, bo, gamma, beta):
            b, l, _ = hidden_state.shape
            s = encoder_hidden_state.shape[1]
            q = hidden_state @ Wq + bq
            k = encoder_hidden_state @ Wk + bk
            v = encoder_hidden_state @ Wv + bv
            q = q.reshape(b, l, KVH, GROUPS, HD).transpose(0, 2, 3, 1, 4)
            k = k.reshape(b, s, KVH, HD).transpose(0, 2, 1, 3)
            v = v.reshape(b, s, KVH, HD).transpose(0, 2, 1, 3)
            scale = 1.0 / jnp.sqrt(jnp.asarray(HD, q.dtype))
            scores = jnp.einsum('bkgld,bksd->bkgls', q, k) * scale
            scores = scores + encoder_attention_mask[:, :, None, :, :]
            attn = jax.nn.softmax(scores, axis=-1)
            out = jnp.einsum('bkgls,bksd->bkgld', attn, v)
            out = out.transpose(0, 3, 1, 2, 4).reshape(b, l, H)
            out = out @ Wo + bo
            x = out + hidden_state
            mu = jnp.mean(x, axis=-1, keepdims=True)
            var = jnp.var(x, axis=-1, keepdims=True)
            return (x - mu) * jax.lax.rsqrt(var + EPS) * gamma + beta
        key = jax.random.key(seed)
        ks = jax.random.split(key, 12)
        sd = 0.02
        return {'hidden_state': jax.random.normal(ks[0], (B, L, H), jnp.float32), 'encoder_hidden_state': jax.random.normal(ks[1], (B, S, H), jnp.float32), 'encoder_attention_mask': jnp.zeros((B, 1, L, S), jnp.float32), 'Wq': jax.random.normal(ks[2], (H, H), jnp.float32) * sd, 'bq': jnp.zeros((H,), jnp.float32), 'Wk': jax.random.normal(ks[3], (H, KVH * HD), jnp.float32) * sd, 'bk': jnp.zeros((KVH * HD,), jnp.float32), 'Wv': jax.random.normal(ks[4], (H, KVH * HD), jnp.float32) * sd, 'bv': jnp.zeros((KVH * HD,), jnp.float32), 'Wo': jax.random.normal(ks[5], (H, H), jnp.float32) * sd, 'bo': jnp.zeros((H,), jnp.float32), 'gamma': jnp.ones((H,), jnp.float32), 'beta': jnp.zeros((H,), jnp.float32)}
    _L0_xattn_all = _L0_xattn_setup()
    _L0_xattn_in = {k: v for k, v in _L0_xattn_all.items() if k in ('Wq', 'bq', 'Wk', 'bk', 'Wv', 'bv', 'Wo', 'bo', 'gamma', 'beta')}
    del _L0_xattn_all

    def _L1_xattn_setup():
        import jax, jax.numpy as jnp
        import numpy as np
        B, C, CI, N = (16, 128, 64, 256)
        EPS = 1e-05

        def _conv1x1(w, b, x):
            return jnp.einsum('oc,bcn->bon', w, x) + b[None, :, None]
        key = jax.random.key(seed)
        ks = jax.random.split(key, 14)
        s = 0.02
        return {'x': jax.random.normal(ks[0], (B, C, N), jnp.float32), 'x_2': jax.random.normal(ks[1], (B, C, N), jnp.float32), 'theta_w': jax.random.normal(ks[2], (CI, C), jnp.float32) * s, 'theta_b': jax.random.normal(ks[3], (CI,), jnp.float32) * s, 'phi_w': jax.random.normal(ks[4], (CI, C), jnp.float32) * s, 'phi_b': jax.random.normal(ks[5], (CI,), jnp.float32) * s, 'g_w': jax.random.normal(ks[6], (CI, C), jnp.float32) * s, 'g_b': jax.random.normal(ks[7], (CI,), jnp.float32) * s, 'w_w': jax.random.normal(ks[8], (C, CI), jnp.float32) * s, 'w_b': jax.random.normal(ks[9], (C,), jnp.float32) * s, 'bn_gamma': jax.random.normal(ks[10], (C,), jnp.float32), 'bn_beta': jax.random.normal(ks[11], (C,), jnp.float32), 'bn_mean': jax.random.normal(ks[12], (C,), jnp.float32), 'bn_var': jax.random.uniform(ks[13], (C,), jnp.float32, 0.5, 1.5)}
    _L1_xattn_all = _L1_xattn_setup()
    _L1_xattn_in = {k: v for k, v in _L1_xattn_all.items() if k in ('theta_w', 'theta_b', 'phi_w', 'phi_b', 'g_w', 'g_b', 'w_w', 'w_b', 'bn_gamma', 'bn_beta', 'bn_mean', 'bn_var')}
    del _L1_xattn_all

    def _L2_xattn_setup():
        import jax, jax.numpy as jnp
        import numpy as np
        B, Q, S1, S2 = (4, 32, 256, 256)
        D, H, K, F = (256, 16, 128, 1024)
        LN_EPS = 1e-05

        def _layer_norm(x, scale, offset):
            mu = jnp.mean(x, axis=-1, keepdims=True)
            var = jnp.var(x, axis=-1, keepdims=True)
            return (x - mu) * jax.lax.rsqrt(var + LN_EPS) * scale + offset

        def _cross_attention(q_in, kv_in, wq, bq, wk, bk, wv, bv, wo, bo, bias_k, bias_v):
            b, q_len, _ = q_in.shape
            t = kv_in.shape[1]
            qh = (q_in @ wq + bq).reshape(b, q_len, H, K)
            kh = (kv_in @ wk + bk).reshape(b, t, H, K)
            vh = (kv_in @ wv + bv).reshape(b, t, H, K)
            kh = jnp.concatenate([kh, jnp.broadcast_to(bias_k, (b, 1, H, K))], axis=1)
            vh = jnp.concatenate([vh, jnp.broadcast_to(bias_v, (b, 1, H, K))], axis=1)
            scale = jnp.sqrt(jnp.asarray(K, q_in.dtype))
            logits = jnp.einsum('bqhk,bthk->bhqt', qh, kh) / scale
            weights = jax.nn.softmax(logits, axis=-1)
            ctx = jnp.einsum('bhqt,bthk->bqhk', weights, vh).reshape(b, q_len, H * K)
            return ctx @ wo + bo

        def _forward(x, xf_1, xf_2, ln1_scale, ln1_offset, wq1, bq1, wk1, bk1, wv1, bv1, wo1, bo1, bias_k1, bias_v1, ln2_scale, ln2_offset, wq2, bq2, wk2, bk2, wv2, bv2, wo2, bo2, bias_k2, bias_v2, ln_mlp_scale, ln_mlp_offset, w_fc1, b_fc1, w_fc2, b_fc2):
            res = x
            h = _layer_norm(x, ln1_scale, ln1_offset)
            x = res + _cross_attention(h, xf_1, wq1, bq1, wk1, bk1, wv1, bv1, wo1, bo1, bias_k1, bias_v1)
            res = x
            h = _layer_norm(x, ln2_scale, ln2_offset)
            x = res + _cross_attention(h, xf_2, wq2, bq2, wk2, bk2, wv2, bv2, wo2, bo2, bias_k2, bias_v2)
            h = _layer_norm(x, ln_mlp_scale, ln_mlp_offset)
            h = jax.nn.gelu(h @ w_fc1 + b_fc1, approximate=False) @ w_fc2 + b_fc2
            return x + h
        key = jax.random.key(seed)
        ks = iter(jax.random.split(key, 64))

        def rn(shape, s=0.02):
            return jax.random.normal(next(ks), shape, jnp.float32) * s
        inp = {'x': rn((B, Q, D), 1.0), 'xf_1': rn((B, S1, D), 1.0), 'xf_2': rn((B, S2, D), 1.0)}
        for i in (1, 2):
            inp[f'ln{i}_scale'] = jnp.ones((D,), jnp.float32)
            inp[f'ln{i}_offset'] = jnp.zeros((D,), jnp.float32)
            inp[f'wq{i}'] = rn((D, H * K))
            inp[f'bq{i}'] = jnp.zeros((H * K,), jnp.float32)
            inp[f'wk{i}'] = rn((D, H * K))
            inp[f'bk{i}'] = jnp.zeros((H * K,), jnp.float32)
            inp[f'wv{i}'] = rn((D, H * K))
            inp[f'bv{i}'] = jnp.zeros((H * K,), jnp.float32)
            inp[f'wo{i}'] = rn((H * K, D))
            inp[f'bo{i}'] = jnp.zeros((D,), jnp.float32)
            inp[f'bias_k{i}'] = rn((1, 1, H, K))
            inp[f'bias_v{i}'] = rn((1, 1, H, K))
        inp['ln_mlp_scale'] = jnp.ones((D,), jnp.float32)
        inp['ln_mlp_offset'] = jnp.zeros((D,), jnp.float32)
        inp['w_fc1'] = rn((D, F))
        inp['b_fc1'] = jnp.zeros((F,), jnp.float32)
        inp['w_fc2'] = rn((F, D))
        inp['b_fc2'] = jnp.zeros((D,), jnp.float32)
        return inp
    _L2_xattn_all = _L2_xattn_setup()
    _L2_xattn_in = {k: v for k, v in _L2_xattn_all.items() if k in ('ln1_scale', 'ln1_offset', 'wq1', 'bq1', 'wk1', 'bk1', 'wv1', 'bv1', 'wo1', 'bo1', 'bias_k1', 'bias_v1', 'ln2_scale', 'ln2_offset', 'wq2', 'bq2', 'wk2', 'bk2', 'wv2', 'bv2', 'wo2', 'bo2', 'bias_k2', 'bias_v2', 'ln_mlp_scale', 'ln_mlp_offset', 'w_fc1', 'b_fc1', 'w_fc2', 'b_fc2')}
    del _L2_xattn_all

    def _L3_xattn_setup():
        import jax, jax.numpy as jnp
        import numpy as np
        H = 256
        NH = 16
        HD = H // NH
        EPS = 1e-05

        def gelu(x):
            return 0.5 * x * (1.0 + jnp.tanh(0.7978845608028654 * x * (1.0 + 0.044715 * x * x)))

        def layernorm(x, scale, bias):
            m = jnp.mean(x, axis=-1, keepdims=True)
            v = jnp.mean(jnp.square(x - m), axis=-1, keepdims=True)
            return (x - m) * jax.lax.rsqrt(v + EPS) * scale + bias

        def split_heads(x):
            b, s, _ = x.shape
            return x.reshape(b, s, NH, HD).transpose(0, 2, 1, 3)

        def merge_heads(x):
            b, nh, s, hd = x.shape
            return x.transpose(0, 2, 1, 3).reshape(b, s, nh * hd)

        def attention(q, k, v, mask):
            scores = jnp.einsum('bhqd,bhkd->bhqk', q, k) / jnp.sqrt(jnp.float32(HD))
            scores = scores * mask - 10000.0 * (1.0 - mask)
            probs = jax.nn.softmax(scores, axis=-1)
            return jnp.einsum('bhqk,bhkd->bhqd', probs, v)
        key = jax.random.key(seed)
        ks = jax.random.split(key, 16)
        b, s, t = (2, 128, 128)
        w = lambda k, i, o: jax.random.normal(k, (i, o), jnp.float32) * 0.02
        inp = {'hidden_states': jax.random.normal(ks[0], (b, s, H), jnp.float32), 'encoder_states': jax.random.normal(ks[1], (b, t, H), jnp.float32), 'ltor_mask': jnp.tril(jnp.ones((1, 1, s, s), jnp.float32)), 'cross_mask': jnp.ones((b, 1, s, t), jnp.float32), 'ln1_s': jnp.ones((H,), jnp.float32), 'ln1_b': jnp.zeros((H,), jnp.float32), 'w_qkv': w(ks[2], H, 3 * H), 'b_qkv': jnp.zeros((3 * H,), jnp.float32), 'w_ao': w(ks[3], H, H), 'b_ao': jnp.zeros((H,), jnp.float32), 'ln2_s': jnp.ones((H,), jnp.float32), 'ln2_b': jnp.zeros((H,), jnp.float32), 'w_q': w(ks[4], H, H), 'b_q': jnp.zeros((H,), jnp.float32), 'w_kv': w(ks[5], H, 2 * H), 'b_kv': jnp.zeros((2 * H,), jnp.float32), 'w_co': w(ks[6], H, H), 'b_co': jnp.zeros((H,), jnp.float32), 'ln3_s': jnp.ones((H,), jnp.float32), 'ln3_b': jnp.zeros((H,), jnp.float32), 'w1': w(ks[7], H, 4 * H), 'b1': jnp.zeros((4 * H,), jnp.float32), 'w2': w(ks[8], 4 * H, H), 'b2': jnp.zeros((H,), jnp.float32)}
        return inp
    _L3_xattn_all = _L3_xattn_setup()
    _L3_xattn_in = {k: v for k, v in _L3_xattn_all.items() if k in ('ln1_s', 'ln1_b', 'w_qkv', 'b_qkv', 'w_ao', 'b_ao', 'ln2_s', 'ln2_b', 'w_q', 'b_q', 'w_kv', 'b_kv', 'w_co', 'b_co', 'ln3_s', 'ln3_b', 'w1', 'b1', 'w2', 'b2')}
    del _L3_xattn_all
    return {'x': x, 'ctx_2048': ctx_2048, 'mask_Bx1xSxS2_ff0': mask_Bx1xSxS2_ff0, 'mask_1x1xSxS2_fc1': mask_1x1xSxS2_fc1, 'mask_Bx1xSxS2_ff1': mask_Bx1xSxS2_ff1, 'L0_xattn_Wq': _L0_xattn_in['Wq'], 'L0_xattn_bq': _L0_xattn_in['bq'], 'L0_xattn_Wk': _L0_xattn_in['Wk'], 'L0_xattn_bk': _L0_xattn_in['bk'], 'L0_xattn_Wv': _L0_xattn_in['Wv'], 'L0_xattn_bv': _L0_xattn_in['bv'], 'L0_xattn_Wo': _L0_xattn_in['Wo'], 'L0_xattn_bo': _L0_xattn_in['bo'], 'L0_xattn_gamma': _L0_xattn_in['gamma'], 'L0_xattn_beta': _L0_xattn_in['beta'], 'L1_xattn_theta_w': _L1_xattn_in['theta_w'], 'L1_xattn_theta_b': _L1_xattn_in['theta_b'], 'L1_xattn_phi_w': _L1_xattn_in['phi_w'], 'L1_xattn_phi_b': _L1_xattn_in['phi_b'], 'L1_xattn_g_w': _L1_xattn_in['g_w'], 'L1_xattn_g_b': _L1_xattn_in['g_b'], 'L1_xattn_w_w': _L1_xattn_in['w_w'], 'L1_xattn_w_b': _L1_xattn_in['w_b'], 'L1_xattn_bn_gamma': _L1_xattn_in['bn_gamma'], 'L1_xattn_bn_beta': _L1_xattn_in['bn_beta'], 'L1_xattn_bn_mean': _L1_xattn_in['bn_mean'], 'L1_xattn_bn_var': _L1_xattn_in['bn_var'], 'L2_xattn_ln1_scale': _L2_xattn_in['ln1_scale'], 'L2_xattn_ln1_offset': _L2_xattn_in['ln1_offset'], 'L2_xattn_wq1': _L2_xattn_in['wq1'], 'L2_xattn_bq1': _L2_xattn_in['bq1'], 'L2_xattn_wk1': _L2_xattn_in['wk1'], 'L2_xattn_bk1': _L2_xattn_in['bk1'], 'L2_xattn_wv1': _L2_xattn_in['wv1'], 'L2_xattn_bv1': _L2_xattn_in['bv1'], 'L2_xattn_wo1': _L2_xattn_in['wo1'], 'L2_xattn_bo1': _L2_xattn_in['bo1'], 'L2_xattn_bias_k1': _L2_xattn_in['bias_k1'], 'L2_xattn_bias_v1': _L2_xattn_in['bias_v1'], 'L2_xattn_ln2_scale': _L2_xattn_in['ln2_scale'], 'L2_xattn_ln2_offset': _L2_xattn_in['ln2_offset'], 'L2_xattn_wq2': _L2_xattn_in['wq2'], 'L2_xattn_bq2': _L2_xattn_in['bq2'], 'L2_xattn_wk2': _L2_xattn_in['wk2'], 'L2_xattn_bk2': _L2_xattn_in['bk2'], 'L2_xattn_wv2': _L2_xattn_in['wv2'], 'L2_xattn_bv2': _L2_xattn_in['bv2'], 'L2_xattn_wo2': _L2_xattn_in['wo2'], 'L2_xattn_bo2': _L2_xattn_in['bo2'], 'L2_xattn_bias_k2': _L2_xattn_in['bias_k2'], 'L2_xattn_bias_v2': _L2_xattn_in['bias_v2'], 'L2_xattn_ln_mlp_scale': _L2_xattn_in['ln_mlp_scale'], 'L2_xattn_ln_mlp_offset': _L2_xattn_in['ln_mlp_offset'], 'L2_xattn_w_fc1': _L2_xattn_in['w_fc1'], 'L2_xattn_b_fc1': _L2_xattn_in['b_fc1'], 'L2_xattn_w_fc2': _L2_xattn_in['w_fc2'], 'L2_xattn_b_fc2': _L2_xattn_in['b_fc2'], 'L3_xattn_ln1_s': _L3_xattn_in['ln1_s'], 'L3_xattn_ln1_b': _L3_xattn_in['ln1_b'], 'L3_xattn_w_qkv': _L3_xattn_in['w_qkv'], 'L3_xattn_b_qkv': _L3_xattn_in['b_qkv'], 'L3_xattn_w_ao': _L3_xattn_in['w_ao'], 'L3_xattn_b_ao': _L3_xattn_in['b_ao'], 'L3_xattn_ln2_s': _L3_xattn_in['ln2_s'], 'L3_xattn_ln2_b': _L3_xattn_in['ln2_b'], 'L3_xattn_w_q': _L3_xattn_in['w_q'], 'L3_xattn_b_q': _L3_xattn_in['b_q'], 'L3_xattn_w_kv': _L3_xattn_in['w_kv'], 'L3_xattn_b_kv': _L3_xattn_in['b_kv'], 'L3_xattn_w_co': _L3_xattn_in['w_co'], 'L3_xattn_b_co': _L3_xattn_in['b_co'], 'L3_xattn_ln3_s': _L3_xattn_in['ln3_s'], 'L3_xattn_ln3_b': _L3_xattn_in['ln3_b'], 'L3_xattn_w1': _L3_xattn_in['w1'], 'L3_xattn_b1': _L3_xattn_in['b1'], 'L3_xattn_w2': _L3_xattn_in['w2'], 'L3_xattn_b2': _L3_xattn_in['b2']}

def reference(x, ctx_2048, mask_Bx1xSxS2_ff0, mask_1x1xSxS2_fc1, mask_Bx1xSxS2_ff1, L0_xattn_Wq, L0_xattn_bq, L0_xattn_Wk, L0_xattn_bk, L0_xattn_Wv, L0_xattn_bv, L0_xattn_Wo, L0_xattn_bo, L0_xattn_gamma, L0_xattn_beta, L1_xattn_theta_w, L1_xattn_theta_b, L1_xattn_phi_w, L1_xattn_phi_b, L1_xattn_g_w, L1_xattn_g_b, L1_xattn_w_w, L1_xattn_w_b, L1_xattn_bn_gamma, L1_xattn_bn_beta, L1_xattn_bn_mean, L1_xattn_bn_var, L2_xattn_ln1_scale, L2_xattn_ln1_offset, L2_xattn_wq1, L2_xattn_bq1, L2_xattn_wk1, L2_xattn_bk1, L2_xattn_wv1, L2_xattn_bv1, L2_xattn_wo1, L2_xattn_bo1, L2_xattn_bias_k1, L2_xattn_bias_v1, L2_xattn_ln2_scale, L2_xattn_ln2_offset, L2_xattn_wq2, L2_xattn_bq2, L2_xattn_wk2, L2_xattn_bk2, L2_xattn_wv2, L2_xattn_bv2, L2_xattn_wo2, L2_xattn_bo2, L2_xattn_bias_k2, L2_xattn_bias_v2, L2_xattn_ln_mlp_scale, L2_xattn_ln_mlp_offset, L2_xattn_w_fc1, L2_xattn_b_fc1, L2_xattn_w_fc2, L2_xattn_b_fc2, L3_xattn_ln1_s, L3_xattn_ln1_b, L3_xattn_w_qkv, L3_xattn_b_qkv, L3_xattn_w_ao, L3_xattn_b_ao, L3_xattn_ln2_s, L3_xattn_ln2_b, L3_xattn_w_q, L3_xattn_b_q, L3_xattn_w_kv, L3_xattn_b_kv, L3_xattn_w_co, L3_xattn_b_co, L3_xattn_ln3_s, L3_xattn_ln3_b, L3_xattn_w1, L3_xattn_b1, L3_xattn_w2, L3_xattn_b2):
    import jax
    import jax.numpy as jnp

    def _L0_xattn_ref(hidden_state, encoder_hidden_state, encoder_attention_mask, Wq, bq, Wk, bk, Wv, bv, Wo, bo, gamma, beta):
        import jax, jax.numpy as jnp
        import numpy as np
        H = 256
        NH = 32
        KVH = 8
        HD = H // NH
        GROUPS = NH // KVH
        EPS = 1e-06
        B, L, S = (4, 128, 128)

        def _gqa_forward(hidden_state, encoder_hidden_state, encoder_attention_mask, Wq, bq, Wk, bk, Wv, bv, Wo, bo, gamma, beta):
            b, l, _ = hidden_state.shape
            s = encoder_hidden_state.shape[1]
            q = hidden_state @ Wq + bq
            k = encoder_hidden_state @ Wk + bk
            v = encoder_hidden_state @ Wv + bv
            q = q.reshape(b, l, KVH, GROUPS, HD).transpose(0, 2, 3, 1, 4)
            k = k.reshape(b, s, KVH, HD).transpose(0, 2, 1, 3)
            v = v.reshape(b, s, KVH, HD).transpose(0, 2, 1, 3)
            scale = 1.0 / jnp.sqrt(jnp.asarray(HD, q.dtype))
            scores = jnp.einsum('bkgld,bksd->bkgls', q, k) * scale
            scores = scores + encoder_attention_mask[:, :, None, :, :]
            attn = jax.nn.softmax(scores, axis=-1)
            out = jnp.einsum('bkgls,bksd->bkgld', attn, v)
            out = out.transpose(0, 3, 1, 2, 4).reshape(b, l, H)
            out = out @ Wo + bo
            x = out + hidden_state
            mu = jnp.mean(x, axis=-1, keepdims=True)
            var = jnp.var(x, axis=-1, keepdims=True)
            return (x - mu) * jax.lax.rsqrt(var + EPS) * gamma + beta
        return _gqa_forward(hidden_state, encoder_hidden_state, encoder_attention_mask, Wq, bq, Wk, bk, Wv, bv, Wo, bo, gamma, beta)

    def _L1_xattn_ref(x, x_2, theta_w, theta_b, phi_w, phi_b, g_w, g_b, w_w, w_b, bn_gamma, bn_beta, bn_mean, bn_var):
        import jax, jax.numpy as jnp
        import numpy as np
        B, C, CI, N = (16, 128, 64, 256)
        EPS = 1e-05

        def _conv1x1(w, b, x):
            return jnp.einsum('oc,bcn->bon', w, x) + b[None, :, None]
        g_x = _conv1x1(g_w, g_b, x_2).transpose(0, 2, 1)
        theta_x = _conv1x1(theta_w, theta_b, x).transpose(0, 2, 1)
        phi_x = _conv1x1(phi_w, phi_b, x_2)
        W = jnp.einsum('bnc,bcm->bnm', theta_x, phi_x) / phi_x.shape[-1]
        y = jnp.einsum('bnm,bmc->bnc', W, g_x).transpose(0, 2, 1)
        wy = _conv1x1(w_w, w_b, y)
        inv_std = jax.lax.rsqrt(bn_var + EPS)
        wy = bn_gamma[None, :, None] * (wy - bn_mean[None, :, None]) * inv_std[None, :, None] + bn_beta[None, :, None]
        return wy + x

    def _L2_xattn_ref(x, xf_1, xf_2, ln1_scale, ln1_offset, wq1, bq1, wk1, bk1, wv1, bv1, wo1, bo1, bias_k1, bias_v1, ln2_scale, ln2_offset, wq2, bq2, wk2, bk2, wv2, bv2, wo2, bo2, bias_k2, bias_v2, ln_mlp_scale, ln_mlp_offset, w_fc1, b_fc1, w_fc2, b_fc2):
        import jax, jax.numpy as jnp
        import numpy as np
        B, Q, S1, S2 = (4, 32, 256, 256)
        D, H, K, F = (256, 16, 128, 1024)
        LN_EPS = 1e-05

        def _layer_norm(x, scale, offset):
            mu = jnp.mean(x, axis=-1, keepdims=True)
            var = jnp.var(x, axis=-1, keepdims=True)
            return (x - mu) * jax.lax.rsqrt(var + LN_EPS) * scale + offset

        def _cross_attention(q_in, kv_in, wq, bq, wk, bk, wv, bv, wo, bo, bias_k, bias_v):
            b, q_len, _ = q_in.shape
            t = kv_in.shape[1]
            qh = (q_in @ wq + bq).reshape(b, q_len, H, K)
            kh = (kv_in @ wk + bk).reshape(b, t, H, K)
            vh = (kv_in @ wv + bv).reshape(b, t, H, K)
            kh = jnp.concatenate([kh, jnp.broadcast_to(bias_k, (b, 1, H, K))], axis=1)
            vh = jnp.concatenate([vh, jnp.broadcast_to(bias_v, (b, 1, H, K))], axis=1)
            scale = jnp.sqrt(jnp.asarray(K, q_in.dtype))
            logits = jnp.einsum('bqhk,bthk->bhqt', qh, kh) / scale
            weights = jax.nn.softmax(logits, axis=-1)
            ctx = jnp.einsum('bhqt,bthk->bqhk', weights, vh).reshape(b, q_len, H * K)
            return ctx @ wo + bo

        def _forward(x, xf_1, xf_2, ln1_scale, ln1_offset, wq1, bq1, wk1, bk1, wv1, bv1, wo1, bo1, bias_k1, bias_v1, ln2_scale, ln2_offset, wq2, bq2, wk2, bk2, wv2, bv2, wo2, bo2, bias_k2, bias_v2, ln_mlp_scale, ln_mlp_offset, w_fc1, b_fc1, w_fc2, b_fc2):
            res = x
            h = _layer_norm(x, ln1_scale, ln1_offset)
            x = res + _cross_attention(h, xf_1, wq1, bq1, wk1, bk1, wv1, bv1, wo1, bo1, bias_k1, bias_v1)
            res = x
            h = _layer_norm(x, ln2_scale, ln2_offset)
            x = res + _cross_attention(h, xf_2, wq2, bq2, wk2, bk2, wv2, bv2, wo2, bo2, bias_k2, bias_v2)
            h = _layer_norm(x, ln_mlp_scale, ln_mlp_offset)
            h = jax.nn.gelu(h @ w_fc1 + b_fc1, approximate=False) @ w_fc2 + b_fc2
            return x + h
        return _forward(x, xf_1, xf_2, ln1_scale, ln1_offset, wq1, bq1, wk1, bk1, wv1, bv1, wo1, bo1, bias_k1, bias_v1, ln2_scale, ln2_offset, wq2, bq2, wk2, bk2, wv2, bv2, wo2, bo2, bias_k2, bias_v2, ln_mlp_scale, ln_mlp_offset, w_fc1, b_fc1, w_fc2, b_fc2)

    def _L3_xattn_ref(hidden_states, encoder_states, ltor_mask, cross_mask, ln1_s, ln1_b, w_qkv, b_qkv, w_ao, b_ao, ln2_s, ln2_b, w_q, b_q, w_kv, b_kv, w_co, b_co, ln3_s, ln3_b, w1, b1, w2, b2):
        import jax, jax.numpy as jnp
        import numpy as np
        H = 256
        NH = 16
        HD = H // NH
        EPS = 1e-05

        def gelu(x):
            return 0.5 * x * (1.0 + jnp.tanh(0.7978845608028654 * x * (1.0 + 0.044715 * x * x)))

        def layernorm(x, scale, bias):
            m = jnp.mean(x, axis=-1, keepdims=True)
            v = jnp.mean(jnp.square(x - m), axis=-1, keepdims=True)
            return (x - m) * jax.lax.rsqrt(v + EPS) * scale + bias

        def split_heads(x):
            b, s, _ = x.shape
            return x.reshape(b, s, NH, HD).transpose(0, 2, 1, 3)

        def merge_heads(x):
            b, nh, s, hd = x.shape
            return x.transpose(0, 2, 1, 3).reshape(b, s, nh * hd)

        def attention(q, k, v, mask):
            scores = jnp.einsum('bhqd,bhkd->bhqk', q, k) / jnp.sqrt(jnp.float32(HD))
            scores = scores * mask - 10000.0 * (1.0 - mask)
            probs = jax.nn.softmax(scores, axis=-1)
            return jnp.einsum('bhqk,bhkd->bhqd', probs, v)
        ln_out = layernorm(hidden_states, ln1_s, ln1_b)
        qkv = ln_out @ w_qkv + b_qkv
        q, k, v = jnp.split(qkv, 3, axis=-1)
        ctx = merge_heads(attention(split_heads(q), split_heads(k), split_heads(v), ltor_mask))
        attn_out = ctx @ w_ao + b_ao
        x = hidden_states + attn_out
        ln_out = layernorm(x, ln2_s, ln2_b)
        q = ln_out @ w_q + b_q
        kv = encoder_states @ w_kv + b_kv
        k, v = jnp.split(kv, 2, axis=-1)
        ctx = merge_heads(attention(split_heads(q), split_heads(k), split_heads(v), cross_mask))
        cross_out = ctx @ w_co + b_co
        x = x + cross_out
        ln_out = layernorm(x, ln3_s, ln3_b)
        mlp_out = gelu(ln_out @ w1 + b1) @ w2 + b2
        return x + mlp_out
    x = _L0_xattn_ref(x, ctx_2048, mask_Bx1xSxS2_ff0, L0_xattn_Wq, L0_xattn_bq, L0_xattn_Wk, L0_xattn_bk, L0_xattn_Wv, L0_xattn_bv, L0_xattn_Wo, L0_xattn_bo, L0_xattn_gamma, L0_xattn_beta)
    x = _L1_xattn_ref(x, ctx_2048, L1_xattn_theta_w, L1_xattn_theta_b, L1_xattn_phi_w, L1_xattn_phi_b, L1_xattn_g_w, L1_xattn_g_b, L1_xattn_w_w, L1_xattn_w_b, L1_xattn_bn_gamma, L1_xattn_bn_beta, L1_xattn_bn_mean, L1_xattn_bn_var)
    x = _L2_xattn_ref(x, ctx_2048, ctx_2048, L2_xattn_ln1_scale, L2_xattn_ln1_offset, L2_xattn_wq1, L2_xattn_bq1, L2_xattn_wk1, L2_xattn_bk1, L2_xattn_wv1, L2_xattn_bv1, L2_xattn_wo1, L2_xattn_bo1, L2_xattn_bias_k1, L2_xattn_bias_v1, L2_xattn_ln2_scale, L2_xattn_ln2_offset, L2_xattn_wq2, L2_xattn_bq2, L2_xattn_wk2, L2_xattn_bk2, L2_xattn_wv2, L2_xattn_bv2, L2_xattn_wo2, L2_xattn_bo2, L2_xattn_bias_k2, L2_xattn_bias_v2, L2_xattn_ln_mlp_scale, L2_xattn_ln_mlp_offset, L2_xattn_w_fc1, L2_xattn_b_fc1, L2_xattn_w_fc2, L2_xattn_b_fc2)
    x = _L3_xattn_ref(x, ctx_2048, mask_1x1xSxS2_fc1, mask_Bx1xSxS2_ff1, L3_xattn_ln1_s, L3_xattn_ln1_b, L3_xattn_w_qkv, L3_xattn_b_qkv, L3_xattn_w_ao, L3_xattn_b_ao, L3_xattn_ln2_s, L3_xattn_ln2_b, L3_xattn_w_q, L3_xattn_b_q, L3_xattn_w_kv, L3_xattn_b_kv, L3_xattn_w_co, L3_xattn_b_co, L3_xattn_ln3_s, L3_xattn_ln3_b, L3_xattn_w1, L3_xattn_b1, L3_xattn_w2, L3_xattn_b2)
    return x

_drawn_inputs = setup_inputs


def setup_inputs(seed=0):
    import zlib

    import numpy as np

    out = dict(_drawn_inputs(seed))
    spreads = {'L0_xattn_bq': (0.0, 0.8),
     'L0_xattn_bk': (0.0, 2.0),
     'L0_xattn_bv': (0.0, 0.411),
     'L0_xattn_bo': (0.0, 0.1),
     'L0_xattn_gamma': (1.0, 0.2),
     'L0_xattn_beta': (0.0, 0.1),
     'L2_xattn_ln1_scale': (1.0, 0.6),
     'L2_xattn_ln1_offset': (0.0, 2.0),
     'L2_xattn_bq1': (0.0, 2.0),
     'L2_xattn_bk1': (0.0, 2.0),
     'L2_xattn_bv1': (0.0, 0.8),
     'L2_xattn_bo1': (0.0, 0.8),
     'L2_xattn_ln2_scale': (1.0, 0.6),
     'L2_xattn_ln2_offset': (0.0, 2.0),
     'L2_xattn_bq2': (0.0, 2.0),
     'L2_xattn_bk2': (0.0, 2.0),
     'L2_xattn_bv2': (0.0, 0.8),
     'L2_xattn_bo2': (0.0, 0.8),
     'L2_xattn_ln_mlp_scale': (1.0, 0.6),
     'L2_xattn_ln_mlp_offset': (0.0, 2.0),
     'L2_xattn_b_fc1': (0.0, 2.0),
     'L2_xattn_b_fc2': (0.0, 2.0),
     'L3_xattn_ln1_s': (1.0, 0.6),
     'L3_xattn_ln1_b': (0.0, 2.0),
     'L3_xattn_b_qkv': (0.0, 2.0),
     'L3_xattn_b_ao': (0.0, 2.0),
     'L3_xattn_ln2_s': (1.0, 0.6),
     'L3_xattn_ln2_b': (0.0, 2.0),
     'L3_xattn_b_q': (0.0, 2.0),
     'L3_xattn_b_kv': (0.0, 2.0),
     'L3_xattn_b_co': (0.0, 2.0),
     'L3_xattn_ln3_s': (1.0, 0.6),
     'L3_xattn_ln3_b': (0.0, 2.0),
     'L3_xattn_b1': (0.0, 2.0),
     'L3_xattn_b2': (0.0, 2.0)}
    factors = {'L0_xattn_Wq': 8.0,
     'L0_xattn_Wk': 8.0,
     'L1_xattn_theta_w': 8.0,
     'L1_xattn_theta_b': 8.0,
     'L1_xattn_phi_w': 8.0,
     'L1_xattn_phi_b': 8.0,
     'L1_xattn_g_w': 8.0,
     'L1_xattn_g_b': 8.0,
     'L1_xattn_w_w': 8.0,
     'L1_xattn_w_b': 90.189,
     'L2_xattn_wq1': 48.907,
     'L2_xattn_wk1': 48.652,
     'L2_xattn_bias_k1': 200.0,
     'L2_xattn_bias_v1': 200.0,
     'L2_xattn_wq2': 48.886,
     'L2_xattn_wk2': 48.43,
     'L2_xattn_bias_k2': 200.0,
     'L2_xattn_bias_v2': 200.0,
     'L3_xattn_w_qkv': 11.609,
     'L3_xattn_w_q': 64.0,
     'L2_xattn_wv1': 5.322,
     'L2_xattn_wo1': 5.167,
     'L2_xattn_wv2': 5.387,
     'L2_xattn_wo2': 5.129,
     'L2_xattn_w_fc1': 8.0,
     'L2_xattn_w_fc2': 6.816,
     'L3_xattn_w_ao': 3.965,
     'L3_xattn_w_kv': 8.0,
     'L3_xattn_w_co': 8.0,
     'L3_xattn_w1': 8.0,
     'L3_xattn_w2': 6.262}
    for name, (base, spread) in spreads.items():
        noise = np.random.default_rng([zlib.crc32(name.encode()), seed]).standard_normal(out[name].shape)
        drawn = base * np.exp(spread * noise) if base else spread * noise
        out[name] = jnp.asarray(drawn.astype(out[name].dtype))
    for name, factor in factors.items():
        out[name] = (out[name] * factor).astype(out[name].dtype)
    return out
```

```python
from contextlib import ExitStack

import concourse.bass as bass
from concourse import mybir

F32 = mybir.dt.float32
F32R = mybir.dt.float32r
ALU = mybir.AluOpType
ACT = mybir.ActivationFunctionType
X = mybir.AxisListType.X

P = 128
B = 8
S = 128
D = 256
KC = D // P
TOK = B * S
HALF = 512
NHALF = TOK // HALF


class Env:

    def __init__(self, nc):
        self.nc = nc


class Product:

    def __init__(self, lhs, rhs, n, out, bias):
        self.lhs, self.rhs, self.n, self.out, self.bias = lhs, rhs, n, out, bias


def make_env(nc, ctx):
    env = Env(nc)

    def scoped(stack):
        def sb(name, shape, dt=F32):
            return stack.enter_context(nc.sbuf_tensor(name, shape, dt))
        return sb

    env.scoped = scoped
    env.lasting_sem = lambda name: ctx.enter_context(nc.semaphore(name))
    env.stage_sems = []

    def sem(name):
        env.stage_sems.append(nc.alloc_semaphore(name=name))
        return env.stage_sems[-1]

    env.sem = sem
    env.bank = [ctx.enter_context(nc.psum_tensor(f"bank{i}", [P, 512], F32)) for i in range(8)]
    return env


def free_semaphores(env):
    env.nc.clear_and_free_semaphores(env.stage_sems)
    env.nc.all_engine_barrier()
    env.stage_sems = []


def f32_view(ap):
    return ap.bitcast(F32)


def split_product(pe, out, lhs, rhs, start, stop):
    n = len(lhs)
    for k in range(n):
        (lh, ll), (rh, rl) = lhs[k], rhs[k]
        pe.matmul(out, ll, rh, start=start and k == 0, stop=False)
        pe.matmul(out, lh, rl, start=False, stop=False)
        mm = pe.matmul(out, lh, rh, start=False, stop=stop and k == n - 1)
    return mm


def load_weights(env, sp, a, weights, sem):
    for name, dst in weights.items():
        k = a[name].shape[0] // P
        sp.dma_start(dst[:, :, :], a[name].rearrange("(c p) n -> p c n", c=k)).then_inc(sem, 16)


ROW_VECTORS = [
    ("L0_xattn_bq", 2), ("L1_xattn_w_b", 1), ("L1_xattn_bn_gamma", 1), ("L1_xattn_bn_beta", 1),
    ("L1_xattn_bn_mean", 1), ("L1_xattn_bn_var", 1),
    ("L2_xattn_ln1_scale", 2), ("L2_xattn_ln1_offset", 2),
    ("L2_xattn_bq1", 16), ("L2_xattn_bk1", 16), ("L2_xattn_bv1", 16),
    ("L2_xattn_bias_k1", 16), ("L2_xattn_bias_v1", 16),
    ("L3_xattn_ln1_s", 2), ("L3_xattn_ln1_b", 2), ("L3_xattn_b_qkv", 6),
    ("L3_xattn_ln2_s", 2), ("L3_xattn_ln2_b", 2), ("L3_xattn_b_q", 2), ("L3_xattn_b_kv", 4),
    ("L3_xattn_ln3_s", 2), ("L3_xattn_ln3_b", 2),
    ("L2_xattn_ln2_scale", 2), ("L2_xattn_ln2_offset", 2),
    ("L2_xattn_bq2", 16), ("L2_xattn_bk2", 16), ("L2_xattn_bv2", 16),
    ("L2_xattn_bias_k2", 16), ("L2_xattn_bias_v2", 16),
    ("L2_xattn_ln_mlp_scale", 2), ("L2_xattn_ln_mlp_offset", 2), ("L2_xattn_b_fc1", 8),
    ("L3_xattn_b1", 8),
    ("bk_of_heads", 2), ("bv_of_heads", 2),
]
FREE_VECTORS = ["L0_xattn_bo", "L0_xattn_gamma", "L0_xattn_beta", "L2_xattn_bo1", "L2_xattn_bo2",
                "L2_xattn_b_fc2", "L3_xattn_b_ao", "L3_xattn_b_co", "L3_xattn_b2"]
KV_HEADS, GROUP, HD0 = 8, 4, 8


def place_rows():
    at, tile, row = {}, 0, 0
    for name, n in ROW_VECTORS:
        if row + n > P:
            tile, row = tile + 1, 0
        at[name] = (tile, row, n)
        row += n
    used = [max(r + n for t, r, n in at.values() if t == k) for k in range(tile + 1)]
    return at, used


def flat(ap):
    if len(ap.shape) == 4:
        return ap.rearrange("a b c d -> (a b c d)")
    return ap


def setup(env, a):
    nc = env.nc
    N1 = D
    CI = 64
    with ExitStack() as stack:
        sb = env.scoped(stack)
        at, used = place_rows()
        rows = [sb(f"rows{t}", [P, P]) for t in range(len(used))]
        ctx_tok = sb("ctx_tok", [P, B, D])
        ctx_f = sb("ctx_f", [P, KC, TOK])
        pg_w = sb("pg_w", [P, P])
        w_w = sb("w_w", [P, CI])
        theta_w = sb("theta_w", [CI, P])
        theta_b = sb("theta_b", [CI, 2])
        pg_bias = sb("pg_bias", [P, P])
        pg_wT = sb("pg_wT", [P, P])
        w_wT = sb("w_wT", [CI, P])
        pg = sb("pg", [P, 2, KC, P])
        mT = sb("mT", [CI, 2, CI])
        pT = sb("pT", [CI, 2, P])
        nhalf1 = sb("nhalf1", [P, 1])
        inv = sb("inv", [P, 2])

        rows_in = env.sem("rows_in")
        ctx_in = env.sem("ctx_in")
        nl_in = env.sem("nl_in")
        pool_init = env.sem("pool_init")
        cols_up = env.sem("cols_up")
        cols_down = env.sem("cols_down")
        ctx_up = env.sem("ctx_up")
        ctx_down = env.sem("ctx_down")
        ctx_split = env.sem("ctx_split")
        nl_wt_up = env.sem("nl_wt_up")
        nl_wt_down = env.sem("nl_wt_down")
        pg_up, pg_down = env.sem("pg_up"), env.sem("pg_down")
        mt_up, mt_down = env.sem("mt_up"), env.sem("mt_down")
        pt_up, pt_down = env.sem("pt_up"), env.sem("pt_down")
        qt_up, qt_down = env.sem("qt_up"), env.sem("qt_down")
        bn = env.sem("bn")
        bn_pow = env.sem("bn_pow")
        block = stack.enter_context(nc.Block())

        @block.sync
        def _(sp):
            count = 0
            for name, (t, r, n) in at.items():
                if name in ("bk_of_heads", "bv_of_heads"):
                    src = a["L0_xattn_bk" if name == "bk_of_heads" else "L0_xattn_bv"]
                    for j in range(GROUP):
                        dst = rows[t][r:r + n, :].rearrange("c (g j d) -> c g j d", j=GROUP, d=HD0)
                        for c in range(n):
                            sp.dma_start(dst[c:c + 1, :, j, :],
                                         src.rearrange("(c g d) -> c g d", g=4, d=HD0)[c:c + 1])\
                                .then_inc(rows_in, 16)
                            count += 16
                    continue
                sp.dma_start(rows[t][r:r + n, :], flat(a[name]).rearrange("(r p) -> r p", p=P))\
                    .then_inc(rows_in, 16)
                count += 16
            env.rows_count = count
            sp.dma_start(env.x[:, :, :], a["x"].rearrange("b s d -> s b d")).then_inc(env.x_in, 16)
            for name, dst in (("Wq", env.w_q0), ("Wo", env.w_o0)):
                sp.dma_start(dst[:, :, :], a["L0_xattn_" + name].rearrange("(c p) n -> p c n", p=P))\
                    .then_inc(env.w0_in, 16)
            sp.dma_start(env.w_k0[:, :, :], a["L0_xattn_Wk"].rearrange("(c p) n -> p c n", p=P))\
                .then_inc(env.w0_in, 16)
            sp.dma_start(env.w_v0[:, :, :], a["L0_xattn_Wv"].rearrange("(c p) n -> p c n", p=P))\
                .then_inc(env.w0_in, 16)
            sp.dma_start(env.mask0[:, :, :], a["mask_Bx1xSxS2_ff0"].rearrange("b o q s -> q (b o) s"))\
                .then_inc(env.mask_in, 16)
            sp.dma_start(env.mask_self[:, 0, :], a["mask_1x1xSxS2_fc1"][0, 0]).then_inc(env.mask_in, 16)
            sp.dma_start(env.mask_cross[:, :, :], a["mask_Bx1xSxS2_ff1"].rearrange("b o q s -> q (b o) s"))\
                .then_inc(env.mask_in, 16)
            for name in FREE_VECTORS:
                sp.dma_start(env.free[name][:, :],
                             a[name].rearrange("(a n) -> a n", a=1).to_broadcast([P, D]))\
                    .then_inc(env.free_in, 16)
            load_weights(env, sp, a, env.w_ff2, env.ff2_in)

        @block.gpsimd
        def _(pool):
            pool.memset(env.ident[:, :], 0.0).then_inc(pool_init, 1)
            pool.wait_ge(pool_init, 1)
            pool.affine_select(out=env.ident[:, :], in_=env.ident[:, :], compare_op=ALU.not_equal,
                               fill=1.0, base=0, pattern=[[-1, P]], channel_multiplier=1)\
                .then_inc(pool_init, 1)
            pool.memset(env.nhalf[:, :], -0.5).then_inc(pool_init, 1)
            pool.memset(nhalf1[:, :], -0.5).then_inc(pool_init, 1)
            for mask, hd in ((env.head_mask8, 8), (env.head_mask16, 16)):
                n = P // hd
                pool.memset(mask[:, :], 1.0).then_inc(env.masks_made, 1)
            for k, (mask, hd) in enumerate(((env.head_mask8, 8), (env.head_mask16, 16))):
                n = P // hd
                pool.wait_ge(env.masks_made, 2 + 2 * k)
                pool.affine_select(out=mask[:, :], in_=mask[:, :], compare_op=ALU.is_ge, fill=0.0,
                                   base=0, pattern=[[-hd, n]], channel_multiplier=1)\
                    .then_inc(env.masks_made, 1)
                pool.wait_ge(env.masks_made, 3 + 2 * k)
                pool.affine_select(out=mask[:, :], in_=mask[:, :], compare_op=ALU.is_ge, fill=0.0,
                                   base=hd - 1, pattern=[[hd, n]], channel_multiplier=-1)\
                    .then_inc(env.masks_made, 1)
            pool.wait_ge(bn, 1)
            pool.tensor_tensor(inv[:, 1:2], inv[:, 0:1], nhalf1[:, :], ALU.pow).then_inc(bn_pow, 1)

        @block.tensor
        def _(pe):
            pe.wait_ge(pool_init, 2)
            pe.wait_ge(rows_in, env.rows_count)
            for t, n in enumerate(used):
                mm = pe.transpose(env.bank[0][:, P * t:P * t + n], rows[t][0:n, :], env.ident[0:n, 0:n])
            mm.then_inc(cols_up, 1)
            pe.wait_ge(nl_in, 16 * 7)
            pe.transpose(env.bank[1][:, 0:P], pg_w[:, :], env.ident[:, :])
            pe.transpose(env.bank[1][0:CI, P:2 * P], w_w[:, :], env.ident[:, :]).then_inc(nl_wt_up, 1)
            pe.wait_ge(ctx_in, 16)
            for c in range(KC):
                for half in range(NHALF):
                    n = c * NHALF + half
                    for k in range(4):
                        b = half * 4 + k
                        mm = pe.transpose(env.bank[2 + n][:, k * P:(k + 1) * P],
                                          ctx_tok[:, b, c * P:(c + 1) * P], env.ident[:, :])
                    mm.then_inc(ctx_up, 1)
            pe.wait_ge(nl_wt_down, 1)
            pe.wait_ge(cols_down, 1)
            pe.wait_ge(ctx_down, NHALF * KC)
            for b in range(B):
                if b >= 2:
                    pe.wait_ge(pg_down, b - 1)
                for c in range(KC):
                    mm = pe.matmul(env.bank[b % 2][:, c * P:(c + 1) * P], ctx_tok[:, b, c * P:(c + 1) * P],
                                   pg_wT[:, :], start=True, stop=True)
                mm.then_inc(pg_up, 1)
                pe.wait_ge(pg_down, b + 1)
                if b >= 1:
                    pe.wait_ge(mt_down, b)
                for c in range(KC):
                    mm = pe.matmul(env.bank[2][0:CI, 0:CI], pg[:, b % 2, c, CI:P], pg[:, b % 2, c, 0:CI],
                                   start=c == 0, stop=c == KC - 1)
                mm.then_inc(mt_up, 1)
                pe.wait_ge(mt_down, b + 1)
                if b >= 1:
                    pe.wait_ge(pt_down, b)
                pe.matmul(env.bank[3][0:CI, 0:P], mT[:, b % 2, :], w_wT[:, :], start=True, stop=True)\
                    .then_inc(pt_up, 1)
                pe.wait_ge(pt_down, b + 1)
                if b >= 1:
                    pe.wait_ge(qt_down, b)
                pe.matmul(env.bank[4][:, 0:P], theta_w[:, :], pT[:, b % 2, :], start=True, stop=True)
                pe.matmul(env.bank[4][:, P:P + 1], pT[:, b % 2, :], theta_b[:, 0:1], start=True, stop=True)\
                    .then_inc(qt_up, 1)

        @block.scalar
        def _(act):
            act.dma_start(pg_w[0:CI, :], a["L1_xattn_phi_w"]).then_inc(nl_in, 16)
            act.dma_start(pg_w[CI:P, :], a["L1_xattn_g_w"]).then_inc(nl_in, 16)
            act.dma_start(w_w[:, :], a["L1_xattn_w_w"]).then_inc(nl_in, 16)
            act.dma_start(theta_w[:, :], a["L1_xattn_theta_w"]).then_inc(nl_in, 16)
            with nc.allow_non_contiguous_dma(reason="64 values, one to a partition"):
                act.dma_start(theta_b[:, 0:1], a["L1_xattn_theta_b"].rearrange("(c a) -> c a", a=1))\
                    .then_inc(nl_in, 16)
            for k, name in enumerate(("phi_b", "g_b")):
                act.dma_start(pg_bias[:, k * CI:(k + 1) * CI],
                              a["L1_xattn_" + name].rearrange("(a n) -> a n", a=1).to_broadcast([P, CI]))\
                    .then_inc(nl_in, 16)
            act.dma_start(ctx_tok[:, :, :], a["ctx_2048"].rearrange("b s d -> s b d")).then_inc(ctx_in, 16)
            act.wait_ge(nl_wt_up, 1)
            act.activation(pg_wT[:, :], env.bank[1][:, 0:P], ACT.Copy)
            act.activation(w_wT[:, :], env.bank[1][0:CI, P:2 * P], ACT.Copy).then_inc(nl_wt_down, 1)
            for n in range(KC * NHALF):
                c, half = divmod(n, NHALF)
                act.wait_ge(ctx_up, n + 1)
                act.activation(ctx_f[:, c, half * HALF:(half + 1) * HALF], env.bank[2 + n][:, :], ACT.Copy)\
                    .then_inc(ctx_down, 1)
            for b in range(B):
                act.wait_ge(mt_up, b + 1)
                act.activation(mT[:, b % 2, :], env.bank[2][0:CI, 0:CI], ACT.Copy).then_inc(mt_down, 1)
                act.wait_ge(pt_up, b + 1)
                act.activation(pT[:, b % 2, :], env.bank[3][0:CI, 0:P], ACT.Copy, scale=1.0 / N1)\
                    .then_inc(pt_down, 1)
                act.wait_ge(qt_up, b + 1)
                act.activation(env.qT1[:, b, :], env.bank[4][:, 0:P + 1], ACT.Copy).then_inc(qt_down, 1)

        @block.vector
        def _(dve):
            dve.wait_ge(cols_up, 1)
            for t, n in enumerate(used):
                ins = dve.tensor_copy(env.cols[t][:, 0:n], env.bank[0][:, P * t:P * t + n])
            ins.then_inc(cols_down, 1)
            dve.wait_ge(cols_down, 1)
            dve.tensor_scalar(inv[:, 0:1], env.col("L1_xattn_bn_var"), 1e-5, None, ALU.add).then_inc(bn, 1)
            for n in range(KC * NHALF):
                c, half = divmod(n, NHALF)
                dve.wait_ge(ctx_down, n + 1)
                part = (slice(None), c, slice(half * HALF, (half + 1) * HALF))
                dve.tensor_copy(env.ctx_hi[part], ctx_f[part]).then_inc(ctx_split, 1)
                dve.wait_ge(ctx_split, n + 1)
                dve.tensor_tensor(env.ctx_lo[part], ctx_f[part], f32_view(env.ctx_hi[part]), ALU.subtract)
            for b in range(B):
                dve.wait_ge(pg_up, b + 1)
                if b >= 2:
                    dve.wait_ge(mt_up, b - 1)
                dve.tensor_tensor(pg[:, b % 2, :, :],
                                  env.bank[b % 2][:, 0:KC * P].rearrange("p (c n) -> p c n", n=P),
                                  pg_bias[:, :].unsqueeze(1).to_broadcast([P, KC, P]), ALU.add)\
                    .then_inc(pg_down, 1)
            dve.wait_ge(bn_pow, 1)
            dve.tensor_tensor(env.bn_scale[:, :], env.col("L1_xattn_bn_gamma"), inv[:, 1:2], ALU.mult)\
                .then_inc(bn, 1)
            dve.tensor_tensor(inv[:, 0:1], env.col("L1_xattn_w_b"), env.col("L1_xattn_bn_mean"), ALU.subtract)\
                .then_inc(bn, 1)
            dve.wait_ge(qt_down, B)
            dve.wait_ge(bn, 3)
            dve.tensor_scalar(env.bn_shift[:, :], env.qT1[:, :, P], inv[:, 0:1], env.bn_scale[:, 0:1],
                              ALU.add, ALU.mult).then_inc(bn, 1)
            dve.wait_ge(bn, 4)
            dve.tensor_scalar(env.bn_shift[:, :], env.bn_shift[:, :], env.col("L1_xattn_bn_beta"), None,
                              ALU.add).then_inc(bn, 1)


def to_feature_major(env, name, src, gamma, beta, out_hi, out_lo, eps=None, before=None):
    nc = env.nc
    with ExitStack() as stack:
        sb = env.scoped(stack)
        stats = sb(name + "_stats", [P, B, 6])
        mv = sb(name + "_mv", [P, B, 2])
        ve = sb(name + "_ve", [P, B])
        rstd = sb(name + "_rstd", [P, B])
        xn = sb(name + "_xn", [P, B, D]) if eps else src
        full = sb(name + "_full", [P, KC, TOK])
        stats_done = env.sem(name + "_stats_done")
        rstd_done = env.sem(name + "_rstd_done")
        normed = env.sem(name + "_normed")
        turned = env.sem(name + "_turned")
        evacuated = env.sem(name + "_evacuated")
        hi_done = env.sem(name + "_hi_done")
        block = stack.enter_context(nc.Block())

        @block.vector
        def _(dve):
            if before:
                before(dve)
            if eps:
                for b in range(B):
                    dve.bn_stats(stats[:, b, :], src[:, b, :]).then_inc(stats_done, 1)
                for b in range(B):
                    dve.wait_ge(stats_done, b + 1)
                    ins = dve.bn_aggr(mv[:, b, :], stats[:, b, :])
                ins.then_inc(stats_done, 1)
                dve.wait_ge(stats_done, B + 1)
                dve.tensor_scalar(ve[:, :], mv[:, :, 1], eps, None, ALU.add).then_inc(stats_done, 1)
                dve.wait_ge(rstd_done, 1)
                for b in range(B):
                    dve.tensor_scalar(xn[:, b, :], src[:, b, :], mv[:, b, 0:1], rstd[:, b:b + 1],
                                      ALU.subtract, ALU.mult).then_inc(normed, 1)
            for n in range(KC * NHALF):
                half, c = divmod(n, KC)
                part = (slice(None), c, slice(half * HALF, (half + 1) * HALF))
                dve.wait_ge(evacuated, n + 1)
                dve.tensor_copy(out_hi[part], full[part]).then_inc(hi_done, 1)
                dve.wait_ge(hi_done, n + 1)
                dve.tensor_tensor(out_lo[part], full[part], f32_view(out_hi[part]), ALU.subtract)

        @block.gpsimd
        def _(pool):
            if eps:
                pool.wait_ge(stats_done, B + 2)
                pool.tensor_tensor(rstd[:, :], ve[:, :], env.nhalf[:, 0:B], ALU.pow).then_inc(rstd_done, 1)

        @block.tensor
        def _(pe):
            if before:
                before(pe)
            for n in range(KC * NHALF):
                half, c = divmod(n, KC)
                for k in range(4):
                    b = half * 4 + k
                    if eps and c == 0:
                        pe.wait_ge(normed, b + 1)
                    mm = pe.transpose(env.bank[n][:, k * P:(k + 1) * P], xn[:, b, c * P:(c + 1) * P],
                                      env.ident[:, :])
                mm.then_inc(turned, 1)

        @block.scalar
        def _(act):
            for n in range(KC * NHALF):
                half, c = divmod(n, KC)
                out = full[:, c, half * HALF:(half + 1) * HALF]
                act.wait_ge(turned, n + 1)
                if eps:
                    ins = act.activation(out, env.bank[n][:, :], ACT.Identity, scale=gamma[:, c:c + 1],
                                         bias=beta[:, c:c + 1])
                else:
                    ins = act.activation(out, env.bank[n][:, :], ACT.Copy)
                ins.then_inc(evacuated, 1)


def feature_products(w_hi, w_lo, a_hi, a_lo, out, bias):
    jobs = []
    for f in range(out.shape[1]):
        for half in range(NHALF):
            cols = slice(half * HALF, (half + 1) * HALF)
            jobs.append(Product(
                lhs=[(w_hi[:, c, f * P:(f + 1) * P], w_lo[:, c, f * P:(f + 1) * P]) for c in range(KC)],
                rhs=[(a_hi[:, c, cols], a_lo[:, c, cols]) for c in range(KC)],
                n=HALF, out=out[:, f, cols], bias=bias[:, f:f + 1]))
    return jobs


def token_products(w_hi, w_lo, a_hi, a_lo, out, heads, hd):
    jobs = []
    for b in range(B):
        cols = slice(b * S, (b + 1) * S)
        jobs.append(Product(
            lhs=[(a_hi[:, c, cols], a_lo[:, c, cols]) for c in range(KC)],
            rhs=[(w_hi[:, c, :], w_lo[:, c, :]) for c in range(KC)],
            n=heads * hd, out=out[:, b, :, 0:hd], bias=None))
    return jobs


def project(env, name, splits, jobs, before=None, memsets=(), add_bias=None):
    nc = env.nc
    with ExitStack() as stack:
        split_done = env.sem(name + "_split")
        up = env.sem(name + "_up")
        down = env.sem(name + "_down")
        block = stack.enter_context(nc.Block())

        @block.gpsimd
        def _(pool):
            if before:
                before(pool)
            count = 0
            for raw, hi, lo in splits:
                pool.tensor_copy(hi, raw).then_inc(split_done, 1)
                count += 1
                pool.wait_ge(split_done, count)
                pool.tensor_tensor(lo, raw, f32_view(hi), ALU.subtract).then_inc(split_done, 1)
                count += 1
            for ap in memsets:
                pool.memset(ap, 1.0)
            if add_bias is not None:
                pool.tensor_tensor(env.x[:, :, :], env.x[:, :, :],
                                   add_bias[:, :].unsqueeze(1).to_broadcast([P, B, D]), ALU.add)

        @block.tensor
        def _(pe):
            pe.wait_ge(split_done, 2 * len(splits))
            for i, job in enumerate(jobs):
                if i >= 8:
                    pe.wait_ge(down, i - 7)
                out = env.bank[i % 8][:, 0:job.n]
                split_product(pe, out, job.lhs, job.rhs, True, True).then_inc(up, 1)

        @block.scalar
        def _(act):
            for i, job in enumerate(jobs):
                act.wait_ge(up, i + 1)
                src = env.bank[i % 8][:, 0:job.n]
                if job.bias is None:
                    src = src.rearrange("p (h d) -> p h d", d=job.out.shape[-1])
                    ins = act.activation(job.out, src, ACT.Copy)
                else:
                    ins = act.activation(job.out, src, ACT.Identity, bias=job.bias)
                ins.then_inc(down, 1)


def short_head_attention(env, name, heads, hd, kv_heads, scale, mask, per_sequence, multiply,
                         head_mask, q_all, k_all, v_all, w_o, v_bias):
    nc = env.nc
    NG = heads // 4
    HC = P // hd
    BODY = 2 * NG
    W = hd + 1
    LT, LP = 2, 3
    LO, LW = LP + NG, LP + NG + 2
    with ExitStack() as stack:
        sb = env.scoped(stack)
        keys = sb(name + "_keys", [P, 2, KC, HC, P])
        qs = sb(name + "_qs", [P, 2, KC, S])
        vs = sb(name + "_vs", [P, 2, kv_heads, W])
        masked = sb(name + "_masked", [P, 2, 4, S])
        shift = None if not multiply else sb(name + "_shift", [P, mask.shape[1], S])
        nmax = sb(name + "_nmax", [P, 4, 4])
        probs = sb(name + "_probs", [P, 4, 4, S])
        probsT = sb(name + "_probsT", [P, 2, 4 * S])
        rinv = sb(name + "_rinv", [P, 2, heads])
        heads_out = sb(name + "_heads_out", [P, 2, D])
        heads_outT = sb(name + "_heads_outT", [P, 2, KC * S])
        SB, TB, OB, TOB, WB = env.bank[0:2], env.bank[2:4], env.bank[4:6], env.bank[6], env.bank[7]
        staged = env.sem(name + "_staged")
        scores_up = env.sem(name + "_scores_up")
        masked_done = env.sem(name + "_masked")
        shifted = env.sem(name + "_shifted")
        max_done = env.sem(name + "_max")
        exp_done = env.sem(name + "_exp")
        turned = env.sem(name + "_turned")
        turned_out = env.sem(name + "_turned_out")
        pv_done = env.sem(name + "_pv")
        rinv_done = env.sem(name + "_rinv")
        normed = env.sem(name + "_normed")
        heads_turned = env.sem(name + "_heads_turned")
        heads_turned_out = env.sem(name + "_heads_turned_out")
        out_up = env.sem(name + "_out_up")
        added = env.sem(name + "_added")
        shift_done = env.sem(name + "_shift_done")
        block = stack.enter_context(nc.Block())
        LOOPS = B // 2

        def run(step, engine):
            for s in range(BODY):
                step(0, s, lambda lag, s=s: s >= lag, True)
            with engine.Fori(1, B // 2) as it:
                for s in range(BODY):
                    step(it * 2, s, lambda lag: True, True)
            for s in range(LW):
                step(B, s, lambda lag, s=s: s < lag, False)

        @block.gpsimd
        def _(pool):
            def stage(b, par):
                wait(pool, scores_up, (b - 1) * NG)
                wait(pool, pv_done, (b - 1) * NG)
                for c in range(KC):
                    pool.tensor_tensor(keys[:, par, c, :, :],
                                       k_all[:, c, bass.ds(b * S, S)].unsqueeze(1).to_broadcast([P, HC, S]),
                                       head_mask[:, :].unsqueeze(2).to_broadcast([P, HC, S]), ALU.mult)
                pool.tensor_copy(qs[:, par, :, :], q_all[:, :, bass.ds(b * S, S)])
                pool.tensor_copy(vs[:, par, :, :], v_all[:, bass.ds(b, 1), :, :]
                                 .rearrange("p o h w -> p (o h) w")).then_inc(staged, 1)

            stage(0, 0)
            stage(1, 1)
            with pool.Fori(1, B // 2) as it:
                for par in range(2):
                    stage(it * 2 + par, par)

        @block.tensor
        def _(pe):
            def step(seq0, s, live, on):
                g = seq0 * NG + s
                if on:
                    par, grp = s // NG, s % NG
                    c, first = (grp * 4) // HC, (grp * 4) % HC
                    if grp == 0:
                        wait(pe, staged, seq0 + par + 1)
                    wait(pe, masked_done, g - 1)
                    pe.matmul(SB[s % 2][:, :], qs[:, par, c, :], keys[:, par, c, first:first + 4, :],
                              start=True, stop=True).then_inc(scores_up, 1)
                if live(LT):
                    wait(pe, exp_done, g - LT + 1)
                    wait(pe, turned_out, g - LT - 1)
                    for h in range(4):
                        mm = pe.transpose(TB[s % 2][:, h * S:(h + 1) * S], probs[:, (s - LT) % 4, h, :],
                                          env.ident[:, :])
                    mm.then_inc(turned, 1)
                if live(LP):
                    par, grp = ((s - LP) // NG) % 2, (s - LP) % NG
                    wait(pe, turned_out, g - LP + 1)
                    if grp == 0:
                        wait(pe, normed, seq0 + (s - LP) // NG - 1)
                    for h in range(4):
                        head = grp * 4 + h
                        kv = head * kv_heads // heads
                        mm = pe.matmul(OB[par][:, head * W:(head + 1) * W],
                                       probsT[:, (s - LP) % 2, h * S:(h + 1) * S], vs[:, par, kv, :],
                                       start=True, stop=True)
                    mm.then_inc(pv_done, 1)
                if (s - LO) % NG == 0 and live(LO):
                    par, seq = ((s - LO) // NG) % 2, seq0 + (s - LO) // NG
                    wait(pe, normed, seq + 1)
                    wait(pe, heads_turned_out, seq)
                    for c in range(KC):
                        mm = pe.transpose(TOB[:, c * S:(c + 1) * S], heads_out[:, par, c * P:(c + 1) * P],
                                          env.ident[:, :])
                    mm.then_inc(heads_turned, 1)
                if (s - LW) % NG == 0 and live(LW):
                    par, seq = ((s - LW) // NG) % 2, seq0 + (s - LW) // NG
                    wait(pe, heads_turned_out, seq + 1)
                    wait(pe, added, seq)
                    for c in range(KC):
                        mm = pe.matmul(WB[:, 0:D], heads_outT[:, par, c * S:(c + 1) * S], w_o[:, c, :],
                                       start=c == 0, stop=c == KC - 1)
                    mm.then_inc(out_up, 1)

            run(step, pe)

        @block.scalar
        def _(act):
            def step(seq0, s, live, on):
                g = seq0 * NG + s
                if on:
                    wait(act, max_done, g + 1)
                    wait(act, turned, g - 3)
                    for h in range(4):
                        ins = act.activation(probs[:, s % 4, h, :], masked[:, s % 2, h, :], ACT.Exp,
                                             bias=nmax[:, s % 4, h:h + 1])
                    ins.then_inc(exp_done, 1)
                if live(LT):
                    wait(act, turned, g - LT + 1)
                    wait(act, pv_done, g - LT - 1)
                    act.activation(probsT[:, s % 2, :], TB[s % 2][:, :], ACT.Copy).then_inc(turned_out, 1)
                if (s - LO) % NG == 0 and live(LO):
                    par, seq = ((s - LO) // NG) % 2, seq0 + (s - LO) // NG
                    wait(act, heads_turned, seq + 1)
                    wait(act, out_up, seq - 1)
                    for c in range(KC):
                        ins = act.activation(heads_outT[:, par, c * S:(c + 1) * S], TOB[:, c * S:(c + 1) * S],
                                             ACT.Identity, bias=v_bias[:, c:c + 1])
                    ins.then_inc(heads_turned_out, 1)

            run(step, act)

        @block.vector
        def _(dve):
            if multiply:
                dve.tensor_scalar(shift[:, :, :], mask[:, :, :], 10000.0, -10000.0, ALU.mult, ALU.add)\
                    .then_inc(shift_done, 1)
                dve.wait_ge(shift_done, 1)

            def step(seq0, s, live, on):
                g = seq0 * NG + s
                if on:
                    b = seq0 + s // NG if per_sequence else 0
                    wait(dve, scores_up, g + 1)
                    wait(dve, exp_done, g - 1)
                    dve.scalar_tensor_tensor(masked[:, s % 2, :, :],
                                             SB[s % 2][:, :].rearrange("p (h n) -> p h n", n=S), scale,
                                             mask[:, bass.ds(b, 1), :].to_broadcast([P, 4, S]),
                                             ALU.mult, ALU.mult if multiply else ALU.add)\
                        .then_inc(masked_done, 1)
                    wait(dve, masked_done, g + 1)
                    if multiply:
                        dve.tensor_tensor(masked[:, s % 2, :, :], masked[:, s % 2, :, :],
                                          shift[:, bass.ds(b, 1), :].to_broadcast([P, 4, S]), ALU.add)\
                            .then_inc(shifted, 1)
                        wait(dve, shifted, g + 1)
                    dve.tensor_reduce(nmax[:, s % 4, :], masked[:, s % 2, :, :], X, ALU.max, negate=True)\
                        .then_inc(max_done, 1)
                if (s - LP) % NG == NG - 1 and live(LP):
                    k = (s - LP) // NG
                    par, seq = k % 2, seq0 + k
                    o = OB[par][:, 0:heads * W].rearrange("p (h w) -> p h w", w=W)
                    wait(dve, pv_done, g - LP + 1)
                    dve.reciprocal(rinv[:, par, :], o[:, :, hd]).then_inc(rinv_done, 1)
                    wait(dve, rinv_done, seq + 1)
                    wait(dve, heads_turned, seq - 1)
                    dve.tensor_tensor(heads_out[:, par, :].rearrange("p (h d) -> p h d", d=hd), o[:, :, 0:hd],
                                      rinv[:, par, :].unsqueeze(2).to_broadcast([P, heads, hd]), ALU.mult)\
                        .then_inc(normed, 1)
                if (s - LW) % NG == 0 and live(LW):
                    seq = seq0 + (s - LW) // NG
                    wait(dve, out_up, seq + 1)
                    xb = env.x[:, bass.ds(seq, 1), :].rearrange("p o d -> p (o d)")
                    dve.tensor_tensor(xb, WB[:, 0:D], xb, ALU.add).then_inc(added, 1)

            run(step, dve)


def norm_token_major(env, name, eps, gamma, beta):
    nc = env.nc
    with ExitStack() as stack:
        sb = env.scoped(stack)
        stats = sb(name + "_stats", [P, B, 6])
        mv = sb(name + "_mv", [P, B, 2])
        ve = sb(name + "_ve", [P, B])
        rstd = sb(name + "_rstd", [P, B])
        stats_done = env.sem(name + "_stats_done")
        rstd_done = env.sem(name + "_rstd_done")
        normed = env.sem(name + "_normed")
        scaled = env.sem(name + "_scaled")
        block = stack.enter_context(nc.Block())

        @block.vector
        def _(dve):
            for b in range(B):
                dve.bn_stats(stats[:, b, :], env.x[:, b, :]).then_inc(stats_done, 1)
            for b in range(B):
                dve.wait_ge(stats_done, b + 1)
                ins = dve.bn_aggr(mv[:, b, :], stats[:, b, :])
            ins.then_inc(stats_done, 1)
            dve.wait_ge(stats_done, B + 1)
            dve.tensor_scalar(ve[:, :], mv[:, :, 1], eps, None, ALU.add).then_inc(stats_done, 1)
            dve.wait_ge(rstd_done, 1)
            for b in range(B):
                dve.tensor_scalar(env.x[:, b, :], env.x[:, b, :], mv[:, b, 0:1], rstd[:, b:b + 1],
                                  ALU.subtract, ALU.mult).then_inc(normed, 1)
            for half in range(2):
                xh = env.x[:, half * 4:half * 4 + 4, :]
                dve.wait_ge(normed, 4 * half + 4)
                dve.tensor_tensor(xh, xh, gamma[:, :].unsqueeze(1).to_broadcast([P, 4, D]), ALU.mult)\
                    .then_inc(scaled, 1)
            for half in range(2):
                xh = env.x[:, half * 4:half * 4 + 4, :]
                dve.wait_ge(scaled, half + 1)
                dve.tensor_tensor(xh, xh, beta[:, :].unsqueeze(1).to_broadcast([P, 4, D]), ALU.add)

        @block.gpsimd
        def _(pool):
            pool.wait_ge(stats_done, B + 2)
            pool.tensor_tensor(rstd[:, :], ve[:, :], env.nhalf[:, 0:B], ALU.pow).then_inc(rstd_done, 1)


def non_local(env):
    nc = env.nc
    with ExitStack() as stack:
        sb = env.scoped(stack)
        wy = sb("wy", [P, B, D])
        up, scaled = env.sem("nl_up"), env.sem("nl_scaled")
        block = stack.enter_context(nc.Block())

        @block.tensor
        def _(pe):
            for b in range(B):
                pe.matmul(env.bank[b][:, 0:D], env.qT1[:, b, 0:P], env.x[:, b, :], start=True, stop=True)\
                    .then_inc(up, 1)

        @block.scalar
        def _(act):
            for b in range(B):
                act.wait_ge(up, b + 1)
                act.activation(wy[:, b, :], env.bank[b][:, 0:D], ACT.Identity, scale=env.bn_scale[:, 0:1],
                               bias=env.bn_shift[:, b:b + 1]).then_inc(scaled, 1)

        @block.vector
        def _(dve):
            for b in range(B):
                dve.wait_ge(scaled, b + 1)
                dve.tensor_tensor(env.x[:, b, :], env.x[:, b, :], wy[:, b, :], ALU.add)


def long_head_attention(env, name, a, wq, wk, wv, wo, bq, bk, bv, bias_k, bias_v, bo):
    nc = env.nc
    H, K, PAIRS = 16, P, 8
    T = S + 2
    SCALE = float(K) ** -0.5
    GR = H + 2
    PREP_DONE = 6
    LT, LP, LW = 1, 2, 3
    with ExitStack() as stack:
        sb = env.scoped(stack)
        w_raw = sb(name + "_w_raw", [P, 2, 3, KC, 2 * K])
        w_hi = sb(name + "_w_hi", [P, 2, 3, KC, 2 * K], F32R)
        w_lo = sb(name + "_w_lo", [P, 2, 3, KC, 2 * K], F32R)
        wo_raw = sb(name + "_wo_raw", [P, 2, 2, D])
        wo_hi = sb(name + "_wo_hi", [P, 2, 2, D], F32R)
        wo_lo = sb(name + "_wo_lo", [P, 2, 2, D], F32R)
        qT = sb(name + "_qT", [P, 2, 2, TOK])
        kT = sb(name + "_kT", [P, 2, 2, B, T])
        v = sb(name + "_v", [P, 2, B, 2 * K])
        bq_scaled = sb(name + "_bq_scaled", [P, H])
        extra = sb(name + "_extra", [P, H, GR])
        extra_hi = sb(name + "_extra_hi", [P, H, GR], F32R)
        extra_lo = sb(name + "_extra_lo", [P, H, GR], F32R)
        extra_now = sb(name + "_extra_now", [P, 2, 2, 2, GR], F32R)
        wb = sb(name + "_wb", [P, B, GR])
        wbT = sb(name + "_wbT", [GR, 2, P])
        G = sb(name + "_G", [GR, D])
        nmax = sb(name + "_nmax", [P, 2, 2])
        den = sb(name + "_den", [P, 2, 2])
        rinv = sb(name + "_rinv", [P, 2, 2])
        probs = sb(name + "_probs", [P, 2, 2, T])
        probs_n = sb(name + "_probs_n", [P, 2, 2, S + 1])
        probsT = sb(name + "_probsT", [P, 2, 2 * S])
        o_hi = sb(name + "_o_hi", [P, 2, 2 * S], F32R)
        o_lo = sb(name + "_o_lo", [P, 2, 2 * S], F32R)
        SB, KQB, VB = env.bank[0:2], env.bank[2], env.bank[3]
        TB, OB, WB, GB = env.bank[4], env.bank[5], env.bank[6], env.bank[7]
        sem = lambda s: env.sem(name + "_" + s)
        w_in = [sem("w_in0"), sem("w_in1")]
        wo_in = [sem("wo_in0"), sem("wo_in1")]
        w_split = sem("w_split")
        wo_split = sem("wo_split")
        side = sem("side")
        prep = sem("prep")
        kq_up, kq_down = sem("kq_up"), sem("kq_down")
        v_up, v_down = sem("v_up"), sem("v_down")
        scores_up = sem("scores_up")
        max_done = sem("max")
        exp_done = sem("exp")
        rinv_done = sem("rinv")
        scaled = sem("scaled")
        turned, turned_out = sem("turned"), sem("turned_out")
        pv_done = sem("pv")
        o_hi_done, o_lo_done = sem("o_hi"), sem("o_lo")
        out_up, added = sem("out_up"), sem("added")
        g_done = sem("g_done")
        wb_done = sem("wb_done")
        g_out = sem("g_out")
        wb_up, wb_down = sem("wb_up"), sem("wb_down")
        rest_up, rest_added = sem("rest_up"), sem("rest_added")
        bo_added = sem("bo_added")
        act_gate, pool_gate = sem("act_gate"), sem("pool_gate")
        block = stack.enter_context(nc.Block())

        w_dram = [w.rearrange("(c p) n -> p c n", p=P) for w in (a[wq], a[wk], a[wv])]
        wo_dram = a[wo].rearrange("(h d) n -> d h n", d=K)

        def run(step, engine):
            for b in range(B):
                step(0, 0, b, lambda lag, b=b: b >= lag, True, True)
            with engine.Fori(0, 3) as it:
                for k in range(2):
                    for b in range(B):
                        step(it * 2 + 1 + k, (1 + k) % 2, b, lambda lag: True, True, True)
            for b in range(B):
                step(PAIRS - 1, (PAIRS - 1) % 2, b, lambda lag: True, True, False)
            for b in range(LW):
                step(PAIRS, PAIRS % 2, b, lambda lag, b=b: b < lag, False, False)

        @block.sync
        def _(sp):
            def load_qkv(pair, par):
                wait(sp, w_split, 2 * (pair - 1))
                for k in range(3):
                    sp.dma_start(w_raw[:, par, k, :, :], w_dram[k][:, :, bass.ds(pair * 2 * K, 2 * K)])\
                        .then_inc(w_in[par], 16)

            def load_o(pair, par):
                wait(sp, wo_split, 2 * (pair - 1))
                sp.dma_start(wo_raw[:, par, :, :], wo_dram[:, bass.ds(pair * 2, 2), :]).then_inc(wo_in[par], 16)

            for pair in range(2):
                load_qkv(pair, pair)
                load_o(pair, pair)
            with sp.Fori(1, PAIRS // 2) as it:
                for par in range(2):
                    load_qkv(it * 2 + par, par)
                    load_o(it * 2 + par, par)

        @block.gpsimd
        def _(pool):
            def split_qkv(pair, par, turn):
                wait(pool, w_in[par], 48 * (turn + 1))
                wait(pool, kq_up, 8 * (pair - 1))
                wait(pool, v_up, 8 * (pair - 1))
                pool.sem_inc(pool_gate, 1)
                pool.tensor_copy(w_hi[:, par], w_raw[:, par]).then_inc(w_split, 1)
                wait(pool, w_split, 2 * pair + 1)
                pool.tensor_tensor(w_lo[:, par], w_raw[:, par], f32_view(w_hi[:, par]), ALU.subtract)\
                    .then_inc(w_split, 1)

            def split_o(pair, par, turn):
                wait(pool, wo_in[par], 16 * (turn + 1))
                wait(pool, out_up, 8 * (pair - 1))
                wait(pool, g_done, pair - 1)
                pool.sem_inc(pool_gate, 1)
                pool.tensor_copy(wo_hi[:, par], wo_raw[:, par]).then_inc(wo_split, 1)
                wait(pool, wo_split, 2 * pair + 1)
                pool.tensor_tensor(wo_lo[:, par], wo_raw[:, par], f32_view(wo_hi[:, par]), ALU.subtract)\
                    .then_inc(wo_split, 1)
                pool.tensor_copy(extra_now[:, par, 0, :, :],
                                 f32_view(extra_hi[:, bass.ds(pair * 2, 2), :]))
                pool.tensor_copy(extra_now[:, par, 1, :, :],
                                 f32_view(extra_lo[:, bass.ds(pair * 2, 2), :]))
                wait(pool, scores_up, 8 * (pair - 1))
                pool.sem_inc(pool_gate, 1)
                pool.tensor_copy(kT[:, par, :, :, S:T],
                                 bias_k[:, bass.ds(pair * 2, 2)].unsqueeze(2).unsqueeze(3)
                                 .to_broadcast([P, 2, B, 2])).then_inc(side, 1)

            split_qkv(0, 0, 0)
            split_qkv(1, 1, 0)
            pool.wait_ge(prep, PREP_DONE)
            split_o(0, 0, 0)
            split_o(1, 1, 0)
            with pool.Fori(1, PAIRS // 2) as it:
                for par in range(2):
                    split_qkv(it * 2 + par, par, it)
                    split_o(it * 2 + par, par, it)

        @block.tensor
        def _(pe):
            def project(pair, par, b):
                if b == 0:
                    wait(pe, w_split, 2 * (pair + 1))
                which, head, half = (1 if b < 4 else 0), (b % 4) // 2, b % 2
                a_hi, a_lo = (env.ctx_hi, env.ctx_lo) if which else (env.h_hi, env.h_lo)
                cols = slice(half * HALF, (half + 1) * HALF)
                wait(pe, kq_down, 8 * pair + b)
                split_product(pe, KQB[:, :],
                              [(w_hi[:, par, which, c, head * K:(head + 1) * K],
                                w_lo[:, par, which, c, head * K:(head + 1) * K]) for c in range(KC)],
                              [(a_hi[:, c, cols], a_lo[:, c, cols]) for c in range(KC)], True, True)\
                    .then_inc(kq_up, 1)
                cols = slice(b * S, (b + 1) * S)
                wait(pe, v_down, 8 * pair + b)
                split_product(pe, VB[:, 0:2 * K],
                              [(env.ctx_hi[:, c, cols], env.ctx_lo[:, c, cols]) for c in range(KC)],
                              [(w_hi[:, par, 2, c, :], w_lo[:, par, 2, c, :]) for c in range(KC)], True, True)\
                    .then_inc(v_up, 1)

            def step(pair, par, b, live, attend, then_project):
                g = pair * 8 + b
                if attend:
                    if b == 0:
                        wait(pe, side, pair + 1)
                        wait(pe, kq_down, 8 * (pair + 1))
                    wait(pe, max_done, g - 1)
                    wait(pe, exp_done, g - 1)
                    for h in range(2):
                        mm = pe.matmul(SB[b % 2][:, h * T:(h + 1) * T], qT[:, par, h, b * S:(b + 1) * S],
                                       kT[:, par, h, b, :], start=True, stop=True)
                    mm.then_inc(scores_up, 1)
                if then_project:
                    project(pair + 1, 1 - par, b)
                if live(LT):
                    wait(pe, scaled, g - LT + 1)
                    wait(pe, turned_out, g - LT)
                    for h in range(2):
                        mm = pe.transpose(TB[:, h * S:(h + 1) * S], probs_n[:, (b - LT) % 2, h, 0:S],
                                          env.ident[:, :])
                    mm.then_inc(turned, 1)
                if live(LP):
                    own = par if b >= LP else 1 - par
                    if b == LP:
                        wait(pe, v_down, 8 * (pair + 1))
                    wait(pe, turned_out, g - LP + 1)
                    wait(pe, o_lo_done, g - LP)
                    for h in range(2):
                        mm = pe.matmul(OB[:, h * S:(h + 1) * S], v[:, own, (b - LP) % B, h * K:(h + 1) * K],
                                       probsT[:, (b - LP) % 2, h * S:(h + 1) * S], start=True, stop=True)
                    mm.then_inc(pv_done, 1)
                if live(LW):
                    own = par if b >= LW else 1 - par
                    if b == LW:
                        wait(pe, wo_split, 2 * (pair + 1))
                        wait(pe, side, pair + 1)
                    wait(pe, o_lo_done, g - LW + 1)
                    wait(pe, added, g - LW)
                    o = (slice(None), (b - LW) % 2)
                    split_product(pe, WB[:, 0:D],
                                  [(o_hi[o + (slice(h * S, (h + 1) * S),)], o_lo[o + (slice(h * S, (h + 1) * S),)])
                                   for h in range(2)],
                                  [(wo_hi[:, own, h, :], wo_lo[:, own, h, :]) for h in range(2)], True, True)\
                        .then_inc(out_up, 1)
                if attend and b == LW:
                    first = isinstance(pair, int) and pair == 0
                    last = isinstance(pair, int) and pair == PAIRS - 1
                    for h in range(2):
                        lo, hi = extra_now[:, par, 1, h, :], extra_now[:, par, 0, h, :]
                        pe.matmul(GB[0:GR, 0:D], lo, wo_hi[:, par, h, :], start=first and h == 0, stop=False,
                                  skip_group_check=True)
                        pe.matmul(GB[0:GR, 0:D], hi, wo_lo[:, par, h, :], start=False, stop=False,
                                  skip_group_check=True)
                        mm = pe.matmul(GB[0:GR, 0:D], hi, wo_hi[:, par, h, :], start=False,
                                       stop=last and h == 1, skip_group_check=True)
                    mm.then_inc(g_done, 1)

            for b in range(B):
                project(0, 0, b)
            run(step, pe)
            for b in range(B):
                pe.wait_ge(wb_done, PAIRS * B + 1)
                wait(pe, wb_down, b - 1)
                pe.transpose(SB[b % 2][0:GR, 0:P], wb[:, b, :], env.ident[:, :]).then_inc(wb_up, 1)
                pe.wait_ge(wb_down, b + 1)
                pe.wait_ge(g_out, 1)
                wait(pe, rest_added, b - 1)
                pe.matmul((KQB, VB)[b % 2][:, 0:D], wbT[:, b % 2, :], G[:, :], start=True, stop=True)\
                    .then_inc(rest_up, 1)

        @block.scalar
        def _(act):
            def project(pair, par, b):
                which, head, half = (1 if b < 4 else 0), (b % 4) // 2, b % 2
                wait(act, kq_up, 8 * pair + b + 1)
                wait(act, scores_up, 8 * (pair - 1))
                act.sem_inc(act_gate, 1)
                at = bass.ds(pair * 2 + head, 1)
                if which:
                    act.activation(kT[:, par, head, half * 4:half * 4 + 4, 0:S],
                                   KQB[:, :].rearrange("p (b t) -> p b t", t=S), ACT.Identity,
                                   bias=bk[:, at]).then_inc(kq_down, 1)
                else:
                    act.activation(qT[:, par, head, half * HALF:(half + 1) * HALF], KQB[:, :], ACT.Identity,
                                   bias=bq_scaled[:, at], scale=SCALE).then_inc(kq_down, 1)
                wait(act, v_up, 8 * pair + b + 1)
                wait(act, pv_done, 8 * (pair - 2) + b + 1)
                act.activation(v[:, par, b, :], VB[:, 0:2 * K], ACT.Copy).then_inc(v_down, 1)

            def step(pair, par, b, live, attend, then_project):
                g = pair * 8 + b
                if attend:
                    wait(act, max_done, g + 1)
                    wait(act, scaled, g - 1)
                    for h in range(2):
                        ins = act.activation(probs[:, b % 2, h, 0:S + 1], SB[b % 2][:, h * T:h * T + S + 1],
                                             ACT.Exp, bias=nmax[:, b % 2, h:h + 1],
                                             accum_out=den[:, b % 2, h:h + 1])
                    ins.then_inc(exp_done, 1)
                if then_project:
                    project(pair + 1, 1 - par, b)
                if live(LP):
                    wait(act, pv_done, g - LP + 1)
                    wait(act, out_up, g - LP - 1)
                    act.activation(o_hi[:, b % 2, :], OB[:, 0:2 * S], ACT.Copy).then_inc(o_hi_done, 1)

            act.wait_ge(prep, 1)
            for b in range(B):
                project(0, 0, b)
            run(step, act)
            act.wait_ge(g_done, PAIRS)
            act.activation(G[:, :], GB[0:GR, 0:D], ACT.Copy).then_inc(g_out, 1)
            for b in range(B):
                act.wait_ge(wb_up, b + 1)
                wait(act, rest_up, b - 1)
                act.activation(wbT[:, b % 2, :], SB[b % 2][0:GR, 0:P], ACT.Copy).then_inc(wb_down, 1)


        @block.vector
        def _(dve):
            dve.tensor_scalar(bq_scaled[:, :], bq, SCALE, None, ALU.mult).then_inc(prep, 1)
            dve.memset(extra[:, :, :], 0.0).then_inc(prep, 1)
            dve.wait_ge(prep, 2)
            flat_extra = extra[:, :, :].rearrange("p h g -> p (h g)")
            dve.tensor_tensor(flat_extra[:, 0:(GR + 1) * (H - 1) + 1:GR + 1], bias_v, bv, ALU.subtract)\
                .then_inc(prep, 1)
            dve.tensor_copy(extra[:, :, H], bv).then_inc(prep, 1)
            dve.wait_ge(prep, 4)
            dve.tensor_copy(extra_hi[:, :, :], extra[:, :, :]).then_inc(prep, 1)
            dve.wait_ge(prep, 5)
            dve.tensor_tensor(extra_lo[:, :, :], extra[:, :, :], f32_view(extra_hi[:, :, :]), ALU.subtract)\
                .then_inc(prep, 1)
            dve.memset(wb[:, :, H:H + 1], 1.0)
            dve.memset(wb[:, :, H + 1:GR], 0.0).then_inc(wb_done, 1)
            dve.tensor_tensor(env.x[:, :, :], env.x[:, :, :],
                              bo[:, :].unsqueeze(1).to_broadcast([P, B, D]), ALU.add).then_inc(bo_added, 1)
            dve.wait_ge(bo_added, 1)

            def step(pair, par, b, live, attend, then_project):
                g = pair * 8 + b
                if attend:
                    wait(dve, scores_up, g + 1)
                    wait(dve, exp_done, g - 1)
                    dve.tensor_reduce(nmax[:, b % 2, :],
                                      SB[b % 2][:, 0:2 * T].rearrange("p (h t) -> p h t", t=T)[:, :, 0:S + 1],
                                      X, ALU.max, negate=True).then_inc(max_done, 1)
                    wait(dve, exp_done, g + 1)
                    dve.reciprocal(rinv[:, b % 2, :], den[:, b % 2, :]).then_inc(rinv_done, 1)
                    wait(dve, rinv_done, g + 1)
                    wait(dve, turned, g - 1)
                    wait(dve, wb_done, g)
                    for h in range(2):
                        ins = dve.tensor_scalar(probs_n[:, b % 2, h, :], probs[:, b % 2, h, 0:S + 1],
                                                rinv[:, b % 2, h:h + 1], None, ALU.mult)
                    ins.then_inc(scaled, 1)
                    wait(dve, scaled, g + 1)
                    dve.tensor_copy(wb[:, b, bass.ds(pair * 2, 2)], probs_n[:, b % 2, :, S]).then_inc(wb_done, 1)
                if live(LT):
                    wait(dve, turned, g - LT + 1)
                    wait(dve, pv_done, g - LT - 1)
                    dve.tensor_copy(probsT[:, (b - LT) % 2, :], TB[:, 0:2 * S]).then_inc(turned_out, 1)
                if live(LP):
                    wait(dve, o_hi_done, g - LP + 1)
                    wait(dve, out_up, g - LP - 1)
                    dve.tensor_tensor(o_lo[:, b % 2, :], OB[:, 0:2 * S], f32_view(o_hi[:, b % 2, :]),
                                      ALU.subtract).then_inc(o_lo_done, 1)
                if live(LW):
                    wait(dve, out_up, g - LW + 1)
                    xb = env.x[:, (b - LW) % B, :]
                    dve.tensor_tensor(xb, WB[:, 0:D], xb, ALU.add).then_inc(added, 1)

            run(step, dve)
            for b in range(B):
                dve.wait_ge(rest_up, b + 1)
                dve.wait_ge(added, PAIRS * B)
                dve.tensor_tensor(env.x[:, b, :], (KQB, VB)[b % 2][:, 0:D], env.x[:, b, :], ALU.add)\
                    .then_inc(rest_added, 1)


def feed_forward(env, name, w1, w2, b1, b2, func, w_in=None, load_next=None, out=None):
    nc = env.nc
    F = w1.shape[2]
    FC = F // P
    with ExitStack() as stack:
        sb = env.scoped(stack)
        w1_hi, w1_lo = sb(name + "_w1_hi", [P, KC, F], F32R), sb(name + "_w1_lo", [P, KC, F], F32R)
        w2_hi, w2_lo = sb(name + "_w2_hi", [P, FC, D], F32R), sb(name + "_w2_lo", [P, FC, D], F32R)
        act_full = sb(name + "_act", [P, 2, HALF])
        act_hi = sb(name + "_act_hi", [P, NHALF, FC, HALF], F32R)
        act_lo = sb(name + "_act_lo", [P, NHALF, FC, HALF], F32R)
        w_hi_done, w_lo_done = env.sem(name + "_w_hi"), env.sem(name + "_w_lo")
        b2_added = env.sem(name + "_b2")
        up, acted = env.sem(name + "_up"), env.sem(name + "_acted")
        hi_done, lo_done = env.sem(name + "_hi"), env.sem(name + "_lo")
        out_up, added = env.sem(name + "_out_up"), env.sem(name + "_added")
        stored = env.sem(name + "_stored")
        NJ = FC * NHALF
        block = stack.enter_context(nc.Block())

        @block.gpsimd
        def _(pool):
            if w_in:
                pool.wait_ge(*w_in)
            count = 0
            for f in range(FC):
                cols = slice(f * P, (f + 1) * P)
                pool.tensor_copy(w1_hi[:, :, cols], w1[:, :, cols]).then_inc(w_hi_done, 1)
                count += 1
                pool.wait_ge(w_hi_done, count)
                pool.tensor_tensor(w1_lo[:, :, cols], w1[:, :, cols], f32_view(w1_hi[:, :, cols]), ALU.subtract)\
                    .then_inc(w_lo_done, 1)
            for f in range(FC):
                pool.tensor_copy(w2_hi[:, f, :], w2[:, f, :]).then_inc(w_hi_done, 1)
                count += 1
                pool.wait_ge(w_hi_done, count)
                pool.tensor_tensor(w2_lo[:, f, :], w2[:, f, :], f32_view(w2_hi[:, f, :]), ALU.subtract)\
                    .then_inc(w_lo_done, 1)

        @block.tensor
        def _(pe):
            for half in range(NHALF):
                cols = slice(half * HALF, (half + 1) * HALF)
                for f in range(FC):
                    j = half * FC + f
                    fs = slice(f * P, (f + 1) * P)
                    pe.wait_ge(w_lo_done, f + 1)
                    wait(pe, acted, j - 3)
                    split_product(pe, env.bank[j % 4][:, :],
                                  [(w1_hi[:, c, fs], w1_lo[:, c, fs]) for c in range(KC)],
                                  [(env.h_hi[:, c, cols], env.h_lo[:, c, cols]) for c in range(KC)], True, True)\
                        .then_inc(up, 1)
            pe.wait_ge(w_lo_done, 2 * FC)
            for b in range(B):
                half, k = divmod(b, 4)
                pe.wait_ge(lo_done, FC * (half + 1))
                wait(pe, added, b - 3)
                cols = slice(k * S, (k + 1) * S)
                split_product(pe, env.bank[4 + b % 4][:, 0:D],
                              [(act_hi[:, half, f, cols], act_lo[:, half, f, cols]) for f in range(FC)],
                              [(w2_hi[:, f, :], w2_lo[:, f, :]) for f in range(FC)], True, True)\
                    .then_inc(out_up, 1)

        @block.scalar
        def _(act):
            for j in range(NJ):
                f = j % FC
                act.wait_ge(up, j + 1)
                wait(act, lo_done, j - 1)
                act.activation(act_full[:, j % 2, :], env.bank[j % 4][:, :], func, bias=b1[:, f:f + 1])\
                    .then_inc(acted, 1)

        @block.vector
        def _(dve):
            dve.tensor_tensor(env.x[:, :, :], env.x[:, :, :],
                              b2[:, :].unsqueeze(1).to_broadcast([P, B, D]), ALU.add).then_inc(b2_added, 1)
            for j in range(NJ):
                half, f = divmod(j, FC)
                dve.wait_ge(acted, j + 1)
                dve.tensor_copy(act_hi[:, half, f, :], act_full[:, j % 2, :]).then_inc(hi_done, 1)
                dve.wait_ge(hi_done, j + 1)
                dve.tensor_tensor(act_lo[:, half, f, :], act_full[:, j % 2, :],
                                  f32_view(act_hi[:, half, f, :]), ALU.subtract).then_inc(lo_done, 1)
            dve.wait_ge(b2_added, 1)
            for b in range(B):
                dve.wait_ge(out_up, b + 1)
                dve.tensor_tensor(env.x[:, b, :], env.bank[4 + b % 4][:, 0:D], env.x[:, b, :], ALU.add)\
                    .then_inc(added, 1)

        @block.sync
        def _(sp):
            if load_next:
                load_next(sp)
            if out is not None:
                for b in range(B):
                    sp.wait_ge(added, b + 1)
                    sp.dma_start(out[b], env.x[:, b, :]).then_inc(stored, 16)
                sp.wait_ge(stored, 16 * B)


def build(nc, a, out, until=99):
    ctx = ExitStack()
    with ctx:
        env = make_env(nc, ctx)
        sb = env.scoped(ctx)
        env.x = sb("x", [P, B, D])
        env.ident = sb("ident", [P, P])
        env.nhalf = sb("nhalf", [P, B])
        at, used = place_rows()
        env.cols = [sb(f"cols{t}", [P, n]) for t, n in enumerate(used)]

        def col(name, first=0, n=None):
            t, r, rows = at[name]
            return env.cols[t][:, r + first:r + first + (rows if n is None else n)]

        env.col = col
        env.free = {name: sb("free_" + name, [P, D]) for name in FREE_VECTORS}
        env.ctx_hi, env.ctx_lo = sb("ctx_hi", [P, KC, TOK], F32R), sb("ctx_lo", [P, KC, TOK], F32R)
        env.h_hi, env.h_lo = sb("h_hi", [P, KC, TOK], F32R), sb("h_lo", [P, KC, TOK], F32R)
        env.qT1 = sb("qT1", [P, B, P + 1])
        env.bn_scale, env.bn_shift = sb("bn_scale", [P, 1]), sb("bn_shift", [P, B])
        env.head_mask8, env.head_mask16 = sb("head_mask8", [P, 16]), sb("head_mask16", [P, 8])
        env.mask_self, env.mask_cross = sb("mask_self", [P, 1, S]), sb("mask_cross", [P, B, S])
        env.x_in, env.w0_in, env.mask_in = (env.lasting_sem(n) for n in ("x_in", "w0_in", "mask_in"))
        env.free_in, env.ff2_in, env.l3_in = (env.lasting_sem(n) for n in ("free_in", "ff2_in", "l3_in"))
        env.masks_made = env.lasting_sem("masks_made")
        with ExitStack() as late:
            lsb = env.scoped(late)

            def weights(shapes):
                return {name: lsb(name, [P, k, n]) for name, k, n in shapes}

            L = env.w_ff2 = weights((("L2_xattn_w_fc1", 2, 1024), ("L2_xattn_w_fc2", 8, 256)))

            with ExitStack() as l0:
                zsb = env.scoped(l0)
                env.w_q0, env.w_o0 = zsb("w_q0", [P, KC, D]), zsb("w_o0", [P, KC, D])
                env.w_k0, env.w_v0 = zsb("w_k0", [P, KC, 64]), zsb("w_v0", [P, KC, 64])
                env.mask0 = zsb("mask0", [P, B, S])
                setup(env, a)
                layer0(env)
            if until >= 1:
                non_local(env)
            for k, (eps_scale, eps_offset) in enumerate((("ln1_scale", "ln1_offset"), ("ln2_scale", "ln2_offset"))):
                if until >= 2 + k:
                    n = str(k + 1)
                    L2 = "L2_xattn_"
                    to_feature_major(env, "ln2" + n, env.x, env.col(L2 + eps_scale), env.col(L2 + eps_offset),
                                     env.h_hi, env.h_lo, eps=1e-5)
                    long_head_attention(env, "la" + n, a, L2 + "wq" + n, L2 + "wk" + n, L2 + "wv" + n, L2 + "wo" + n,
                                        env.col(L2 + "bq" + n), env.col(L2 + "bk" + n), env.col(L2 + "bv" + n),
                                        env.col(L2 + "bias_k" + n), env.col(L2 + "bias_v" + n),
                                        env.free[L2 + "bo" + n])
                    free_semaphores(env)
            L3 = weights((("L3_xattn_w_qkv", 2, 768), ("L3_xattn_w_ao", 2, 256),
                          ("L3_xattn_w_q", 2, 256), ("L3_xattn_w_kv", 2, 512),
                          ("L3_xattn_w_co", 2, 256), ("L3_xattn_w1", 2, 1024), ("L3_xattn_w2", 8, 256)))
            if until >= 4:
                to_feature_major(env, "ln2m", env.x, env.col("L2_xattn_ln_mlp_scale"),
                                 env.col("L2_xattn_ln_mlp_offset"), env.h_hi, env.h_lo, eps=1e-5)
                feed_forward(env, "ff2", L["L2_xattn_w_fc1"], L["L2_xattn_w_fc2"], env.col("L2_xattn_b_fc1"),
                             env.free["L2_xattn_b_fc2"], ACT.Gelu, w_in=(env.ff2_in, 32),
                             load_next=lambda sp: load_weights(env, sp, a, L3, env.l3_in))
            if until >= 5:
                layer3_attention(env, "sa", "ln1", L3["L3_xattn_w_qkv"], None, "b_qkv", None,
                                 env.free["L3_xattn_b_ao"], L3["L3_xattn_w_ao"], env.mask_self, False)
            if until >= 6:
                layer3_attention(env, "ca", "ln2", L3["L3_xattn_w_q"], L3["L3_xattn_w_kv"], "b_q", "b_kv",
                                 env.free["L3_xattn_b_co"], L3["L3_xattn_w_co"], env.mask_cross, True)
            if until >= 7:
                to_feature_major(env, "ln3m", env.x, env.col("L3_xattn_ln3_s"), env.col("L3_xattn_ln3_b"),
                                 env.h_hi, env.h_lo, eps=1e-5)
                feed_forward(env, "ff3", L3["L3_xattn_w1"], L3["L3_xattn_w2"], env.col("L3_xattn_b1"),
                             env.free["L3_xattn_b2"], ACT.Gelu_apprx_tanh, out=out)
            else:
                dump(env, out)


def wait(engine, sem, value):
    if not isinstance(value, int) or value > 0:
        engine.wait_ge(sem, value)


def dump(env, out):
    stored = env.sem("stored")
    with env.nc.Block() as block:
        @block.sync
        def _(sp):
            sp.dma_start(out.rearrange("b s d -> s b d"), env.x[:, :, :]).then_inc(stored, 16)
            sp.wait_ge(stored, 16)


def layer0(env):
    with ExitStack() as stack:
        sb = env.scoped(stack)
        q_all, k_all = sb("q_all0", [P, KC, TOK]), sb("k_all0", [P, KC, TOK])
        v_all = sb("v_all0", [P, B, KV_HEADS, HD0 + 1])
        with ExitStack() as parts:
            psb = env.scoped(parts)
            wq_hi, wq_lo = psb("wq0_hi", [P, KC, D], F32R), psb("wq0_lo", [P, KC, D], F32R)
            wk = psb("wk0_rep", [P, KC, 8, GROUP, HD0])
            wk_hi, wk_lo = psb("wk0_hi", [P, KC, D], F32R), psb("wk0_lo", [P, KC, D], F32R)
            wv_hi, wv_lo = psb("wv0_hi", [P, KC, 64], F32R), psb("wv0_lo", [P, KC, 64], F32R)
            to_feature_major(env, "t0", env.x, None, None, env.h_hi, env.h_lo,
                             before=lambda eng: eng.wait_ge(env.x_in, 16))
            spread = env.sem("wk0_spread")

            def before(pool):
                pool.wait_ge(env.w0_in, 64)
                pool.wait_ge(env.free_in, 16 * len(FREE_VECTORS))
                for c in range(KC):
                    pool.tensor_copy(wk[:, c, :, :, :],
                                     env.w_k0[:, c, :].rearrange("p (g d) -> p g d", d=HD0).unsqueeze(2)
                                     .to_broadcast([P, 8, GROUP, HD0])).then_inc(spread, 1)
                pool.wait_ge(spread, KC)

            flat_wk = wk[:, :, :, :, :].rearrange("p c g j d -> p c (g j d)")
            project(env, "p0",
                    [(env.w_q0[:, :, :], wq_hi[:, :, :], wq_lo[:, :, :]), (flat_wk, wk_hi[:, :, :], wk_lo[:, :, :]),
                     (env.w_v0[:, :, :], wv_hi[:, :, :], wv_lo[:, :, :])],
                    feature_products(wq_hi, wq_lo, env.h_hi, env.h_lo, q_all, env.col("L0_xattn_bq"))
                    + feature_products(wk_hi, wk_lo, env.ctx_hi, env.ctx_lo, k_all, env.col("bk_of_heads"))
                    + token_products(wv_hi, wv_lo, env.ctx_hi, env.ctx_lo, v_all, KV_HEADS, HD0),
                    before=before, memsets=[v_all[:, :, :, HD0:HD0 + 1]], add_bias=env.free["L0_xattn_bo"])
        short_head_attention(env, "a0", 32, HD0, KV_HEADS, float(HD0) ** -0.5, env.mask0, True, False,
                             env.head_mask8, q_all, k_all, v_all, env.w_o0, env.col("bv_of_heads"))
        norm_token_major(env, "n0", 1e-6, env.free["L0_xattn_gamma"], env.free["L0_xattn_beta"])


def layer3_attention(env, name, ln, w_q, w_kv, b_q, b_kv, b_out, w_out, mask, per_sequence):
    heads, hd = 16, 16
    L3 = "L3_xattn_"
    with ExitStack() as stack:
        sb = env.scoped(stack)
        q_all, k_all = sb(name + "_q", [P, KC, TOK]), sb(name + "_k", [P, KC, TOK])
        v_all = sb(name + "_v", [P, B, heads, hd + 1])
        with ExitStack() as parts:
            psb = env.scoped(parts)
            to_feature_major(env, name + "_ln", env.x, env.col(L3 + ln + "_s"), env.col(L3 + ln + "_b"),
                             env.h_hi, env.h_lo, eps=1e-5)
            raws = [w_q] if w_kv is None else [w_q, w_kv]
            parts_of = []
            for i, raw in enumerate(raws):
                n = raw.shape[2]
                parts_of.append((raw[:, :, :], psb(f"{name}_w{i}_hi", [P, KC, n], F32R),
                                 psb(f"{name}_w{i}_lo", [P, KC, n], F32R)))
            if w_kv is None:
                _, hi, lo = parts_of[0]
                wq, wk, wv = [(hi[:, :, k * D:(k + 1) * D], lo[:, :, k * D:(k + 1) * D]) for k in range(3)]
                src = (env.h_hi, env.h_lo)
                bq, bk, bv = (env.col(L3 + b_q, 2 * k, 2) for k in range(3))
            else:
                wq = (parts_of[0][1][:, :, :], parts_of[0][2][:, :, :])
                _, hi, lo = parts_of[1]
                wk, wv = [(hi[:, :, k * D:(k + 1) * D], lo[:, :, k * D:(k + 1) * D]) for k in range(2)]
                src = (env.ctx_hi, env.ctx_lo)
                bq = env.col(L3 + b_q)
                bk, bv = (env.col(L3 + b_kv, 2 * k, 2) for k in range(2))
            project(env, name + "_p", [(r, h[:, :, :], l[:, :, :]) for r, h, l in parts_of],
                    feature_products(*wq, env.h_hi, env.h_lo, q_all, bq)
                    + feature_products(*wk, *src, k_all, bk)
                    + token_products(*wv, *src, v_all, heads, hd),
                    before=lambda pool: pool.wait_ge(env.l3_in, 16 * 7),
                    memsets=[v_all[:, :, :, hd:hd + 1]], add_bias=b_out)
        short_head_attention(env, name, heads, hd, heads, float(hd) ** -0.5, mask, per_sequence, True,
                             env.head_mask16, q_all, k_all, v_all, w_out, bv)


_OUT = (B, S, D)


def kernel(**inputs):
    import numpy as _np
    import concourse.bacc as _bacc
    from concourse import mybir as _mybir
    from concourse.bass_utils import run_bass_kernel_spmd as _run

    nc = _bacc.Bacc("TRN2", target_bir_lowering=False, num_devices=1)
    arrays, args = {}, {}
    for name, value in inputs.items():
        value = _np.ascontiguousarray(value)
        arrays[f"in_{name}"] = value
        args[name] = nc.dram_tensor(f"in_{name}", value.shape, _mybir.dt.from_np(value.dtype),
                                    kind="ExternalInput").ap()
    out = nc.dram_tensor("out_0", _OUT, F32, kind="ExternalOutput").ap()
    build(nc, args, out)
    r = _run(nc, [arrays], core_ids=[0])
    return r.results[0]["out_0"]
```

```python
from contextlib import ExitStack

import concourse.bass as bass
from concourse import mybir

F32 = mybir.dt.float32
F32R = mybir.dt.float32r
ALU = mybir.AluOpType
ACT = mybir.ActivationFunctionType
X = mybir.AxisListType.X

P = 128
B = 8
S = 128
D = 256
KC = D // P
TOK = B * S
HALF = 512
NHALF = TOK // HALF


class Env:

    def __init__(self, nc):
        self.nc = nc


class Product:

    def __init__(self, lhs, rhs, n, out, bias, weights, half):
        self.lhs, self.rhs, self.n, self.out, self.bias = lhs, rhs, n, out, bias
        self.weights, self.half = weights, half


def make_env(nc, ctx):
    env = Env(nc)

    def scoped(stack):
        def sb(name, shape, dt=F32):
            return stack.enter_context(nc.sbuf_tensor(name, shape, dt))
        return sb

    env.scoped = scoped
    env.lasting_sem = lambda name: ctx.enter_context(nc.semaphore(name))
    env.stage_sems = []

    def sem(name):
        env.stage_sems.append(nc.alloc_semaphore(name=name))
        return env.stage_sems[-1]

    env.sem = sem
    env.bank = [ctx.enter_context(nc.psum_tensor(f"bank{i}", [P, 512], F32)) for i in range(8)]
    return env


def free_semaphores(env):
    env.nc.clear_and_free_semaphores(env.stage_sems)
    env.nc.all_engine_barrier()
    env.stage_sems = []


def f32_view(ap):
    return ap.bitcast(F32)


def split_product(pe, out, lhs, rhs, start, stop):
    n = len(lhs)
    for k in range(n):
        (lh, ll), (rh, rl) = lhs[k], rhs[k]
        pe.matmul(out, ll, rh, start=start and k == 0, stop=False)
        pe.matmul(out, lh, rl, start=False, stop=False)
        mm = pe.matmul(out, lh, rh, start=False, stop=stop and k == n - 1)
    return mm


def load_weights(env, sp, a, weights, sem):
    for name, dst in weights.items():
        k = a[name].shape[0] // P
        sp.dma_start(dst[:, :, :], a[name].rearrange("(c p) n -> p c n", c=k)).then_inc(sem, 16)


ROW_VECTORS = [
    ("L0_xattn_bq", 2), ("L1_xattn_w_b", 1), ("L1_xattn_bn_gamma", 1), ("L1_xattn_bn_beta", 1),
    ("L1_xattn_bn_mean", 1), ("L1_xattn_bn_var", 1),
    ("L2_xattn_ln1_scale", 2), ("L2_xattn_ln1_offset", 2),
    ("L2_xattn_bq1", 16), ("L2_xattn_bk1", 16), ("L2_xattn_bv1", 16),
    ("L2_xattn_bias_k1", 16), ("L2_xattn_bias_v1", 16),
    ("L3_xattn_ln1_s", 2), ("L3_xattn_ln1_b", 2), ("L3_xattn_b_qkv", 6),
    ("L3_xattn_ln2_s", 2), ("L3_xattn_ln2_b", 2), ("L3_xattn_b_q", 2), ("L3_xattn_b_kv", 4),
    ("L3_xattn_ln3_s", 2), ("L3_xattn_ln3_b", 2),
    ("L2_xattn_ln2_scale", 2), ("L2_xattn_ln2_offset", 2),
    ("L2_xattn_bq2", 16), ("L2_xattn_bk2", 16), ("L2_xattn_bv2", 16),
    ("L2_xattn_bias_k2", 16), ("L2_xattn_bias_v2", 16),
    ("L2_xattn_ln_mlp_scale", 2), ("L2_xattn_ln_mlp_offset", 2), ("L2_xattn_b_fc1", 8),
    ("L3_xattn_b1", 8),
    ("bk_of_heads", 2), ("bv_of_heads", 2),
]
FREE_VECTORS = ["L0_xattn_bo", "L0_xattn_gamma", "L0_xattn_beta", "L2_xattn_bo1", "L2_xattn_bo2",
                "L2_xattn_b_fc2", "L3_xattn_b_ao", "L3_xattn_b_co", "L3_xattn_b2"]
KV_HEADS, GROUP, HD0 = 8, 4, 8


def place_rows():
    at, tile, row = {}, 0, 0
    for name, n in ROW_VECTORS:
        if row + n > P:
            tile, row = tile + 1, 0
        at[name] = (tile, row, n)
        row += n
    used = [max(r + n for t, r, n in at.values() if t == k) for k in range(tile + 1)]
    return at, used


def flat(ap):
    if len(ap.shape) == 4:
        return ap.rearrange("a b c d -> (a b c d)")
    return ap


def setup(env, a):
    nc = env.nc
    N1 = D
    CI = 64
    with ExitStack() as stack:
        sb = env.scoped(stack)
        at, used = place_rows()
        rows = [sb(f"rows{t}", [P, P]) for t in range(len(used))]
        ctx_tok = sb("ctx_tok", [P, B, D])
        ctx_f = sb("ctx_f", [P, KC, TOK])
        pg_w = sb("pg_w", [P, P])
        w_w = sb("w_w", [P, CI])
        theta_w = sb("theta_w", [CI, P])
        theta_b = sb("theta_b", [CI, 2])
        pg_bias = sb("pg_bias", [P, P])
        pg_wT = sb("pg_wT", [P, P])
        w_wT = sb("w_wT", [CI, P])
        pg = sb("pg", [P, 2, KC, P])
        mT = sb("mT", [CI, 2, CI])
        pT = sb("pT", [CI, 2, P])
        nhalf1 = sb("nhalf1", [P, 1])
        inv = sb("inv", [P, 2])

        rows_in = env.sem("rows_in")
        ctx_in = env.sem("ctx_in")
        nl_in = env.sem("nl_in")
        pool_init = env.sem("pool_init")
        cols_up = env.sem("cols_up")
        cols_down = env.sem("cols_down")
        ctx_up = env.sem("ctx_up")
        ctx_down = env.sem("ctx_down")
        ctx_split = env.sem("ctx_split")
        nl_wt_up = env.sem("nl_wt_up")
        nl_wt_down = env.sem("nl_wt_down")
        pg_up, pg_down = env.sem("pg_up"), env.sem("pg_down")
        mt_up, mt_down = env.sem("mt_up"), env.sem("mt_down")
        pt_up, pt_down = env.sem("pt_up"), env.sem("pt_down")
        qt_up, qt_down = env.sem("qt_up"), env.sem("qt_down")
        bn = env.sem("bn")
        bn_pow = env.sem("bn_pow")
        block = stack.enter_context(nc.Block())

        @block.sync
        def _(sp):
            count = 0
            for name, (t, r, n) in at.items():
                if name in ("bk_of_heads", "bv_of_heads"):
                    src = a["L0_xattn_bk" if name == "bk_of_heads" else "L0_xattn_bv"]
                    for j in range(GROUP):
                        dst = rows[t][r:r + n, :].rearrange("c (g j d) -> c g j d", j=GROUP, d=HD0)
                        for c in range(n):
                            sp.dma_start(dst[c:c + 1, :, j, :],
                                         src.rearrange("(c g d) -> c g d", g=4, d=HD0)[c:c + 1])\
                                .then_inc(rows_in, 16)
                            count += 16
                    continue
                sp.dma_start(rows[t][r:r + n, :], flat(a[name]).rearrange("(r p) -> r p", p=P))\
                    .then_inc(rows_in, 16)
                count += 16
            env.rows_count = count
            sp.dma_start(env.x[:, :, :], a["x"].rearrange("b s d -> s b d")).then_inc(env.x_in, 16)
            for name, dst in (("Wq", env.w_q0), ("Wo", env.w_o0)):
                sp.dma_start(dst[:, :, :], a["L0_xattn_" + name].rearrange("(c p) n -> p c n", p=P))\
                    .then_inc(env.w0_in, 16)
            sp.dma_start(env.w_k0[:, :, :], a["L0_xattn_Wk"].rearrange("(c p) n -> p c n", p=P))\
                .then_inc(env.w0_in, 16)
            sp.dma_start(env.w_v0[:, :, :], a["L0_xattn_Wv"].rearrange("(c p) n -> p c n", p=P))\
                .then_inc(env.w0_in, 16)
            sp.dma_start(env.mask0[:, :, :], a["mask_Bx1xSxS2_ff0"].rearrange("b o q s -> q (b o) s"))\
                .then_inc(env.mask_in, 16)
            for name in FREE_VECTORS:
                sp.dma_start(env.free[name][:, :],
                             a[name].rearrange("(a n) -> a n", a=1).to_broadcast([P, D]))\
                    .then_inc(env.free_in, 16)
            load_weights(env, sp, a, env.w_ff2, env.ff2_in)

        @block.gpsimd
        def _(pool):
            pool.memset(env.ident[:, :], 0.0).then_inc(pool_init, 1)
            pool.wait_ge(pool_init, 1)
            pool.affine_select(out=env.ident[:, :], in_=env.ident[:, :], compare_op=ALU.not_equal,
                               fill=1.0, base=0, pattern=[[-1, P]], channel_multiplier=1)\
                .then_inc(pool_init, 1)
            pool.memset(env.nhalf[:, :], -0.5).then_inc(pool_init, 1)
            pool.memset(nhalf1[:, :], -0.5).then_inc(pool_init, 1)
            for mask, hd in ((env.head_mask8, 8), (env.head_mask16, 16)):
                n = P // hd
                pool.memset(mask[:, :], 1.0).then_inc(env.masks_made, 1)
            for k, (mask, hd) in enumerate(((env.head_mask8, 8), (env.head_mask16, 16))):
                n = P // hd
                pool.wait_ge(env.masks_made, 2 + 2 * k)
                pool.affine_select(out=mask[:, :], in_=mask[:, :], compare_op=ALU.is_ge, fill=0.0,
                                   base=0, pattern=[[-hd, n]], channel_multiplier=1)\
                    .then_inc(env.masks_made, 1)
                pool.wait_ge(env.masks_made, 3 + 2 * k)
                pool.affine_select(out=mask[:, :], in_=mask[:, :], compare_op=ALU.is_ge, fill=0.0,
                                   base=hd - 1, pattern=[[hd, n]], channel_multiplier=-1)\
                    .then_inc(env.masks_made, 1)
            pool.wait_ge(bn, 1)
            pool.tensor_tensor(inv[:, 1:2], inv[:, 0:1], nhalf1[:, :], ALU.pow).then_inc(bn_pow, 1)

        @block.tensor
        def _(pe):
            pe.wait_ge(pool_init, 2)
            pe.wait_ge(rows_in, env.rows_count)
            for t, n in enumerate(used):
                mm = pe.transpose(env.bank[0][:, P * t:P * t + n], rows[t][0:n, :], env.ident[0:n, 0:n])
            mm.then_inc(cols_up, 1)
            pe.wait_ge(nl_in, 16 * 7)
            pe.transpose(env.bank[1][:, 0:P], pg_w[:, :], env.ident[:, :])
            pe.transpose(env.bank[1][0:CI, P:2 * P], w_w[:, :], env.ident[:, :]).then_inc(nl_wt_up, 1)
            pe.wait_ge(ctx_in, 16)
            for c in range(KC):
                for half in range(NHALF):
                    n = c * NHALF + half
                    for k in range(4):
                        b = half * 4 + k
                        mm = pe.transpose(env.bank[2 + n][:, k * P:(k + 1) * P],
                                          ctx_tok[:, b, c * P:(c + 1) * P], env.ident[:, :])
                    mm.then_inc(ctx_up, 1)
            pe.wait_ge(nl_wt_down, 1)
            pe.wait_ge(cols_down, 1)
            pe.wait_ge(ctx_down, NHALF * KC)
            for b in range(B):
                if b >= 2:
                    pe.wait_ge(pg_down, b - 1)
                for c in range(KC):
                    mm = pe.matmul(env.bank[b % 2][:, c * P:(c + 1) * P], ctx_tok[:, b, c * P:(c + 1) * P],
                                   pg_wT[:, :], start=True, stop=True)
                mm.then_inc(pg_up, 1)
                pe.wait_ge(pg_down, b + 1)
                if b >= 1:
                    pe.wait_ge(mt_down, b)
                for c in range(KC):
                    mm = pe.matmul(env.bank[2][0:CI, 0:CI], pg[:, b % 2, c, CI:P], pg[:, b % 2, c, 0:CI],
                                   start=c == 0, stop=c == KC - 1)
                mm.then_inc(mt_up, 1)
                pe.wait_ge(mt_down, b + 1)
                if b >= 1:
                    pe.wait_ge(pt_down, b)
                pe.matmul(env.bank[3][0:CI, 0:P], mT[:, b % 2, :], w_wT[:, :], start=True, stop=True)\
                    .then_inc(pt_up, 1)
                pe.wait_ge(pt_down, b + 1)
                if b >= 1:
                    pe.wait_ge(qt_down, b)
                pe.matmul(env.bank[4][:, 0:P], theta_w[:, :], pT[:, b % 2, :], start=True, stop=True)
                pe.matmul(env.bank[4][:, P:P + 1], pT[:, b % 2, :], theta_b[:, 0:1], start=True, stop=True)\
                    .then_inc(qt_up, 1)

        @block.scalar
        def _(act):
            act.dma_start(pg_w[0:CI, :], a["L1_xattn_phi_w"]).then_inc(nl_in, 16)
            act.dma_start(pg_w[CI:P, :], a["L1_xattn_g_w"]).then_inc(nl_in, 16)
            act.dma_start(w_w[:, :], a["L1_xattn_w_w"]).then_inc(nl_in, 16)
            act.dma_start(theta_w[:, :], a["L1_xattn_theta_w"]).then_inc(nl_in, 16)
            with nc.allow_non_contiguous_dma(reason="64 values, one to a partition"):
                act.dma_start(theta_b[:, 0:1], a["L1_xattn_theta_b"].rearrange("(c a) -> c a", a=1))\
                    .then_inc(nl_in, 16)
            for k, name in enumerate(("phi_b", "g_b")):
                act.dma_start(pg_bias[:, k * CI:(k + 1) * CI],
                              a["L1_xattn_" + name].rearrange("(a n) -> a n", a=1).to_broadcast([P, CI]))\
                    .then_inc(nl_in, 16)
            act.dma_start(ctx_tok[:, :, :], a["ctx_2048"].rearrange("b s d -> s b d")).then_inc(ctx_in, 16)
            act.wait_ge(nl_wt_up, 1)
            act.activation(pg_wT[:, :], env.bank[1][:, 0:P], ACT.Copy)
            act.activation(w_wT[:, :], env.bank[1][0:CI, P:2 * P], ACT.Copy).then_inc(nl_wt_down, 1)
            for n in range(KC * NHALF):
                c, half = divmod(n, NHALF)
                act.wait_ge(ctx_up, n + 1)
                act.activation(ctx_f[:, c, half * HALF:(half + 1) * HALF], env.bank[2 + n][:, :], ACT.Copy)\
                    .then_inc(ctx_down, 1)
            for b in range(B):
                act.wait_ge(mt_up, b + 1)
                act.activation(mT[:, b % 2, :], env.bank[2][0:CI, 0:CI], ACT.Copy).then_inc(mt_down, 1)
                act.wait_ge(pt_up, b + 1)
                act.activation(pT[:, b % 2, :], env.bank[3][0:CI, 0:P], ACT.Copy, scale=1.0 / N1)\
                    .then_inc(pt_down, 1)
                act.wait_ge(qt_up, b + 1)
                act.activation(env.qT1[:, b, :], env.bank[4][:, 0:P + 1], ACT.Copy).then_inc(qt_down, 1)

        @block.vector
        def _(dve):
            dve.wait_ge(cols_up, 1)
            for t, n in enumerate(used):
                ins = dve.tensor_copy(env.cols[t][:, 0:n], env.bank[0][:, P * t:P * t + n])
            ins.then_inc(cols_down, 1)
            dve.wait_ge(cols_down, 1)
            dve.tensor_scalar(inv[:, 0:1], env.col("L1_xattn_bn_var"), 1e-5, None, ALU.add).then_inc(bn, 1)
            for n in range(KC * NHALF):
                c, half = divmod(n, NHALF)
                dve.wait_ge(ctx_down, n + 1)
                part = (slice(None), c, slice(half * HALF, (half + 1) * HALF))
                dve.tensor_copy(env.ctx_hi[part], ctx_f[part]).then_inc(ctx_split, 1)
                dve.wait_ge(ctx_split, n + 1)
                dve.tensor_tensor(env.ctx_lo[part], ctx_f[part], f32_view(env.ctx_hi[part]), ALU.subtract)
            for b in range(B):
                dve.wait_ge(pg_up, b + 1)
                if b >= 2:
                    dve.wait_ge(mt_up, b - 1)
                dve.tensor_tensor(pg[:, b % 2, :, :],
                                  env.bank[b % 2][:, 0:KC * P].rearrange("p (c n) -> p c n", n=P),
                                  pg_bias[:, :].unsqueeze(1).to_broadcast([P, KC, P]), ALU.add)\
                    .then_inc(pg_down, 1)
            dve.wait_ge(bn_pow, 1)
            dve.tensor_tensor(env.bn_scale[:, :], env.col("L1_xattn_bn_gamma"), inv[:, 1:2], ALU.mult)\
                .then_inc(bn, 1)
            dve.tensor_tensor(inv[:, 0:1], env.col("L1_xattn_w_b"), env.col("L1_xattn_bn_mean"), ALU.subtract)\
                .then_inc(bn, 1)
            dve.wait_ge(qt_down, B)
            dve.wait_ge(bn, 3)
            dve.tensor_scalar(env.bn_shift[:, :], env.qT1[:, :, P], inv[:, 0:1], env.bn_scale[:, 0:1],
                              ALU.add, ALU.mult).then_inc(bn, 1)
            dve.wait_ge(bn, 4)
            dve.tensor_scalar(env.bn_shift[:, :], env.bn_shift[:, :], env.col("L1_xattn_bn_beta"), None,
                              ALU.add).then_inc(bn, 1)


class Norm:

    def __init__(self, env, sb, name, gamma, beta, eps, banks):
        self.env, self.gamma, self.beta, self.eps, self.banks = env, gamma, beta, eps, banks
        if eps:
            self.stats = sb(name + "_stats", [P, B, 6])
            self.mv = sb(name + "_mv", [P, B, 2])
            self.ve = sb(name + "_ve", [P, B])
            self.rstd = sb(name + "_rstd", [P, B])
        self.xn = sb(name + "_xn", [P, B, D]) if eps else env.x
        self.full = sb(name + "_full", [P, KC, TOK])
        self.stats_done = env.sem(name + "_stats_done")
        self.aggregated = env.sem(name + "_aggregated")
        self.rstd_done = env.sem(name + "_rstd_done")
        self.normed = env.sem(name + "_normed")
        self.turned = env.sem(name + "_turned")
        self.evacuated = env.sem(name + "_evacuated")
        self.hi_done = env.sem(name + "_hi_done")
        self.h_ready = env.sem(name + "_h_ready")

    def dve_stats(self, dve, half):
        x = self.env.x
        own = range(half * 4, half * 4 + 4)
        for b in own:
            dve.bn_stats(self.stats[:, b, :], x[:, b, :]).then_inc(self.stats_done, 1)
        for b in own:
            dve.wait_ge(self.stats_done, b + 1)
            ins = dve.bn_aggr(self.mv[:, b, :], self.stats[:, b, :])
        ins.then_inc(self.aggregated, 1)
        dve.wait_ge(self.aggregated, 2 * half + 1)
        dve.tensor_scalar(self.ve[:, half * 4:half * 4 + 4], self.mv[:, half * 4:half * 4 + 4, 1], self.eps,
                          None, ALU.add).then_inc(self.aggregated, 1)

    def pool_rstd(self, pool, half):
        own = slice(half * 4, half * 4 + 4)
        pool.wait_ge(self.aggregated, 2 * half + 2)
        pool.tensor_tensor(self.rstd[:, own], self.ve[:, own], self.env.nhalf[:, own], ALU.pow)\
            .then_inc(self.rstd_done, 1)

    def dve_normalise(self, dve, half):
        dve.wait_ge(self.rstd_done, half + 1)
        for b in range(half * 4, half * 4 + 4):
            dve.tensor_scalar(self.xn[:, b, :], self.env.x[:, b, :], self.mv[:, b, 0:1],
                              self.rstd[:, b:b + 1], ALU.subtract, ALU.mult).then_inc(self.normed, 1)

    def pe_turn(self, pe, half):
        for c in range(KC):
            wait(pe, self.evacuated, KC * (half - 1) + c + 1)
            for k in range(4):
                b = half * 4 + k
                if self.eps and c == 0:
                    pe.wait_ge(self.normed, b + 1)
                mm = pe.transpose(self.banks[c][:, k * P:(k + 1) * P], self.xn[:, b, c * P:(c + 1) * P],
                                  self.env.ident[:, :])
            mm.then_inc(self.turned, 1)

    def act_evacuate(self, act, half):
        for c in range(KC):
            out = self.full[:, c, half * HALF:(half + 1) * HALF]
            act.wait_ge(self.turned, KC * half + c + 1)
            if self.eps:
                ins = act.activation(out, self.banks[c][:, :], ACT.Identity, scale=self.gamma[:, c:c + 1],
                                     bias=self.beta[:, c:c + 1])
            else:
                ins = act.activation(out, self.banks[c][:, :], ACT.Copy)
            ins.then_inc(self.evacuated, 1)

    def dve_split(self, dve, half):
        env = self.env
        for c in range(KC):
            n = KC * half + c
            part = (slice(None), c, slice(half * HALF, (half + 1) * HALF))
            dve.wait_ge(self.evacuated, n + 1)
            dve.tensor_copy(env.h_hi[part], self.full[part]).then_inc(self.hi_done, 1)
            dve.wait_ge(self.hi_done, n + 1)
            dve.tensor_tensor(env.h_lo[part], self.full[part], f32_view(env.h_hi[part]), ALU.subtract)\
                .then_inc(self.h_ready, 1)

    def dve_all(self, dve):
        if self.eps:
            for half in range(NHALF):
                self.dve_stats(dve, half)
            for half in range(NHALF):
                self.dve_normalise(dve, half)
        for half in range(NHALF):
            self.dve_split(dve, half)

    def pool_all(self, pool):
        if self.eps:
            for half in range(NHALF):
                self.pool_rstd(pool, half)


class Weights:

    def __init__(self, raw, hi, lo, by_pool):
        self.raw, self.hi, self.lo, self.by_pool = raw, hi, lo, by_pool
        self.done = None


def feature_products(w, a_hi, a_lo, out, bias):
    jobs = []
    for half in range(NHALF):
        for f in range(out.shape[1]):
            cols = slice(half * HALF, (half + 1) * HALF)
            jobs.append(Product(
                lhs=[(w.hi[:, c, f * P:(f + 1) * P], w.lo[:, c, f * P:(f + 1) * P]) for c in range(KC)],
                rhs=[(a_hi[:, c, cols], a_lo[:, c, cols]) for c in range(KC)],
                n=HALF, out=out[:, f, cols], bias=bias[:, f:f + 1], weights=w, half=half))
    return jobs


def token_products(w, a_hi, a_lo, out, heads, hd):
    jobs = []
    for b in range(B):
        cols = slice(b * S, (b + 1) * S)
        jobs.append(Product(
            lhs=[(a_hi[:, c, cols], a_lo[:, c, cols]) for c in range(KC)],
            rhs=[(w.hi[:, c, :], w.lo[:, c, :]) for c in range(KC)],
            n=heads * hd, out=out[:, b, :, 0:hd], bias=None, weights=w, half=b // 4))
    return jobs


def project(env, sb, name, gamma, beta, eps, weights, early, jobs, add_bias, waits_act=(), waits_pool=(),
            pool_first=None, ones=None):
    nc = env.nc
    norm = Norm(env, sb, name + "_ln", gamma, beta, eps, env.bank[6:8])
    NB = 6
    hi_act = env.sem(name + "_hi_act")
    lo_dve = env.sem(name + "_lo_dve")
    hi_pool, lo_pool = env.sem(name + "_hi_pool"), env.sem(name + "_lo_pool")
    up, down = env.sem(name + "_up"), env.sem(name + "_down")
    pooled = [w for w in weights if w.by_pool]
    others = [w for w in weights if not w.by_pool]
    for i, w in enumerate(pooled):
        w.done = (lo_pool, i + 1)
    for i, w in enumerate(others):
        w.done = (lo_dve, i + 1)
    with nc.Block() as block:
        @block.gpsimd
        def _(pool):
            for sem, value in waits_pool:
                pool.wait_ge(sem, value)
            if pool_first:
                pool_first(pool)
            for i, w in enumerate(pooled):
                pool.tensor_copy(w.hi, w.raw).then_inc(hi_pool, 1)
                pool.wait_ge(hi_pool, i + 1)
                pool.tensor_tensor(w.lo, w.raw, f32_view(w.hi), ALU.subtract).then_inc(lo_pool, 1)
            norm.pool_all(pool)
            pool.memset(ones, 1.0)
            pool.wait_ge(norm.evacuated, KC * NHALF)
            pool.tensor_tensor(env.x[:, :, :], env.x[:, :, :],
                               add_bias[:, :].unsqueeze(1).to_broadcast([P, B, D]), ALU.add)

        @block.tensor
        def _(pe):
            def run(batch, start):
                for i, job in enumerate(batch, start):
                    pe.wait_ge(*job.weights.done)
                    wait(pe, down, i - NB + 1)
                    if batch is jobs:
                        pe.wait_ge(norm.h_ready, KC * (job.half + 1))
                    split_product(pe, env.bank[i % NB][:, 0:job.n], job.lhs, job.rhs, True, True)\
                        .then_inc(up, 1)

            run(early, 0)
            if not eps:
                pe.wait_ge(env.x_in, 16)
            for half in range(NHALF):
                norm.pe_turn(pe, half)
            run(jobs, len(early))

        @block.scalar
        def _(act):
            for sem, value in waits_act:
                act.wait_ge(sem, value)
            for w in others:
                act.activation(w.hi, w.raw, ACT.Copy).then_inc(hi_act, 1)

            def run(batch, start):
                for i, job in enumerate(batch, start):
                    act.wait_ge(up, i + 1)
                    src = env.bank[i % NB][:, 0:job.n]
                    if job.bias is None:
                        src = src.rearrange("p (h d) -> p h d", d=job.out.shape[-1])
                        ins = act.activation(job.out, src, ACT.Copy)
                    else:
                        ins = act.activation(job.out, src, ACT.Identity, bias=job.bias)
                    ins.then_inc(down, 1)

            run(early, 0)
            for half in range(NHALF):
                norm.act_evacuate(act, half)
            run(jobs, len(early))

        @block.vector
        def _(dve):
            for i, w in enumerate(others):
                dve.wait_ge(hi_act, i + 1)
                dve.tensor_tensor(w.lo, w.raw, f32_view(w.hi), ALU.subtract).then_inc(lo_dve, 1)
            norm.dve_all(dve)


def short_head_attention(env, name, heads, hd, kv_heads, scale, mask, per_sequence, multiply,
                         head_mask, q_all, k_all, v_all, w_o, v_bias):
    nc = env.nc
    dve_evacuates = not multiply
    NG = heads // 4
    HC = P // hd
    BODY = 2 * NG
    W = hd + 1
    LT, LP = 3, 4
    LO, LW = LP + NG, LP + NG + 2
    with ExitStack() as stack:
        sb = env.scoped(stack)
        keys = sb(name + "_keys", [P, 2, KC, HC, P])
        qs = sb(name + "_qs", [P, 2, KC, S])
        masked = sb(name + "_masked", [P, 4, 4, S])
        shift = None if not multiply else sb(name + "_shift", [P, mask.shape[1], S])
        nmax = sb(name + "_nmax", [P, 4, 4])
        probs = sb(name + "_probs", [P, 4, 4, S])
        probsT = sb(name + "_probsT", [P, 2, 4 * S])
        rinv = sb(name + "_rinv", [P, 2, heads])
        heads_out = sb(name + "_heads_out", [P, 2, D])
        heads_outT = sb(name + "_heads_outT", [P, 2, KC * S])
        SB, TB, OB, TOB, WB = env.bank[0:2], env.bank[2:4], env.bank[4:6], env.bank[6], env.bank[7]
        staged = env.sem(name + "_staged")
        scores_up = env.sem(name + "_scores_up")
        masked_done = env.sem(name + "_masked")
        shifted = env.sem(name + "_shifted")
        max_done = env.sem(name + "_max")
        exp_done = env.sem(name + "_exp")
        turned = env.sem(name + "_turned")
        turned_out = env.sem(name + "_turned_out")
        pv_done = env.sem(name + "_pv")
        rinv_done = env.sem(name + "_rinv")
        normed = env.sem(name + "_normed")
        heads_turned = env.sem(name + "_heads_turned")
        heads_turned_out = env.sem(name + "_heads_turned_out")
        out_up = env.sem(name + "_out_up")
        added = env.sem(name + "_added")
        shift_done = env.sem(name + "_shift_done")
        block = stack.enter_context(nc.Block())
        LOOPS = B // 2

        def run(step, engine):
            for s in range(BODY):
                step(0, s, lambda lag, s=s: s >= lag, True)
            with engine.Fori(1, B // 2) as it:
                for s in range(BODY):
                    step(it * 2, s, lambda lag: True, True)
            for s in range(LW):
                step(B, s, lambda lag, s=s: s < lag, False)

        def take_turned(engine, g, s):
            wait(engine, turned, g - LT + 1)
            wait(engine, pv_done, g - LT - 1)
            out = probsT[:, (s - LT) % 2, :]
            copy = (lambda: engine.tensor_copy(out, TB[s % 2][:, :])) if dve_evacuates else \
                (lambda: engine.activation(out, TB[s % 2][:, :], ACT.Copy))
            copy().then_inc(turned_out, 1)

        @block.gpsimd
        def _(pool):
            def stage(b, par):
                wait(pool, scores_up, (b - 1) * NG)
                for c in range(KC):
                    pool.tensor_tensor(keys[:, par, c, :, :],
                                       k_all[:, c, bass.ds(b * S, S)].unsqueeze(1).to_broadcast([P, HC, S]),
                                       head_mask[:, :].unsqueeze(2).to_broadcast([P, HC, S]), ALU.mult)
                pool.tensor_copy(qs[:, par, :, :], q_all[:, :, bass.ds(b * S, S)]).then_inc(staged, 1)

            stage(0, 0)
            stage(1, 1)
            with pool.Fori(1, B // 2) as it:
                for par in range(2):
                    stage(it * 2 + par, par)

        @block.tensor
        def _(pe):
            def step(seq0, s, live, on):
                g = seq0 * NG + s
                if on:
                    par, grp = s // NG, s % NG
                    c, first = (grp * 4) // HC, (grp * 4) % HC
                    if grp == 0:
                        wait(pe, staged, seq0 + par + 1)
                    wait(pe, masked_done, g - 1)
                    pe.matmul(SB[s % 2][:, :], qs[:, par, c, :], keys[:, par, c, first:first + 4, :],
                              start=True, stop=True).then_inc(scores_up, 1)
                if live(LT):
                    wait(pe, exp_done, g - LT + 1)
                    wait(pe, turned_out, g - LT - 1)
                    for h in range(4):
                        mm = pe.transpose(TB[s % 2][:, h * S:(h + 1) * S], probs[:, (s - LT) % 4, h, :],
                                          env.ident[:, :])
                    mm.then_inc(turned, 1)
                if live(LP):
                    par, grp = ((s - LP) // NG) % 2, (s - LP) % NG
                    b = seq0 + (s - LP) // NG
                    wait(pe, turned_out, g - LP + 1)
                    for h in range(4):
                        head = grp * 4 + h
                        kv = head * kv_heads // heads
                        mm = pe.matmul(OB[par][:, head * W:(head + 1) * W],
                                       probsT[:, (s - LP) % 2, h * S:(h + 1) * S],
                                       v_all[:, bass.ds(b, 1), kv, :].rearrange("p o w -> p (o w)"),
                                       start=True, stop=True)
                    mm.then_inc(pv_done, 1)
                if (s - LO) % NG == 0 and live(LO):
                    par, seq = ((s - LO) // NG) % 2, seq0 + (s - LO) // NG
                    wait(pe, normed, seq + 1)
                    for c in range(KC):
                        mm = pe.transpose(TOB[:, c * S:(c + 1) * S], heads_out[:, par, c * P:(c + 1) * P],
                                          env.ident[:, :])
                    mm.then_inc(heads_turned, 1)
                if (s - LW) % NG == 0 and live(LW):
                    par, seq = ((s - LW) // NG) % 2, seq0 + (s - LW) // NG
                    wait(pe, heads_turned_out, seq + 1)
                    wait(pe, added, seq + 1)
                    for c in range(KC):
                        mm = pe.matmul(WB[:, 0:D], heads_outT[:, par, c * S:(c + 1) * S], w_o[:, c, :],
                                       start=c == 0, stop=c == KC - 1)
                    mm.then_inc(out_up, 1)

            run(step, pe)

        @block.scalar
        def _(act):
            def step(seq0, s, live, on):
                g = seq0 * NG + s
                if live(LT) and not dve_evacuates:
                    take_turned(act, g, s)
                if on:
                    wait(act, max_done, g + 1)
                    wait(act, turned, g - 3)
                    for h in range(4):
                        ins = act.activation(probs[:, s % 4, h, :], masked[:, s % 4, h, :], ACT.Exp,
                                             bias=nmax[:, s % 4, h:h + 1])
                    ins.then_inc(exp_done, 1)
                if (s - LO) % NG == 0 and live(LO):
                    par, seq = ((s - LO) // NG) % 2, seq0 + (s - LO) // NG
                    wait(act, heads_turned, seq + 1)
                    for c in range(KC):
                        ins = act.activation(heads_outT[:, par, c * S:(c + 1) * S], TOB[:, c * S:(c + 1) * S],
                                             ACT.Identity, bias=v_bias[:, c:c + 1])
                    ins.then_inc(heads_turned_out, 1)

            run(step, act)

        @block.vector
        def _(dve):
            dve.sem_inc(added, 1)
            dve.wait_ge(env.mask_in, 16)
            if multiply:
                dve.tensor_scalar(shift[:, :, :], mask[:, :, :], 10000.0, -10000.0, ALU.mult, ALU.add)\
                    .then_inc(shift_done, 1)
                dve.wait_ge(shift_done, 1)

            def step(seq0, s, live, on):
                g = seq0 * NG + s
                if on:
                    b = seq0 + s // NG if per_sequence else 0
                    wait(dve, scores_up, g + 1)
                    wait(dve, exp_done, g - 3)
                    dve.scalar_tensor_tensor(masked[:, s % 4, :, :],
                                             SB[s % 2][:, :].rearrange("p (h n) -> p h n", n=S), scale,
                                             mask[:, bass.ds(b, 1), :].to_broadcast([P, 4, S]),
                                             ALU.mult, ALU.mult if multiply else ALU.add)\
                        .then_inc(masked_done, 1)
                    wait(dve, masked_done, g + 1)
                    if multiply:
                        dve.tensor_tensor(masked[:, s % 4, :, :], masked[:, s % 4, :, :],
                                          shift[:, bass.ds(b, 1), :].to_broadcast([P, 4, S]), ALU.add)\
                            .then_inc(shifted, 1)
                        wait(dve, shifted, g + 1)
                    dve.tensor_reduce(nmax[:, s % 4, :], masked[:, s % 4, :, :], X, ALU.max, negate=True)\
                        .then_inc(max_done, 1)
                if live(LT) and dve_evacuates:
                    take_turned(dve, g, s)
                if (s - LP) % NG == NG - 1 and live(LP):
                    k = (s - LP) // NG
                    par, seq = k % 2, seq0 + k
                    o = OB[par][:, 0:heads * W].rearrange("p (h w) -> p h w", w=W)
                    wait(dve, pv_done, g - LP + 1)
                    dve.reciprocal(rinv[:, par, :], o[:, :, hd]).then_inc(rinv_done, 1)
                    wait(dve, rinv_done, seq + 1)
                    dve.tensor_tensor(heads_out[:, par, :].rearrange("p (h d) -> p h d", d=hd), o[:, :, 0:hd],
                                      rinv[:, par, :].unsqueeze(2).to_broadcast([P, heads, hd]), ALU.mult)\
                        .then_inc(normed, 1)
                if (s - LW) % NG == 0 and live(LW):
                    seq = seq0 + (s - LW) // NG
                    wait(dve, out_up, seq + 1)
                    xb = env.x[:, bass.ds(seq, 1), :].rearrange("p o d -> p (o d)")
                    dve.tensor_tensor(xb, WB[:, 0:D], xb, ALU.add).then_inc(added, 1)

            run(step, dve)


def norm_token_major(env, name, eps, gamma, beta):
    nc = env.nc
    with ExitStack() as stack:
        sb = env.scoped(stack)
        stats = sb(name + "_stats", [P, B, 6])
        mv = sb(name + "_mv", [P, B, 2])
        ve = sb(name + "_ve", [P, B])
        rstd = sb(name + "_rstd", [P, B])
        stats_done = env.sem(name + "_stats_done")
        rstd_done = env.sem(name + "_rstd_done")
        normed = env.sem(name + "_normed")
        scaled = env.sem(name + "_scaled")
        block = stack.enter_context(nc.Block())

        @block.vector
        def _(dve):
            for b in range(B):
                dve.bn_stats(stats[:, b, :], env.x[:, b, :]).then_inc(stats_done, 1)
            for b in range(B):
                dve.wait_ge(stats_done, b + 1)
                ins = dve.bn_aggr(mv[:, b, :], stats[:, b, :])
            ins.then_inc(stats_done, 1)
            dve.wait_ge(stats_done, B + 1)
            dve.tensor_scalar(ve[:, :], mv[:, :, 1], eps, None, ALU.add).then_inc(stats_done, 1)
            dve.wait_ge(rstd_done, 1)
            for b in range(B):
                dve.tensor_scalar(env.x[:, b, :], env.x[:, b, :], mv[:, b, 0:1], rstd[:, b:b + 1],
                                  ALU.subtract, ALU.mult).then_inc(normed, 1)
            for half in range(2):
                xh = env.x[:, half * 4:half * 4 + 4, :]
                dve.wait_ge(normed, 4 * half + 4)
                dve.tensor_tensor(xh, xh, gamma[:, :].unsqueeze(1).to_broadcast([P, 4, D]), ALU.mult)\
                    .then_inc(scaled, 1)
            for half in range(2):
                xh = env.x[:, half * 4:half * 4 + 4, :]
                dve.wait_ge(scaled, half + 1)
                dve.tensor_tensor(xh, xh, beta[:, :].unsqueeze(1).to_broadcast([P, 4, D]), ALU.add)

        @block.gpsimd
        def _(pool):
            pool.wait_ge(stats_done, B + 2)
            pool.tensor_tensor(rstd[:, :], ve[:, :], env.nhalf[:, 0:B], ALU.pow).then_inc(rstd_done, 1)


def non_local(env):
    nc = env.nc
    with ExitStack() as stack:
        sb = env.scoped(stack)
        wy = sb("wy", [P, B, D])
        up, scaled = env.sem("nl_up"), env.sem("nl_scaled")
        block = stack.enter_context(nc.Block())

        @block.tensor
        def _(pe):
            for b in range(B):
                pe.matmul(env.bank[b][:, 0:D], env.qT1[:, b, 0:P], env.x[:, b, :], start=True, stop=True)\
                    .then_inc(up, 1)

        @block.scalar
        def _(act):
            for b in range(B):
                act.wait_ge(up, b + 1)
                act.activation(wy[:, b, :], env.bank[b][:, 0:D], ACT.Identity, scale=env.bn_scale[:, 0:1],
                               bias=env.bn_shift[:, b:b + 1]).then_inc(scaled, 1)

        @block.vector
        def _(dve):
            for b in range(B):
                dve.wait_ge(scaled, b + 1)
                dve.tensor_tensor(env.x[:, b, :], env.x[:, b, :], wy[:, b, :], ALU.add)


def long_head_attention(env, name, a, gamma, beta, wq, wk, wv, wo, bq, bk, bv, bias_k, bias_v, bo):
    nc = env.nc
    H, K, PAIRS = 16, P, 8
    T = S + 2
    SCALE = float(K) ** -0.5
    GR = H + 2
    PREP_DONE = 6
    LT, LP, LW = 1, 2, 3
    with ExitStack() as stack:
        sb = env.scoped(stack)
        w_raw = sb(name + "_w_raw", [P, 2, 3, KC, 2 * K])
        w_hi = sb(name + "_w_hi", [P, 2, 3, KC, 2 * K], F32R)
        w_lo = sb(name + "_w_lo", [P, 2, 3, KC, 2 * K], F32R)
        wo_raw = sb(name + "_wo_raw", [P, 2, 2, D])
        wo_hi = sb(name + "_wo_hi", [P, 2, 2, D], F32R)
        wo_lo = sb(name + "_wo_lo", [P, 2, 2, D], F32R)
        qT = sb(name + "_qT", [P, 2, 2, TOK])
        kT = sb(name + "_kT", [P, 2, 2, B, T])
        v = sb(name + "_v", [P, 2, B, 2 * K])
        bq_scaled = sb(name + "_bq_scaled", [P, H])
        extra = sb(name + "_extra", [P, H, GR])
        extra_hi = sb(name + "_extra_hi", [P, H, GR], F32R)
        extra_lo = sb(name + "_extra_lo", [P, H, GR], F32R)
        extra_now = sb(name + "_extra_now", [P, 2, 2, 2, GR], F32R)
        wb = sb(name + "_wb", [P, B, GR])
        wbT = sb(name + "_wbT", [GR, 2, P])
        G = sb(name + "_G", [GR, D])
        nmax = sb(name + "_nmax", [P, 2, 2])
        den = sb(name + "_den", [P, 2, 2])
        rinv = sb(name + "_rinv", [P, 2, 2])
        probs = sb(name + "_probs", [P, 2, 2, T])
        probs_n = sb(name + "_probs_n", [P, 2, 2, S + 1])
        probsT = sb(name + "_probsT", [P, 2, 2 * S])
        o_hi = sb(name + "_o_hi", [P, 2, 2 * S], F32R)
        o_lo = sb(name + "_o_lo", [P, 2, 2 * S], F32R)
        SB, KQB, VB = env.bank[0:2], env.bank[2], env.bank[3]
        TB, OB, WB, GB = env.bank[4], env.bank[5], env.bank[6], env.bank[7]
        sem = lambda s: env.sem(name + "_" + s)
        w_in = [sem("w_in0"), sem("w_in1")]
        wo_in = [sem("wo_in0"), sem("wo_in1")]
        w_split = sem("w_split")
        wo_split = sem("wo_split")
        side = sem("side")
        prep = sem("prep")
        kq_up, kq_down = sem("kq_up"), sem("kq_down")
        v_up, v_down = sem("v_up"), sem("v_down")
        scores_up = sem("scores_up")
        max_done = sem("max")
        exp_done = sem("exp")
        rinv_done = sem("rinv")
        scaled = sem("scaled")
        turned, turned_out = sem("turned"), sem("turned_out")
        pv_done = sem("pv")
        o_hi_done, o_lo_done = sem("o_hi"), sem("o_lo")
        out_up, added = sem("out_up"), sem("added")
        g_done = sem("g_done")
        wb_done = sem("wb_done")
        g_out = sem("g_out")
        wb_up, wb_down = sem("wb_up"), sem("wb_down")
        rest_up, rest_added = sem("rest_up"), sem("rest_added")
        bo_added = sem("bo_added")
        act_gate, pool_gate = sem("act_gate"), sem("pool_gate")
        norm = Norm(env, sb, name + "_ln", gamma, beta, 1e-5, SB)
        block = stack.enter_context(nc.Block())

        w_dram = [w.rearrange("(c p) n -> p c n", p=P) for w in (a[wq], a[wk], a[wv])]
        wo_dram = a[wo].rearrange("(h d) n -> d h n", d=K)

        def run(step, engine):
            for b in range(B):
                step(0, 0, b, lambda lag, b=b: b >= lag, True, True)
            with engine.Fori(0, 3) as it:
                for k in range(2):
                    for b in range(B):
                        step(it * 2 + 1 + k, (1 + k) % 2, b, lambda lag: True, True, True)
            for b in range(B):
                step(PAIRS - 1, (PAIRS - 1) % 2, b, lambda lag: True, True, False)
            for b in range(LW):
                step(PAIRS, PAIRS % 2, b, lambda lag, b=b: b < lag, False, False)

        @block.sync
        def _(sp):
            def load_qkv(pair, par):
                wait(sp, w_split, 2 * (pair - 1))
                for k in range(3):
                    sp.dma_start(w_raw[:, par, k, :, :], w_dram[k][:, :, bass.ds(pair * 2 * K, 2 * K)])\
                        .then_inc(w_in[par], 16)

            def load_o(pair, par):
                wait(sp, wo_split, 2 * (pair - 1))
                sp.dma_start(wo_raw[:, par, :, :], wo_dram[:, bass.ds(pair * 2, 2), :]).then_inc(wo_in[par], 16)

            for pair in range(2):
                load_qkv(pair, pair)
                load_o(pair, pair)
            with sp.Fori(1, PAIRS // 2) as it:
                for par in range(2):
                    load_qkv(it * 2 + par, par)
                    load_o(it * 2 + par, par)

        @block.gpsimd
        def _(pool):
            def split_qkv(pair, par, turn):
                wait(pool, w_in[par], 48 * (turn + 1))
                wait(pool, kq_up, 8 * (pair - 1))
                wait(pool, v_up, 8 * (pair - 1))
                pool.sem_inc(pool_gate, 1)
                pool.tensor_copy(w_hi[:, par], w_raw[:, par]).then_inc(w_split, 1)
                wait(pool, w_split, 2 * pair + 1)
                pool.tensor_tensor(w_lo[:, par], w_raw[:, par], f32_view(w_hi[:, par]), ALU.subtract)\
                    .then_inc(w_split, 1)

            def split_o(pair, par, turn):
                wait(pool, wo_in[par], 16 * (turn + 1))
                wait(pool, out_up, 8 * (pair - 1))
                wait(pool, g_done, pair - 1)
                pool.sem_inc(pool_gate, 1)
                pool.tensor_copy(wo_hi[:, par], wo_raw[:, par]).then_inc(wo_split, 1)
                wait(pool, wo_split, 2 * pair + 1)
                pool.tensor_tensor(wo_lo[:, par], wo_raw[:, par], f32_view(wo_hi[:, par]), ALU.subtract)\
                    .then_inc(wo_split, 1)
                pool.tensor_copy(extra_now[:, par, 0, :, :],
                                 f32_view(extra_hi[:, bass.ds(pair * 2, 2), :]))
                pool.tensor_copy(extra_now[:, par, 1, :, :],
                                 f32_view(extra_lo[:, bass.ds(pair * 2, 2), :]))
                wait(pool, scores_up, 8 * (pair - 1))
                pool.sem_inc(pool_gate, 1)
                pool.tensor_copy(kT[:, par, :, :, S:T],
                                 bias_k[:, bass.ds(pair * 2, 2)].unsqueeze(2).unsqueeze(3)
                                 .to_broadcast([P, 2, B, 2])).then_inc(side, 1)

            split_qkv(0, 0, 0)
            norm.pool_all(pool)
            pool.wait_ge(prep, PREP_DONE)
            split_o(0, 0, 0)
            split_qkv(1, 1, 0)
            pool.wait_ge(norm.normed, B)
            pool.tensor_tensor(env.x[:, :, :], env.x[:, :, :],
                               bo[:, :].unsqueeze(1).to_broadcast([P, B, D]), ALU.add).then_inc(bo_added, 1)
            split_o(1, 1, 0)
            with pool.Fori(1, PAIRS // 2) as it:
                for par in range(2):
                    split_qkv(it * 2 + par, par, it)
                    split_o(it * 2 + par, par, it)

        @block.tensor
        def _(pe):
            def project(pair, par, b):
                if b == 0:
                    wait(pe, w_split, 2 * (pair + 1))
                which, head, half = (1 if b < 4 else 0), (b % 4) // 2, b % 2
                a_hi, a_lo = (env.ctx_hi, env.ctx_lo) if which else (env.h_hi, env.h_lo)
                cols = slice(half * HALF, (half + 1) * HALF)
                if not which and isinstance(pair, int) and pair == 0:
                    pe.wait_ge(norm.h_ready, KC * (half + 1))
                wait(pe, kq_down, 8 * pair + b)
                split_product(pe, KQB[:, :],
                              [(w_hi[:, par, which, c, head * K:(head + 1) * K],
                                w_lo[:, par, which, c, head * K:(head + 1) * K]) for c in range(KC)],
                              [(a_hi[:, c, cols], a_lo[:, c, cols]) for c in range(KC)], True, True)\
                    .then_inc(kq_up, 1)
                cols = slice(b * S, (b + 1) * S)
                wait(pe, v_down, 8 * pair + b)
                split_product(pe, VB[:, 0:2 * K],
                              [(env.ctx_hi[:, c, cols], env.ctx_lo[:, c, cols]) for c in range(KC)],
                              [(w_hi[:, par, 2, c, :], w_lo[:, par, 2, c, :]) for c in range(KC)], True, True)\
                    .then_inc(v_up, 1)

            def step(pair, par, b, live, attend, then_project):
                g = pair * 8 + b
                if attend:
                    if b == 0:
                        wait(pe, side, pair + 1)
                        wait(pe, kq_down, 8 * (pair + 1))
                    wait(pe, max_done, g - 1)
                    wait(pe, exp_done, g - 1)
                    for h in range(2):
                        mm = pe.matmul(SB[b % 2][:, h * T:(h + 1) * T], qT[:, par, h, b * S:(b + 1) * S],
                                       kT[:, par, h, b, :], start=True, stop=True)
                    mm.then_inc(scores_up, 1)
                if then_project:
                    project(pair + 1, 1 - par, b)
                if live(LT):
                    wait(pe, scaled, g - LT + 1)
                    wait(pe, turned_out, g - LT)
                    for h in range(2):
                        mm = pe.transpose(TB[:, h * S:(h + 1) * S], probs_n[:, (b - LT) % 2, h, 0:S],
                                          env.ident[:, :])
                    mm.then_inc(turned, 1)
                if live(LP):
                    own = par if b >= LP else 1 - par
                    if b == LP:
                        wait(pe, v_down, 8 * (pair + 1))
                    wait(pe, turned_out, g - LP + 1)
                    wait(pe, o_lo_done, g - LP)
                    for h in range(2):
                        mm = pe.matmul(OB[:, h * S:(h + 1) * S], v[:, own, (b - LP) % B, h * K:(h + 1) * K],
                                       probsT[:, (b - LP) % 2, h * S:(h + 1) * S], start=True, stop=True)
                    mm.then_inc(pv_done, 1)
                if live(LW):
                    own = par if b >= LW else 1 - par
                    if b == LW:
                        wait(pe, wo_split, 2 * (pair + 1))
                        wait(pe, side, pair + 1)
                    wait(pe, o_lo_done, g - LW + 1)
                    wait(pe, added, g - LW)
                    o = (slice(None), (b - LW) % 2)
                    split_product(pe, WB[:, 0:D],
                                  [(o_hi[o + (slice(h * S, (h + 1) * S),)], o_lo[o + (slice(h * S, (h + 1) * S),)])
                                   for h in range(2)],
                                  [(wo_hi[:, own, h, :], wo_lo[:, own, h, :]) for h in range(2)], True, True)\
                        .then_inc(out_up, 1)
                if attend and b == LW:
                    first = isinstance(pair, int) and pair == 0
                    last = isinstance(pair, int) and pair == PAIRS - 1
                    for h in range(2):
                        lo, hi = extra_now[:, par, 1, h, :], extra_now[:, par, 0, h, :]
                        pe.matmul(GB[0:GR, 0:D], lo, wo_hi[:, par, h, :], start=first and h == 0, stop=False,
                                  skip_group_check=True)
                        pe.matmul(GB[0:GR, 0:D], hi, wo_lo[:, par, h, :], start=False, stop=False,
                                  skip_group_check=True)
                        mm = pe.matmul(GB[0:GR, 0:D], hi, wo_hi[:, par, h, :], start=False,
                                       stop=last and h == 1, skip_group_check=True)
                    mm.then_inc(g_done, 1)

            for b in range(4):
                project(0, 0, b)
            for half in range(NHALF):
                norm.pe_turn(pe, half)
            for b in range(4, B):
                project(0, 0, b)
            run(step, pe)
            for b in range(B):
                pe.wait_ge(wb_done, PAIRS * B + 1)
                wait(pe, wb_down, b - 1)
                pe.transpose(SB[b % 2][0:GR, 0:P], wb[:, b, :], env.ident[:, :]).then_inc(wb_up, 1)
                pe.wait_ge(wb_down, b + 1)
                pe.wait_ge(g_out, 1)
                wait(pe, rest_added, b - 1)
                pe.matmul((KQB, VB)[b % 2][:, 0:D], wbT[:, b % 2, :], G[:, :], start=True, stop=True)\
                    .then_inc(rest_up, 1)

        @block.scalar
        def _(act):
            def project(pair, par, b):
                which, head, half = (1 if b < 4 else 0), (b % 4) // 2, b % 2
                wait(act, kq_up, 8 * pair + b + 1)
                wait(act, scores_up, 8 * (pair - 1))
                act.sem_inc(act_gate, 1)
                at = bass.ds(pair * 2 + head, 1)
                if which:
                    act.activation(kT[:, par, head, half * 4:half * 4 + 4, 0:S],
                                   KQB[:, :].rearrange("p (b t) -> p b t", t=S), ACT.Identity,
                                   bias=bk[:, at]).then_inc(kq_down, 1)
                else:
                    act.activation(qT[:, par, head, half * HALF:(half + 1) * HALF], KQB[:, :], ACT.Identity,
                                   bias=bq_scaled[:, at], scale=SCALE).then_inc(kq_down, 1)
                wait(act, v_up, 8 * pair + b + 1)
                wait(act, pv_done, 8 * (pair - 2) + b + 1)
                act.activation(v[:, par, b, :], VB[:, 0:2 * K], ACT.Copy).then_inc(v_down, 1)

            def step(pair, par, b, live, attend, then_project):
                g = pair * 8 + b
                if attend:
                    wait(act, max_done, g + 1)
                    wait(act, scaled, g - 1)
                    for h in range(2):
                        ins = act.activation(probs[:, b % 2, h, 0:S + 1], SB[b % 2][:, h * T:h * T + S + 1],
                                             ACT.Exp, bias=nmax[:, b % 2, h:h + 1],
                                             accum_out=den[:, b % 2, h:h + 1])
                    ins.then_inc(exp_done, 1)
                if then_project:
                    project(pair + 1, 1 - par, b)
                if live(LP):
                    wait(act, pv_done, g - LP + 1)
                    wait(act, out_up, g - LP - 1)
                    act.activation(o_hi[:, b % 2, :], OB[:, 0:2 * S], ACT.Copy).then_inc(o_hi_done, 1)

            for b in range(4):
                project(0, 0, b)
            for half in range(NHALF):
                norm.act_evacuate(act, half)
            act.wait_ge(prep, 1)
            for b in range(4, B):
                project(0, 0, b)
            run(step, act)
            act.wait_ge(g_done, PAIRS)
            act.activation(G[:, :], GB[0:GR, 0:D], ACT.Copy).then_inc(g_out, 1)
            for b in range(B):
                act.wait_ge(wb_up, b + 1)
                wait(act, rest_up, b - 1)
                act.activation(wbT[:, b % 2, :], SB[b % 2][0:GR, 0:P], ACT.Copy).then_inc(wb_down, 1)


        @block.vector
        def _(dve):
            dve.tensor_scalar(bq_scaled[:, :], bq, SCALE, None, ALU.mult).then_inc(prep, 1)
            dve.memset(extra[:, :, :], 0.0).then_inc(prep, 1)
            dve.wait_ge(prep, 2)
            flat_extra = extra[:, :, :].rearrange("p h g -> p (h g)")
            dve.tensor_tensor(flat_extra[:, 0:(GR + 1) * (H - 1) + 1:GR + 1], bias_v, bv, ALU.subtract)\
                .then_inc(prep, 1)
            dve.tensor_copy(extra[:, :, H], bv).then_inc(prep, 1)
            dve.wait_ge(prep, 4)
            dve.tensor_copy(extra_hi[:, :, :], extra[:, :, :]).then_inc(prep, 1)
            dve.wait_ge(prep, 5)
            dve.tensor_tensor(extra_lo[:, :, :], extra[:, :, :], f32_view(extra_hi[:, :, :]), ALU.subtract)\
                .then_inc(prep, 1)
            dve.memset(wb[:, :, H:H + 1], 1.0)
            dve.memset(wb[:, :, H + 1:GR], 0.0).then_inc(wb_done, 1)
            norm.dve_all(dve)
            dve.wait_ge(bo_added, 1)

            def step(pair, par, b, live, attend, then_project):
                g = pair * 8 + b
                if attend:
                    wait(dve, scores_up, g + 1)
                    wait(dve, exp_done, g - 1)
                    dve.tensor_reduce(nmax[:, b % 2, :],
                                      SB[b % 2][:, 0:2 * T].rearrange("p (h t) -> p h t", t=T)[:, :, 0:S + 1],
                                      X, ALU.max, negate=True).then_inc(max_done, 1)
                    wait(dve, exp_done, g + 1)
                    dve.reciprocal(rinv[:, b % 2, :], den[:, b % 2, :]).then_inc(rinv_done, 1)
                    wait(dve, rinv_done, g + 1)
                    wait(dve, turned, g - 1)
                    wait(dve, wb_done, g)
                    for h in range(2):
                        ins = dve.tensor_scalar(probs_n[:, b % 2, h, :], probs[:, b % 2, h, 0:S + 1],
                                                rinv[:, b % 2, h:h + 1], None, ALU.mult)
                    ins.then_inc(scaled, 1)
                    wait(dve, scaled, g + 1)
                    dve.tensor_copy(wb[:, b, bass.ds(pair * 2, 2)], probs_n[:, b % 2, :, S]).then_inc(wb_done, 1)
                if live(LT):
                    wait(dve, turned, g - LT + 1)
                    wait(dve, pv_done, g - LT - 1)
                    dve.tensor_copy(probsT[:, (b - LT) % 2, :], TB[:, 0:2 * S]).then_inc(turned_out, 1)
                if live(LP):
                    wait(dve, o_hi_done, g - LP + 1)
                    wait(dve, out_up, g - LP - 1)
                    dve.tensor_tensor(o_lo[:, b % 2, :], OB[:, 0:2 * S], f32_view(o_hi[:, b % 2, :]),
                                      ALU.subtract).then_inc(o_lo_done, 1)
                if live(LW):
                    wait(dve, out_up, g - LW + 1)
                    xb = env.x[:, (b - LW) % B, :]
                    dve.tensor_tensor(xb, WB[:, 0:D], xb, ALU.add).then_inc(added, 1)

            run(step, dve)
            for b in range(B):
                dve.wait_ge(rest_up, b + 1)
                dve.wait_ge(added, PAIRS * B)
                dve.tensor_tensor(env.x[:, b, :], (KQB, VB)[b % 2][:, 0:D], env.x[:, b, :], ALU.add)\
                    .then_inc(rest_added, 1)


def feed_forward(env, name, gamma, beta, w1, w2, b1, b2, func, w_in=None, load_next=None, out=None):
    nc = env.nc
    F = w1.shape[2]
    FC = F // P
    with ExitStack() as stack:
        sb = env.scoped(stack)
        w1_hi, w1_lo = sb(name + "_w1_hi", [P, KC, F], F32R), sb(name + "_w1_lo", [P, KC, F], F32R)
        w2_hi, w2_lo = sb(name + "_w2_hi", [P, FC, D], F32R), sb(name + "_w2_lo", [P, FC, D], F32R)
        with ExitStack() as first:
            norm = Norm(env, env.scoped(first), name + "_ln", gamma, beta, 1e-5, env.bank[6:8])
        act_hi = sb(name + "_act_hi", [P, NHALF, FC, HALF], F32R)
        act_lo = sb(name + "_act_lo", [P, NHALF, FC, HALF], F32R)
        act_full = sb(name + "_act", [P, 2, HALF])
        w_hi_done, w_lo_done = env.sem(name + "_w_hi"), env.sem(name + "_w_lo")
        b2_added = env.sem(name + "_b2")
        up, acted = env.sem(name + "_up"), env.sem(name + "_acted")
        hi_done, lo_done = env.sem(name + "_hi"), env.sem(name + "_lo")
        out_up, added = env.sem(name + "_out_up"), env.sem(name + "_added")
        stored = env.sem(name + "_stored")
        NJ = FC * NHALF
        block = stack.enter_context(nc.Block())

        @block.gpsimd
        def _(pool):
            if w_in:
                pool.wait_ge(*w_in)
            count = 0
            for f in range(FC):
                cols = slice(f * P, (f + 1) * P)
                pool.tensor_copy(w1_hi[:, :, cols], w1[:, :, cols]).then_inc(w_hi_done, 1)
                count += 1
                pool.wait_ge(w_hi_done, count)
                pool.tensor_tensor(w1_lo[:, :, cols], w1[:, :, cols], f32_view(w1_hi[:, :, cols]), ALU.subtract)\
                    .then_inc(w_lo_done, 1)
                if f == 1:
                    norm.pool_all(pool)
            for f in range(FC):
                pool.tensor_copy(w2_hi[:, f, :], w2[:, f, :]).then_inc(w_hi_done, 1)
                count += 1
                pool.wait_ge(w_hi_done, count)
                pool.tensor_tensor(w2_lo[:, f, :], w2[:, f, :], f32_view(w2_hi[:, f, :]), ALU.subtract)\
                    .then_inc(w_lo_done, 1)

        @block.tensor
        def _(pe):
            for half in range(NHALF):
                norm.pe_turn(pe, half)
            for half in range(NHALF):
                pe.wait_ge(norm.h_ready, KC * (half + 1))
                cols = slice(half * HALF, (half + 1) * HALF)
                for f in range(FC):
                    j = half * FC + f
                    fs = slice(f * P, (f + 1) * P)
                    pe.wait_ge(w_lo_done, f + 1)
                    wait(pe, acted, j - 3)
                    split_product(pe, env.bank[j % 4][:, :],
                                  [(w1_hi[:, c, fs], w1_lo[:, c, fs]) for c in range(KC)],
                                  [(env.h_hi[:, c, cols], env.h_lo[:, c, cols]) for c in range(KC)], True, True)\
                        .then_inc(up, 1)
            pe.wait_ge(w_lo_done, 2 * FC)
            for b in range(B):
                half, k = divmod(b, 4)
                pe.wait_ge(lo_done, FC * (half + 1))
                wait(pe, added, b - 3)
                cols = slice(k * S, (k + 1) * S)
                split_product(pe, env.bank[4 + b % 4][:, 0:D],
                              [(act_hi[:, half, f, cols], act_lo[:, half, f, cols]) for f in range(FC)],
                              [(w2_hi[:, f, :], w2_lo[:, f, :]) for f in range(FC)], True, True)\
                    .then_inc(out_up, 1)

        @block.scalar
        def _(act):
            for half in range(NHALF):
                norm.act_evacuate(act, half)
            for j in range(NJ):
                f = j % FC
                act.wait_ge(up, j + 1)
                wait(act, lo_done, j - 1)
                act.activation(act_full[:, j % 2, :], env.bank[j % 4][:, :], func, bias=b1[:, f:f + 1])\
                    .then_inc(acted, 1)

        @block.vector
        def _(dve):
            norm.dve_all(dve)
            dve.tensor_tensor(env.x[:, :, :], env.x[:, :, :],
                              b2[:, :].unsqueeze(1).to_broadcast([P, B, D]), ALU.add).then_inc(b2_added, 1)
            for j in range(NJ):
                half, f = divmod(j, FC)
                dve.wait_ge(acted, j + 1)
                dve.tensor_copy(act_hi[:, half, f, :], act_full[:, j % 2, :]).then_inc(hi_done, 1)
                dve.wait_ge(hi_done, j + 1)
                dve.tensor_tensor(act_lo[:, half, f, :], act_full[:, j % 2, :],
                                  f32_view(act_hi[:, half, f, :]), ALU.subtract).then_inc(lo_done, 1)
            dve.wait_ge(b2_added, 1)
            for b in range(B):
                dve.wait_ge(out_up, b + 1)
                dve.tensor_tensor(env.x[:, b, :], env.bank[4 + b % 4][:, 0:D], env.x[:, b, :], ALU.add)\
                    .then_inc(added, 1)

        @block.sync
        def _(sp):
            if load_next:
                load_next(sp)
            if out is not None:
                for b in range(B):
                    sp.wait_ge(added, b + 1)
                    sp.dma_start(out[b], env.x[:, b, :]).then_inc(stored, 16)
                sp.wait_ge(stored, 16 * B)


def build(nc, a, out, until=99):
    ctx = ExitStack()
    with ctx:
        env = make_env(nc, ctx)
        sb = env.scoped(ctx)
        env.x = sb("x", [P, B, D])
        env.ident = sb("ident", [P, P])
        env.nhalf = sb("nhalf", [P, B])
        at, used = place_rows()
        env.cols = [sb(f"cols{t}", [P, n]) for t, n in enumerate(used)]

        def col(name, first=0, n=None):
            t, r, rows = at[name]
            return env.cols[t][:, r + first:r + first + (rows if n is None else n)]

        env.col = col
        env.free = {name: sb("free_" + name, [P, D]) for name in FREE_VECTORS}
        env.ctx_hi, env.ctx_lo = sb("ctx_hi", [P, KC, TOK], F32R), sb("ctx_lo", [P, KC, TOK], F32R)
        env.h_hi, env.h_lo = sb("h_hi", [P, KC, TOK], F32R), sb("h_lo", [P, KC, TOK], F32R)
        env.bn_scale, env.bn_shift = sb("bn_scale", [P, 1]), sb("bn_shift", [P, B])
        env.head_mask8, env.head_mask16 = sb("head_mask8", [P, 16]), sb("head_mask16", [P, 8])
        env.x_in, env.w0_in, env.mask_in = (env.lasting_sem(n) for n in ("x_in", "w0_in", "mask_in"))
        env.free_in, env.ff2_in, env.l3_in = (env.lasting_sem(n) for n in ("free_in", "ff2_in", "l3_in"))
        env.masks_made = env.lasting_sem("masks_made")
        with ExitStack() as late:
            lsb = env.scoped(late)

            def weights(shapes):
                return {name: lsb(name, [P, k, n]) for name, k, n in shapes}

            L = env.w_ff2 = weights((("L2_xattn_w_fc1", 2, 1024), ("L2_xattn_w_fc2", 8, 256)))

            with ExitStack() as l0:
                zsb = env.scoped(l0)
                env.w_q0, env.w_o0 = zsb("w_q0", [P, KC, D]), zsb("w_o0", [P, KC, D])
                env.w_k0, env.w_v0 = zsb("w_k0", [P, KC, 64]), zsb("w_v0", [P, KC, 64])
                env.mask0 = zsb("mask0", [P, B, S])
                env.qT1 = zsb("qT1", [P, B, P + 1])
                setup(env, a)
                layer0(env)
                if until >= 1:
                    non_local(env)
            for k, (ln_scale, ln_offset) in enumerate((("ln1_scale", "ln1_offset"), ("ln2_scale", "ln2_offset"))):
                if until >= 2 + k:
                    n = str(k + 1)
                    L2 = "L2_xattn_"
                    long_head_attention(env, "la" + n, a, env.col(L2 + ln_scale), env.col(L2 + ln_offset), L2 + "wq" + n, L2 + "wk" + n, L2 + "wv" + n, L2 + "wo" + n,
                                        env.col(L2 + "bq" + n), env.col(L2 + "bk" + n), env.col(L2 + "bv" + n),
                                        env.col(L2 + "bias_k" + n), env.col(L2 + "bias_v" + n),
                                        env.free[L2 + "bo" + n])
                    free_semaphores(env)
            L3 = weights((("L3_xattn_w_qkv", 2, 768), ("L3_xattn_w_ao", 2, 256),
                          ("L3_xattn_w_q", 2, 256), ("L3_xattn_w_kv", 2, 512),
                          ("L3_xattn_w_co", 2, 256), ("L3_xattn_w1", 2, 1024), ("L3_xattn_w2", 8, 256)))
            env.mask_self, env.mask_cross = lsb("mask_self", [P, 1, S]), lsb("mask_cross", [P, B, S])

            def load_layer3(sp):
                load_weights(env, sp, a, L3, env.l3_in)
                sp.dma_start(env.mask_self[:, 0, :], a["mask_1x1xSxS2_fc1"][0, 0]).then_inc(env.l3_in, 16)
                sp.dma_start(env.mask_cross[:, :, :], a["mask_Bx1xSxS2_ff1"].rearrange("b o q s -> q (b o) s"))\
                    .then_inc(env.l3_in, 16)

            if until >= 4:
                feed_forward(env, "ff2", env.col("L2_xattn_ln_mlp_scale"), env.col("L2_xattn_ln_mlp_offset"),
                             L["L2_xattn_w_fc1"], L["L2_xattn_w_fc2"], env.col("L2_xattn_b_fc1"),
                             env.free["L2_xattn_b_fc2"], ACT.Gelu, w_in=(env.ff2_in, 32),
                             load_next=load_layer3)
            if until >= 5:
                layer3_attention(env, "sa", "ln1", L3["L3_xattn_w_qkv"], None, "b_qkv", None,
                                 env.free["L3_xattn_b_ao"], L3["L3_xattn_w_ao"], env.mask_self, False)
            if until >= 6:
                layer3_attention(env, "ca", "ln2", L3["L3_xattn_w_q"], L3["L3_xattn_w_kv"], "b_q", "b_kv",
                                 env.free["L3_xattn_b_co"], L3["L3_xattn_w_co"], env.mask_cross, True)
            if until >= 7:
                feed_forward(env, "ff3", env.col("L3_xattn_ln3_s"), env.col("L3_xattn_ln3_b"),
                             L3["L3_xattn_w1"], L3["L3_xattn_w2"], env.col("L3_xattn_b1"),
                             env.free["L3_xattn_b2"], ACT.Gelu_apprx_tanh, out=out)
            else:
                dump(env, out)


def wait(engine, sem, value):
    if not isinstance(value, int) or value > 0:
        engine.wait_ge(sem, value)


def dump(env, out):
    stored = env.sem("stored")
    with env.nc.Block() as block:
        @block.sync
        def _(sp):
            sp.dma_start(out.rearrange("b s d -> s b d"), env.x[:, :, :]).then_inc(stored, 16)
            sp.wait_ge(stored, 16)


def layer0(env):
    with ExitStack() as stack:
        sb = env.scoped(stack)
        q_all, k_all = sb("q_all0", [P, KC, TOK]), sb("k_all0", [P, KC, TOK])
        v_all = sb("v_all0", [P, B, KV_HEADS, HD0 + 1])
        with ExitStack() as parts:
            psb = env.scoped(parts)

            def parts_of(raw, name, n, by_pool):
                hi, lo = psb(name + "_hi", [P, KC, n], F32R), psb(name + "_lo", [P, KC, n], F32R)
                return Weights(raw, hi[:, :, :], lo[:, :, :], by_pool)

            wk_rep = psb("wk0_rep", [P, KC, 8, GROUP, HD0])
            wq = parts_of(env.w_q0[:, :, :], "wq0", D, False)
            wk = parts_of(wk_rep[:, :, :, :, :].rearrange("p c g j d -> p c (g j d)"), "wk0", D, True)
            wv = parts_of(env.w_v0[:, :, :], "wv0", 64, False)
            spread = env.sem("wk0_spread")

            def repeat_keys(pool):
                for c in range(KC):
                    pool.tensor_copy(wk_rep[:, c, :, :, :],
                                     env.w_k0[:, c, :].rearrange("p (g d) -> p g d", d=HD0).unsqueeze(2)
                                     .to_broadcast([P, 8, GROUP, HD0])).then_inc(spread, 1)
                pool.wait_ge(spread, KC)

            project(env, psb, "p0", None, None, None, [wv, wq, wk],
                    token_products(wv, env.ctx_hi, env.ctx_lo, v_all, KV_HEADS, HD0)
                    + feature_products(wk, env.ctx_hi, env.ctx_lo, k_all, env.col("bk_of_heads")),
                    feature_products(wq, env.h_hi, env.h_lo, q_all, env.col("L0_xattn_bq")),
                    env.free["L0_xattn_bo"], waits_act=[(env.w0_in, 64)],
                    waits_pool=[(env.w0_in, 64), (env.free_in, 16 * len(FREE_VECTORS))],
                    pool_first=repeat_keys, ones=v_all[:, :, :, HD0:HD0 + 1])
        short_head_attention(env, "a0", 32, HD0, KV_HEADS, float(HD0) ** -0.5, env.mask0, True, False,
                             env.head_mask8, q_all, k_all, v_all, env.w_o0, env.col("bv_of_heads"))
        norm_token_major(env, "n0", 1e-6, env.free["L0_xattn_gamma"], env.free["L0_xattn_beta"])


def layer3_attention(env, name, ln, w_q, w_kv, b_q, b_kv, b_out, w_out, mask, per_sequence):
    heads, hd = 16, 16
    L3 = "L3_xattn_"
    with ExitStack() as stack:
        sb = env.scoped(stack)
        q_all, k_all = sb(name + "_q", [P, KC, TOK]), sb(name + "_k", [P, KC, TOK])
        v_all = sb(name + "_v", [P, B, heads, hd + 1])
        with ExitStack() as parts:
            psb = env.scoped(parts)

            def parts_of(raw, first, part, by_pool):
                hi = psb(f"{name}_w{part}_hi", [P, KC, D], F32R)
                lo = psb(f"{name}_w{part}_lo", [P, KC, D], F32R)
                return Weights(raw[:, :, first * D:(first + 1) * D], hi[:, :, :], lo[:, :, :], by_pool)

            if w_kv is None:
                wq, wk, wv = parts_of(w_q, 0, "q", False), parts_of(w_q, 1, "k", True), parts_of(w_q, 2, "v", False)
                src = (env.h_hi, env.h_lo)
                bq, bk, bv = (env.col(L3 + b_q, 2 * k, 2) for k in range(3))
            else:
                wq, wk, wv = parts_of(w_q, 0, "q", False), parts_of(w_kv, 0, "k", False), parts_of(w_kv, 1, "v", True)
                src = (env.ctx_hi, env.ctx_lo)
                bq = env.col(L3 + b_q)
                bk, bv = (env.col(L3 + b_kv, 2 * k, 2) for k in range(2))
            kv = feature_products(wk, *src, k_all, bk) + token_products(wv, *src, v_all, heads, hd)
            q = feature_products(wq, env.h_hi, env.h_lo, q_all, bq)
            own = w_kv is None
            project(env, psb, name + "_p", env.col(L3 + ln + "_s"), env.col(L3 + ln + "_b"), 1e-5,
                    [wk, wv, wq], [] if own else kv, sorted(kv + q, key=lambda job: job.half) if own else q,
                    b_out, waits_act=[(env.l3_in, 16 * 9)], waits_pool=[(env.l3_in, 16 * 9)],
                    ones=v_all[:, :, :, hd:hd + 1])
        short_head_attention(env, name, heads, hd, heads, float(hd) ** -0.5, mask, per_sequence, True,
                             env.head_mask16, q_all, k_all, v_all, w_out, bv)


_OUT = (B, S, D)


def kernel(**inputs):
    import numpy as _np
    import concourse.bacc as _bacc
    from concourse import mybir as _mybir
    from concourse.bass_utils import run_bass_kernel_spmd as _run

    nc = _bacc.Bacc("TRN2", target_bir_lowering=False, num_devices=1)
    arrays, args = {}, {}
    for name, value in inputs.items():
        value = _np.ascontiguousarray(value)
        arrays[f"in_{name}"] = value
        args[name] = nc.dram_tensor(f"in_{name}", value.shape, _mybir.dt.from_np(value.dtype),
                                    kind="ExternalInput").ap()
    out = nc.dram_tensor("out_0", _OUT, F32, kind="ExternalOutput").ap()
    build(nc, args, out)
    r = _run(nc, [arrays], core_ids=[0])
    return r.results[0]["out_0"]
```

```python
from contextlib import ExitStack

import concourse.bass as bass
from concourse import mybir

F32 = mybir.dt.float32
F32R = mybir.dt.float32r
ALU = mybir.AluOpType
ACT = mybir.ActivationFunctionType
X = mybir.AxisListType.X

P = 128
B = 8
S = 128
D = 256
KC = D // P
TOK = B * S
HALF = 512
NHALF = TOK // HALF


class Env:

    def __init__(self, nc):
        self.nc = nc


class Product:

    def __init__(self, lhs, rhs, n, out, bias, weights, half, normed):
        self.lhs, self.rhs, self.n, self.out, self.bias = lhs, rhs, n, out, bias
        self.weights, self.half, self.normed = weights, half, normed


def make_env(nc, ctx):
    env = Env(nc)

    def scoped(stack):
        def sb(name, shape, dt=F32):
            return stack.enter_context(nc.sbuf_tensor(name, shape, dt))
        return sb

    env.scoped = scoped
    env.lasting_sem = lambda name: ctx.enter_context(nc.semaphore(name))
    env.stage_sems = []

    def sem(name):
        env.stage_sems.append(nc.alloc_semaphore(name=name))
        return env.stage_sems[-1]

    env.sem = sem
    env.bank = [ctx.enter_context(nc.psum_tensor(f"bank{i}", [P, 512], F32)) for i in range(8)]
    return env


def free_semaphores(env):
    env.nc.clear_and_free_semaphores(env.stage_sems)
    env.nc.all_engine_barrier()
    env.stage_sems = []


def f32_view(ap):
    return ap.bitcast(F32)


def split_product(pe, out, lhs, rhs, start, stop):
    n = len(lhs)
    for k in range(n):
        (lh, ll), (rh, rl) = lhs[k], rhs[k]
        pe.matmul(out, ll, rh, start=start and k == 0, stop=False)
        pe.matmul(out, lh, rl, start=False, stop=False)
        mm = pe.matmul(out, lh, rh, start=False, stop=stop and k == n - 1)
    return mm


def load_weights(env, sp, a, weights, sem):
    for name, dst in weights.items():
        k = a[name].shape[0] // P
        sp.dma_start(dst[:, :, :], a[name].rearrange("(c p) n -> p c n", c=k)).then_inc(sem, 16)


ROW_TILES = [[
    ("L0_xattn_bq", 2), ("bk_of_heads", 2), ("bv_of_heads", 2), ("L1_xattn_w_b", 1),
    ("L1_xattn_bn_gamma", 1), ("L1_xattn_bn_beta", 1), ("L1_xattn_bn_mean", 1), ("L1_xattn_bn_var", 1),
], [
    ("L2_xattn_ln1_scale", 2), ("L2_xattn_ln1_offset", 2),
    ("L2_xattn_bq1", 16), ("L2_xattn_bk1", 16), ("L2_xattn_bv1", 16),
    ("L2_xattn_bias_k1", 16), ("L2_xattn_bias_v1", 16),
    ("L3_xattn_ln1_s", 2), ("L3_xattn_ln1_b", 2), ("L3_xattn_b_qkv", 6),
    ("L3_xattn_ln2_s", 2), ("L3_xattn_ln2_b", 2), ("L3_xattn_b_q", 2), ("L3_xattn_b_kv", 4),
    ("L3_xattn_ln3_s", 2), ("L3_xattn_ln3_b", 2),
], [
    ("L2_xattn_ln2_scale", 2), ("L2_xattn_ln2_offset", 2),
    ("L2_xattn_bq2", 16), ("L2_xattn_bk2", 16), ("L2_xattn_bv2", 16),
    ("L2_xattn_bias_k2", 16), ("L2_xattn_bias_v2", 16),
    ("L2_xattn_ln_mlp_scale", 2), ("L2_xattn_ln_mlp_offset", 2), ("L2_xattn_b_fc1", 8),
    ("L3_xattn_b1", 8),
]]
FREE_VECTORS = ["L0_xattn_bo", "L0_xattn_gamma", "L0_xattn_beta", "L2_xattn_bo1", "L2_xattn_bo2",
                "L2_xattn_b_fc2", "L3_xattn_b_ao", "L3_xattn_b_co", "L3_xattn_b2"]
KV_HEADS, GROUP, HD0 = 8, 4, 8


def place_rows():
    at, used = {}, []
    for tile, vectors in enumerate(ROW_TILES):
        row = 0
        for name, n in vectors:
            at[name] = (tile, row, n)
            row += n
        used.append(row)
    return at, used


def flat(ap):
    if len(ap.shape) == 4:
        return ap.rearrange("a b c d -> (a b c d)")
    return ap


def load_rows(env, sp, a, rows, at, name, sem):
    t, r, n = at[name]
    if name not in ("bk_of_heads", "bv_of_heads"):
        sp.dma_start(rows[t][r:r + n, :], flat(a[name]).rearrange("(r p) -> r p", p=P)).then_inc(sem, 16)
        return 16
    src = a["L0_xattn_bk" if name == "bk_of_heads" else "L0_xattn_bv"]
    for c in range(n):
        dst = rows[t][r + c:r + c + 1, :].rearrange("c (g j d) -> c g j d", j=GROUP, d=HD0)
        sp.dma_start(dst, src.rearrange("(c g d) -> c g d", g=4, d=HD0)[c:c + 1].unsqueeze(2)
                     .to_broadcast([1, 4, GROUP, HD0])).then_inc(sem, 16)
    return 16 * n


def setup(env, a, before):
    nc = env.nc
    N1 = D
    CI = 64
    with ExitStack() as stack:
        sb = env.scoped(stack)
        at, used = place_rows()
        rows = env.rows
        ctx_tok = sb("ctx_tok", [P, B, D])
        ctx_f = sb("ctx_f", [P, KC, TOK])
        pg_w = sb("pg_w", [P, P])
        w_w = sb("w_w", [P, CI])
        theta_w = sb("theta_w", [CI, P])
        theta_b = sb("theta_b", [CI, 2])
        pg_bias = sb("pg_bias", [P, P])
        pg_wT = sb("pg_wT", [P, P])
        w_wT = sb("w_wT", [CI, P])
        pg = sb("pg", [P, B, KC, P])
        mT = sb("mT", [CI, B, CI])
        pT = sb("pT", [CI, B, P])
        nhalf1 = sb("nhalf1", [P, 1])
        inv = sb("inv", [P, 2])

        rows_in = env.sem("rows_in")
        ctx_in = env.sem("ctx_in")
        nl_w_in = env.sem("nl_w_in")
        nl_in = env.sem("nl_in")
        pool_init = env.sem("pool_init")
        cols_up = env.sem("cols_up")
        cols_down = env.sem("cols_down")
        ctx_up = env.sem("ctx_up")
        ctx_down = env.sem("ctx_down")
        ctx_split = env.sem("ctx_split")
        nl_wt_up = env.sem("nl_wt_up")
        nl_wt_down = env.sem("nl_wt_down")
        pg_up, pg_down = env.sem("pg_up"), env.sem("pg_down")
        mt_up, mt_down = env.sem("mt_up"), env.sem("mt_down")
        pt_up, pt_down = env.sem("pt_up"), env.sem("pt_down")
        qt_up, qt_down = env.sem("qt_up"), env.sem("qt_down")
        bn = env.sem("bn")
        bn_pow = env.sem("bn_pow")
        block = stack.enter_context(nc.Block())

        @block.sync
        def _(sp):
            for k, name in enumerate(("phi_b", "g_b")):
                sp.dma_start(pg_bias[:, k * CI:(k + 1) * CI],
                             a["L1_xattn_" + name].rearrange("(a n) -> a n", a=1).to_broadcast([P, CI]))\
                    .then_inc(nl_in, 16)
            sp.dma_start(theta_w[:, :], a["L1_xattn_theta_w"]).then_inc(nl_in, 16)
            with nc.allow_non_contiguous_dma(reason="64 values, one to a partition"):
                sp.dma_start(theta_b[:, 0:1], a["L1_xattn_theta_b"].rearrange("(c a) -> c a", a=1))\
                    .then_inc(nl_in, 16)
            env.rows_count = sum(load_rows(env, sp, a, rows, at, name, rows_in) for name, n in ROW_TILES[0])
            for name, dst in (("Wk", env.w_k0), ("Wv", env.w_v0), ("Wq", env.w_q0), ("Wo", env.w_o0)):
                sp.dma_start(dst[:, :, :], a["L0_xattn_" + name].rearrange("(c p) n -> p c n", p=P))\
                    .then_inc(env.w0_in, 16)
            sp.dma_start(env.x[:, :, :], a["x"].rearrange("b s d -> s b d")).then_inc(env.x_in, 16)

        @block.gpsimd
        def _(pool):
            pool.memset(env.ident[:, :], 0.0).then_inc(pool_init, 1)
            pool.wait_ge(pool_init, 1)
            pool.affine_select(out=env.ident[:, :], in_=env.ident[:, :], compare_op=ALU.not_equal,
                               fill=1.0, base=0, pattern=[[-1, P]], channel_multiplier=1)\
                .then_inc(pool_init, 1)
            pool.memset(env.nhalf[:, :], -0.5).then_inc(pool_init, 1)
            pool.memset(nhalf1[:, :], -0.5).then_inc(pool_init, 1)
            for mask, hd in ((env.head_mask8, 8), (env.head_mask16, 16)):
                n = P // hd
                pool.memset(mask[:, :], 1.0).then_inc(env.masks_made, 1)
            for k, (mask, hd) in enumerate(((env.head_mask8, 8), (env.head_mask16, 16))):
                n = P // hd
                pool.wait_ge(env.masks_made, 2 + 2 * k)
                pool.affine_select(out=mask[:, :], in_=mask[:, :], compare_op=ALU.is_ge, fill=0.0,
                                   base=0, pattern=[[-hd, n]], channel_multiplier=1)\
                    .then_inc(env.masks_made, 1)
                pool.wait_ge(env.masks_made, 3 + 2 * k)
                pool.affine_select(out=mask[:, :], in_=mask[:, :], compare_op=ALU.is_ge, fill=0.0,
                                   base=hd - 1, pattern=[[hd, n]], channel_multiplier=-1)\
                    .then_inc(env.masks_made, 1)
            before.pool_parts(pool)
            pool.wait_ge(bn, 1)
            pool.tensor_tensor(inv[:, 1:2], inv[:, 0:1], nhalf1[:, :], ALU.pow).then_inc(bn_pow, 1)

        @block.tensor
        def _(pe):
            pe.wait_ge(pool_init, 2)
            pe.wait_ge(ctx_in, 16)
            for c in range(KC):
                for half in range(NHALF):
                    n = c * NHALF + half
                    for k in range(4):
                        b = half * 4 + k
                        mm = pe.transpose(env.bank[2 + n][:, k * P:(k + 1) * P],
                                          ctx_tok[:, b, c * P:(c + 1) * P], env.ident[:, :])
                    mm.then_inc(ctx_up, 1)
            pe.wait_ge(nl_w_in, 16 * 3)
            pe.transpose(env.bank[1][:, 0:P], pg_w[:, :], env.ident[:, :])
            pe.transpose(env.bank[1][0:CI, P:2 * P], w_w[:, :], env.ident[:, :]).then_inc(nl_wt_up, 1)
            pe.wait_ge(nl_wt_down, 1)
            for b in range(B):
                wait(pe, pg_down, b - 1)
                for c in range(KC):
                    mm = pe.matmul(env.bank[b % 2][:, c * P:(c + 1) * P], ctx_tok[:, b, c * P:(c + 1) * P],
                                   pg_wT[:, :], start=True, stop=True)
                mm.then_inc(pg_up, 1)
            for half in range(NHALF):
                pe.wait_ge(pg_down, 4 * half + 4)
                for k in range(4):
                    b = half * 4 + k
                    for c in range(KC):
                        mm = pe.matmul(env.bank[6 + half][0:CI, k * CI:(k + 1) * CI], pg[:, b, c, CI:P],
                                       pg[:, b, c, 0:CI], start=c == 0, stop=c == KC - 1)
                mm.then_inc(mt_up, 1)
            pe.wait_ge(rows_in, env.rows_count)
            pe.transpose(env.bank[0][:, 0:used[0]], rows[0][0:used[0], :], env.ident[0:used[0], 0:used[0]])\
                .then_inc(cols_up, 1)
            pe.wait_ge(ctx_down, NHALF * KC)
            for half in range(NHALF):
                pe.wait_ge(mt_down, half + 1)
                for k in range(4):
                    mm = pe.matmul(env.bank[2 + half][0:CI, k * P:(k + 1) * P], mT[:, half * 4 + k, :], w_wT[:, :],
                                   start=True, stop=True)
                mm.then_inc(pt_up, 1)
            for pair in range(B // 2):
                if pair == 0:
                    pe.wait_ge(nl_in, 16 * 4)
                pe.wait_ge(pt_down, pair // 2 + 1)
                wait(pe, qt_down, pair - 1)
                for k in range(2):
                    out = env.bank[4 + pair % 2][:, k * (P + 1):(k + 1) * (P + 1)]
                    b = 2 * pair + k
                    pe.matmul(out[:, 0:P], theta_w[:, :], pT[:, b, :], start=True, stop=True)
                    mm = pe.matmul(out[:, P:P + 1], pT[:, b, :], theta_b[:, 0:1], start=True, stop=True)
                mm.then_inc(qt_up, 1)

        @block.scalar
        def _(act):
            act.dma_start(ctx_tok[:, :, :], a["ctx_2048"].rearrange("b s d -> s b d")).then_inc(ctx_in, 16)
            act.dma_start(pg_w[0:CI, :], a["L1_xattn_phi_w"]).then_inc(nl_w_in, 16)
            act.dma_start(pg_w[CI:P, :], a["L1_xattn_g_w"]).then_inc(nl_w_in, 16)
            act.dma_start(w_w[:, :], a["L1_xattn_w_w"]).then_inc(nl_w_in, 16)
            for n in range(KC * NHALF):
                c, half = divmod(n, NHALF)
                act.wait_ge(ctx_up, n + 1)
                act.activation(ctx_f[:, c, half * HALF:(half + 1) * HALF], env.bank[2 + n][:, :], ACT.Copy)\
                    .then_inc(ctx_down, 1)
            act.wait_ge(nl_wt_up, 1)
            act.activation(pg_wT[:, :], env.bank[1][:, 0:P], ACT.Copy)
            act.activation(w_wT[:, :], env.bank[1][0:CI, P:2 * P], ACT.Copy).then_inc(nl_wt_down, 1)
            before.act_parts(act)
            for half in range(NHALF):
                act.wait_ge(mt_up, half + 1)
                act.activation(mT[:, half * 4:half * 4 + 4, :],
                               env.bank[6 + half][0:CI, 0:4 * CI].rearrange("p (b n) -> p b n", n=CI), ACT.Copy)\
                    .then_inc(mt_down, 1)
            for half in range(NHALF):
                act.wait_ge(pt_up, half + 1)
                act.activation(pT[:, half * 4:half * 4 + 4, :],
                               env.bank[2 + half][0:CI, :].rearrange("p (b n) -> p b n", n=P), ACT.Copy,
                               scale=1.0 / N1).then_inc(pt_down, 1)
            for pair in range(B // 2):
                act.wait_ge(qt_up, pair + 1)
                act.activation(env.qT1[:, 2 * pair:2 * pair + 2, :],
                               env.bank[4 + pair % 2][:, 0:2 * (P + 1)].rearrange("p (b n) -> p b n", n=P + 1),
                               ACT.Copy).then_inc(qt_down, 1)

        @block.vector
        def _(dve):
            dve.wait_ge(nl_in, 16 * 4)
            for b in range(B):
                dve.wait_ge(pg_up, b + 1)
                dve.tensor_tensor(pg[:, b, :, :],
                                  env.bank[b % 2][:, 0:KC * P].rearrange("p (c n) -> p c n", n=P),
                                  pg_bias[:, :].unsqueeze(1).to_broadcast([P, KC, P]), ALU.add)\
                    .then_inc(pg_down, 1)
            before.dve_parts(dve)
            dve.wait_ge(cols_up, 1)
            dve.tensor_copy(env.cols[0][:, 0:used[0]], env.bank[0][:, 0:used[0]]).then_inc(cols_down, 1)
            dve.wait_ge(cols_down, 1)
            dve.tensor_scalar(inv[:, 0:1], env.col("L1_xattn_bn_var"), 1e-5, None, ALU.add).then_inc(bn, 1)
            for n in range(KC * NHALF):
                c, half = divmod(n, NHALF)
                dve.wait_ge(ctx_down, n + 1)
                part = (slice(None), c, slice(half * HALF, (half + 1) * HALF))
                dve.tensor_copy(env.ctx_hi[part], ctx_f[part]).then_inc(ctx_split, 1)
                dve.wait_ge(ctx_split, n + 1)
                dve.tensor_tensor(env.ctx_lo[part], ctx_f[part], f32_view(env.ctx_hi[part]), ALU.subtract)
            dve.wait_ge(bn_pow, 1)
            dve.tensor_tensor(env.bn_scale[:, :], env.col("L1_xattn_bn_gamma"), inv[:, 1:2], ALU.mult)\
                .then_inc(bn, 1)
            dve.tensor_tensor(inv[:, 0:1], env.col("L1_xattn_w_b"), env.col("L1_xattn_bn_mean"), ALU.subtract)\
                .then_inc(bn, 1)
            dve.wait_ge(qt_down, B // 2)
            dve.wait_ge(bn, 3)
            dve.tensor_scalar(env.bn_shift[:, :], env.qT1[:, :, P], inv[:, 0:1], env.bn_scale[:, 0:1],
                              ALU.add, ALU.mult).then_inc(bn, 1)
            dve.wait_ge(bn, 4)
            dve.tensor_scalar(env.bn_shift[:, :], env.bn_shift[:, :], env.col("L1_xattn_bn_beta"), None,
                              ALU.add).then_inc(bn, 1)


class Norm:

    def __init__(self, env, sb, name, gamma, beta, eps, banks, like=None, halves=(0, 1)):
        self.env, self.gamma, self.beta, self.eps, self.banks = env, gamma, beta, eps, banks
        self.halves = halves
        self.stats, self.mv, self.ve, self.rstd = env.norm_stats
        if like:
            self.xn, self.full = like.xn, like.full
        else:
            self.xn = sb(name + "_xn", [P, B, D]) if eps else env.x
            self.full = sb(name + "_full", [P, KC, TOK])
        self.stats_done = env.sem(name + "_stats_done")
        self.aggregated = env.sem(name + "_aggregated")
        self.rstd_done = env.sem(name + "_rstd_done")
        self.normed = env.sem(name + "_normed")
        self.turned = env.sem(name + "_turned")
        self.evacuated = env.sem(name + "_evacuated")
        self.hi_done = env.sem(name + "_hi_done")
        self.h_ready = env.sem(name + "_h_ready")

    def dve_stats(self, dve, half):
        x = self.env.x
        own = range(half * 4, half * 4 + 4)
        for b in own:
            dve.bn_stats(self.stats[:, b, :], x[:, b, :]).then_inc(self.stats_done, 1)
        turn = self.halves.index(half)
        for k, b in enumerate(own):
            dve.wait_ge(self.stats_done, 4 * turn + k + 1)
            ins = dve.bn_aggr(self.mv[:, b, :], self.stats[:, b, :])
        ins.then_inc(self.aggregated, 1)
        dve.wait_ge(self.aggregated, 2 * turn + 1)
        dve.tensor_scalar(self.ve[:, half * 4:half * 4 + 4], self.mv[:, half * 4:half * 4 + 4, 1], self.eps,
                          None, ALU.add).then_inc(self.aggregated, 1)

    def pool_rstd(self, pool, half):
        own = slice(half * 4, half * 4 + 4)
        pool.wait_ge(self.aggregated, 2 * self.halves.index(half) + 2)
        pool.tensor_tensor(self.rstd[:, own], self.ve[:, own], self.env.nhalf[:, own], ALU.pow)\
            .then_inc(self.rstd_done, 1)

    def dve_normalise(self, dve, half):
        dve.wait_ge(self.rstd_done, self.halves.index(half) + 1)
        for b in range(half * 4, half * 4 + 4):
            dve.tensor_scalar(self.xn[:, b, :], self.env.x[:, b, :], self.mv[:, b, 0:1],
                              self.rstd[:, b:b + 1], ALU.subtract, ALU.mult).then_inc(self.normed, 1)

    def pe_turn(self, pe, half):
        turn = self.halves.index(half)
        for c in range(KC):
            wait(pe, self.evacuated, KC * (turn - 1) + c + 1)
            for k in range(4):
                b = half * 4 + k
                if self.eps and c == 0:
                    pe.wait_ge(self.normed, 4 * turn + k + 1)
                mm = pe.transpose(self.banks[c][:, k * P:(k + 1) * P], self.xn[:, b, c * P:(c + 1) * P],
                                  self.env.ident[:, :])
            mm.then_inc(self.turned, 1)

    def act_evacuate(self, act, half):
        for c in range(KC):
            out = self.full[:, c, half * HALF:(half + 1) * HALF]
            act.wait_ge(self.turned, KC * self.halves.index(half) + c + 1)
            if self.eps:
                ins = act.activation(out, self.banks[c][:, :], ACT.Identity, scale=self.gamma[:, c:c + 1],
                                     bias=self.beta[:, c:c + 1])
            else:
                ins = act.activation(out, self.banks[c][:, :], ACT.Copy)
            ins.then_inc(self.evacuated, 1)

    def dve_split(self, dve, half):
        env = self.env
        for c in range(KC):
            n = KC * self.halves.index(half) + c
            part = (slice(None), c, slice(half * HALF, (half + 1) * HALF))
            dve.wait_ge(self.evacuated, n + 1)
            dve.tensor_copy(env.h_hi[part], self.full[part]).then_inc(self.hi_done, 1)
            dve.wait_ge(self.hi_done, n + 1)
            dve.tensor_tensor(env.h_lo[part], self.full[part], f32_view(env.h_hi[part]), ALU.subtract)\
                .then_inc(self.h_ready, 1)

    def pe_wait(self, pe, half):
        if half in self.halves:
            pe.wait_ge(self.h_ready, KC * (self.halves.index(half) + 1))

    def dve_all(self, dve, meanwhile=None):
        if self.eps:
            for half in self.halves:
                self.dve_stats(dve, half)
        if meanwhile:
            meanwhile()
        if self.eps:
            for half in self.halves:
                self.dve_normalise(dve, half)
        for half in self.halves:
            self.dve_split(dve, half)

    def pe_all(self, pe):
        for half in self.halves:
            self.pe_turn(pe, half)

    def act_all(self, act):
        for half in self.halves:
            self.act_evacuate(act, half)

    def pool_all(self, pool):
        if self.eps:
            for half in self.halves:
                self.pool_rstd(pool, half)


class TokenNorm:

    def __init__(self, env, name, half, eps, gamma, beta):
        self.env, self.half, self.eps, self.gamma, self.beta = env, half, eps, gamma, beta
        self.own = slice(half * 4, half * 4 + 4)
        self.stats, self.mv, self.ve, self.rstd = env.norm_stats
        self.stats_done = env.sem(name + "_stats")
        self.rstd_done = env.sem(name + "_rstd")
        self.normed = env.sem(name + "_normed")
        self.done = env.sem(name + "_done")

    def dve_stats(self, dve):
        own = range(self.own.start, self.own.stop)
        for b in own:
            dve.bn_stats(self.stats[:, b, :], self.env.x[:, b, :]).then_inc(self.stats_done, 1)
        for k, b in enumerate(own):
            dve.wait_ge(self.stats_done, k + 1)
            ins = dve.bn_aggr(self.mv[:, b, :], self.stats[:, b, :])
        ins.then_inc(self.stats_done, 1)
        dve.wait_ge(self.stats_done, 5)
        dve.tensor_scalar(self.ve[:, self.own], self.mv[:, self.own, 1], self.eps, None, ALU.add)\
            .then_inc(self.stats_done, 1)

    def pool_rstd(self, pool):
        pool.wait_ge(self.stats_done, 6)
        pool.tensor_tensor(self.rstd[:, self.own], self.ve[:, self.own], self.env.nhalf[:, self.own], ALU.pow)\
            .then_inc(self.rstd_done, 1)

    def dve_normalise(self, dve):
        x = self.env.x
        dve.wait_ge(self.rstd_done, 1)
        for b in range(self.own.start, self.own.stop):
            dve.tensor_scalar(x[:, b, :], x[:, b, :], self.mv[:, b, 0:1], self.rstd[:, b:b + 1],
                              ALU.subtract, ALU.mult).then_inc(self.normed, 1)
        xh = x[:, self.own, :]
        dve.wait_ge(self.normed, 4)
        dve.tensor_tensor(xh, xh, self.gamma[:, :].unsqueeze(1).to_broadcast([P, 4, D]), ALU.mult)\
            .then_inc(self.normed, 1)
        dve.wait_ge(self.normed, 5)
        dve.tensor_tensor(xh, xh, self.beta[:, :].unsqueeze(1).to_broadcast([P, 4, D]), ALU.add)\
            .then_inc(self.done, 1)


class Weights:

    def __init__(self, raw, hi, lo, by_pool):
        self.raw, self.hi, self.lo, self.by_pool = raw, hi, lo, by_pool
        self.done = None


def feature_products(env, w, normed, out, bias):
    jobs = []
    a_hi, a_lo = (env.h_hi, env.h_lo) if normed else (env.ctx_hi, env.ctx_lo)
    for half in range(NHALF):
        for f in range(out.shape[1]):
            cols = slice(half * HALF, (half + 1) * HALF)
            jobs.append(Product(
                lhs=[(w.hi[:, c, f * P:(f + 1) * P], w.lo[:, c, f * P:(f + 1) * P]) for c in range(KC)],
                rhs=[(a_hi[:, c, cols], a_lo[:, c, cols]) for c in range(KC)],
                n=HALF, out=out[:, f, cols], bias=bias[:, f:f + 1], weights=w, half=half, normed=normed))
    return jobs


def token_products(env, w, normed, out, heads, hd):
    jobs = []
    a_hi, a_lo = (env.h_hi, env.h_lo) if normed else (env.ctx_hi, env.ctx_lo)
    for b in range(B):
        cols = slice(b * S, (b + 1) * S)
        jobs.append(Product(
            lhs=[(a_hi[:, c, cols], a_lo[:, c, cols]) for c in range(KC)],
            rhs=[(w.hi[:, c, :], w.lo[:, c, :]) for c in range(KC)],
            n=heads * hd, out=out[:, b, :, 0:hd], bias=None, weights=w, half=b // 4, normed=normed))
    return jobs


class Projection:

    STEPS = 4

    def __init__(self, env, name, norm, weights, early, jobs, deferred, ready_half, add_bias,
                 waits_act=(), waits_pool=(), pool_first=None, ones=None):
        self.env, self.norm, self.early, self.jobs = env, norm, early, jobs
        self.deferred, self.ready_half = deferred, ready_half
        self.main = len(early) + len(jobs)
        self.total = self.main + len(deferred)
        self.add_bias, self.waits_act, self.waits_pool = add_bias, waits_act, waits_pool
        self.pool_first, self.ones = pool_first, ones
        self.NB = 6
        self.hi_act = env.sem(name + "_hi_act")
        self.lo_dve = env.sem(name + "_lo_dve")
        self.hi_pool, self.lo_pool = env.sem(name + "_hi_pool"), env.sem(name + "_lo_pool")
        self.ones_made = env.sem(name + "_ones_made")
        self.bias_added = env.sem(name + "_bias_added")
        self.up, self.down = env.sem(name + "_up"), env.sem(name + "_down")
        self.pooled = [w for w in weights if w.by_pool]
        self.others = [w for w in weights if not w.by_pool]
        for i, w in enumerate(self.pooled):
            w.done = (self.lo_pool, i + 1)
        for i, w in enumerate(self.others):
            w.done = (self.lo_dve, i + 1)

    def pool_parts(self, pool):
        for sem, value in self.waits_pool:
            pool.wait_ge(sem, value)
        if self.pool_first:
            self.pool_first(pool)
        for i, w in enumerate(self.pooled):
            pool.tensor_copy(w.hi, w.raw).then_inc(self.hi_pool, 1)
            pool.wait_ge(self.hi_pool, i + 1)
            pool.tensor_tensor(w.lo, w.raw, f32_view(w.hi), ALU.subtract).then_inc(self.lo_pool, 1)
        self.norm.pool_all(pool)
        pool.memset(self.ones, 1.0).then_inc(self.ones_made, 1)

    def pool_bias(self, pool):
        env = self.env
        pool.wait_ge(env.free_in, 16 * len(FREE_VECTORS))
        pool.wait_ge(self.norm.evacuated, KC * len(self.norm.halves))
        pool.tensor_tensor(env.x[:, :, :], env.x[:, :, :],
                           self.add_bias[:, :].unsqueeze(1).to_broadcast([P, B, D]), ALU.add)\
            .then_inc(self.bias_added, 1)

    def pe_all(self, pe):
        env, NB = self.env, self.NB

        def run(batch, start):
            for i, job in enumerate(batch, start):
                pe.wait_ge(*job.weights.done)
                wait(pe, self.down, i - NB + 1)
                if job.normed:
                    self.norm.pe_wait(pe, job.half)
                split_product(pe, env.bank[i % NB][:, 0:job.n], job.lhs, job.rhs, True, True)\
                    .then_inc(self.up, 1)

        first = []
        if self.early and not self.norm.eps:
            pe.wait_ge(env.x_in, 16)
            self.norm.pe_all(pe)
            run(self.early, 0)
        elif self.early:
            run(self.early, 0)
            self.norm.pe_all(pe)
        else:
            first = self.jobs[:KC]
            run(first, 0)
            self.norm.pe_all(pe)
        run(self.jobs[len(first):], len(self.early) + len(first))
        pe.wait_ge(self.down, self.main)

    def of_step(self, s):
        n = len(self.deferred) // self.STEPS
        return [(self.main + i, self.deferred[i]) for i in range(s * n, (s + 1) * n)] if s < self.STEPS else []

    def pe_deferred(self, pe, s):
        for i, job in self.of_step(s):
            wait(pe, self.down, i - 1)
            split_product(pe, self.env.bank[6 + i % 2][:, 0:job.n], job.lhs, job.rhs, True, True)\
                .then_inc(self.up, 1)
        if s == self.STEPS:
            pe.wait_ge(self.down, self.total)
            pe.wait_ge(self.ones_made, 1)

    def act_deferred(self, act, s):
        for i, job in self.of_step(s):
            act.wait_ge(self.up, i + 1)
            src = self.env.bank[6 + i % 2][:, 0:job.n].rearrange("p (h d) -> p h d", d=job.out.shape[-1])
            act.activation(job.out, src, ACT.Copy).then_inc(self.down, 1)

    def act_parts(self, act):
        for sem, value in self.waits_act:
            act.wait_ge(sem, value)
        for w in self.others:
            act.activation(w.hi, w.raw, ACT.Copy).then_inc(self.hi_act, 1)

    def dve_parts(self, dve, which=slice(None)):
        for i, w in list(enumerate(self.others))[which]:
            dve.wait_ge(self.hi_act, i + 1)
            dve.tensor_tensor(w.lo, w.raw, f32_view(w.hi), ALU.subtract).then_inc(self.lo_dve, 1)

    def act_products(self, act):
        env, NB = self.env, self.NB

        def run(batch, start):
            for i, job in enumerate(batch, start):
                act.wait_ge(self.up, i + 1)
                src = env.bank[i % NB][:, 0:job.n]
                if job.bias is None:
                    src = src.rearrange("p (h d) -> p h d", d=job.out.shape[-1])
                    ins = act.activation(job.out, src, ACT.Copy)
                else:
                    ins = act.activation(job.out, src, ACT.Identity, bias=job.bias)
                ins.then_inc(self.down, 1)

        first = [] if self.early else self.jobs[:KC]
        if self.early and not self.norm.eps:
            self.norm.act_all(act)
            run(self.early, 0)
        else:
            run(self.early + first, 0)
            self.norm.act_all(act)
        run(self.jobs[len(first):], len(self.early) + len(first))


class LateParameters:

    def __init__(self, env, a, bank):
        self.env, self.a, self.bank = env, a, bank
        self.rows_in = env.sem("late_rows_in")
        self.up, self.down = env.sem("late_cols_up"), env.sem("late_cols_down")
        at, self.used = place_rows()

    def load(self, sp):
        env, a = self.env, self.a
        at, used = place_rows()
        sp.dma_start(env.mask0[:, :, :], a["mask_Bx1xSxS2_ff0"].rearrange("b o q s -> q (b o) s"))\
            .then_inc(env.mask_in, 16)
        self.rows_count = sum(load_rows(env, sp, a, env.rows, at, name, self.rows_in)
                              for tile in ROW_TILES[1:] for name, n in tile)
        for name in FREE_VECTORS:
            sp.dma_start(env.free[name][:, :], a[name].rearrange("(a n) -> a n", a=1).to_broadcast([P, D]))\
                .then_inc(env.free_in, 16)
        load_weights(env, sp, a, env.w_ff2, env.ff2_in)
        for pair in range(2):
            env.pair_weights.load(sp, 0, pair, pair)

    def pe_turn(self, pe):
        env = self.env
        pe.wait_ge(self.rows_in, self.rows_count)
        for t, n in list(enumerate(self.used))[1:]:
            mm = pe.transpose(self.bank[:, P * t:P * t + n], env.rows[t][0:n, :], env.ident[0:n, 0:n])
        mm.then_inc(self.up, 1)

    def dve_copy(self, dve):
        dve.wait_ge(self.up, 1)
        for t, n in list(enumerate(self.used))[1:]:
            ins = dve.tensor_copy(self.env.cols[t][:, 0:n], self.bank[:, P * t:P * t + n])
        ins.then_inc(self.down, 1)
        dve.wait_ge(self.down, 1)


def short_head_attention(env, name, heads, hd, kv_heads, scale, mask, per_sequence, multiply,
                         head_mask, q_all, k_all, v_all, w_o, v_bias, before, late=None,
                         ahead=None, norm_after=None, parts_ready=False, pool_after=None):
    nc = env.nc
    NG = heads // 4
    CG = NG // KC
    BODY = 2 * NG
    W = hd + 1
    LT, LP = 3, 4
    LN, LO, LH, LW, LA = LP + NG, LP + NG, LP + NG + 1, LP + NG + 2, LP + NG + 3
    with ExitStack() as stack:
        sb = env.scoped(stack)
        masked = sb(name + "_masked", [P, 4, 4, S])
        probs = sb(name + "_probs", [P, 4, 4, S])
        group_mask = sb(name + "_group_mask", [P, 4])
        row_mask = sb(name + "_row_mask", [P, CG])
        keys = sb(name + "_keys", [P, 2, KC, 4, S])
        qs = sb(name + "_qs", [P, 2, KC, CG, S])
        shift = None if not multiply else sb(name + "_shift", [P, mask.shape[1], S])
        nmax = sb(name + "_nmax", [P, 4, 4])
        probsT = sb(name + "_probsT", [P, 2, 4 * S])
        rinv = sb(name + "_rinv", [P, 2, heads])
        heads_out = sb(name + "_heads_out", [P, 2, D])
        heads_outT = sb(name + "_heads_outT", [P, 2, KC * S])
        SB, TB, OB, TOB, WB = env.bank[0:2], env.bank[2:4], env.bank[4:6], env.bank[6], env.bank[7]
        mask_made = env.sem(name + "_mask_made")
        staged = env.sem(name + "_staged")
        gate = env.sem(name + "_gate")
        scores_up = env.sem(name + "_scores_up")
        masked_done = env.sem(name + "_masked")
        shifted = env.sem(name + "_shifted")
        max_done = env.sem(name + "_max")
        exp_done = env.sem(name + "_exp")
        turned = env.sem(name + "_turned")
        turned_out = env.sem(name + "_turned_out")
        pv_done = env.sem(name + "_pv")
        rinv_done = env.sem(name + "_rinv")
        normed = env.sem(name + "_normed")
        heads_turned = env.sem(name + "_heads_turned")
        heads_turned_out = env.sem(name + "_heads_turned_out")
        out_up = env.sem(name + "_out_up")
        added = env.sem(name + "_added")
        shift_done = env.sem(name + "_shift_done")
        late = LateParameters(env, late, OB[1]) if late else None
        if ahead:
            ahead = Norm(env, sb, name + "_ahead", ahead[0], ahead[1], 1e-5, SB, like=before.norm, halves=(0,))
        block = stack.enter_context(nc.Block())

        def run(step, engine, after=None):
            for s in range(BODY):
                step(0, s, lambda lag, s=s: s >= lag, True)
            with engine.Fori(1, B // 2) as it:
                for s in range(BODY):
                    step(it * 2, s, lambda lag: True, True)
            for s in range(LA):
                step(B, s, lambda lag, s=s: s < lag, False)
                if after:
                    after(s)

        if late:
            @block.sync
            def _(sp):
                late.load(sp)

        @block.gpsimd
        def _(pool):
            def stage(b, par):
                now = bass.ds(b * S, S)
                wait(pool, scores_up, (b - 1) * NG)
                pool.sem_inc(gate, 1)
                for c in range(KC):
                    pool.tensor_tensor(keys[:, par, c, :, :], k_all[:, c, now].unsqueeze(1).to_broadcast([P, 4, S]),
                                       group_mask[:, :].unsqueeze(2).to_broadcast([P, 4, S]), ALU.mult)
                    pool.tensor_tensor(qs[:, par, c, :, :], q_all[:, c, now].unsqueeze(1).to_broadcast([P, CG, S]),
                                       row_mask[:, :].unsqueeze(2).to_broadcast([P, CG, S]), ALU.mult)\
                        .then_inc(staged, 1)

            if not parts_ready:
                before.pool_parts(pool)
            pool.wait_ge(mask_made, 1)
            pool.wait_ge(before.down, before.ready_half)
            stage(0, 0)
            stage(1, 1)
            before.pool_bias(pool)
            pool.wait_ge(before.down, before.main)
            with pool.Fori(1, B // 2) as it:
                for par in range(2):
                    stage(it * 2 + par, par)
            if ahead:
                ahead.pool_all(pool)
            if pool_after:
                pool_after(pool)
            if norm_after:
                norm_after.pool_rstd(pool)

        @block.tensor
        def _(pe):
            def step(seq0, s, live, on):
                g = seq0 * NG + s
                if on:
                    par, grp = s // NG, s % NG
                    c, i = grp // CG, grp % CG
                    if i == 0:
                        wait(pe, staged, KC * (seq0 + par) + c + 1)
                    wait(pe, masked_done, g - 1)
                    pe.matmul(SB[s % 2][:, :], qs[:, par, c, i, :], keys[:, par, c, :, :], start=True, stop=True)\
                        .then_inc(scores_up, 1)
                if isinstance(seq0, int) and on:
                    before.pe_deferred(pe, s)
                if live(LT):
                    wait(pe, exp_done, g - LT + 1)
                    wait(pe, turned_out, g - LT - 1)
                    for h in range(4):
                        mm = pe.transpose(TB[s % 2][:, h * S:(h + 1) * S], probs[:, (s - LT) % 4, h, :],
                                          env.ident[:, :])
                    mm.then_inc(turned, 1)
                if live(LP):
                    par, grp = ((s - LP) // NG) % 2, (s - LP) % NG
                    b = seq0 + (s - LP) // NG
                    wait(pe, turned_out, g - LP + 1)
                    for h in range(4):
                        head = grp * 4 + h
                        kv = head * kv_heads // heads
                        mm = pe.matmul(OB[par][:, head * W:(head + 1) * W],
                                       probsT[:, (s - LP) % 2, h * S:(h + 1) * S],
                                       v_all[:, bass.ds(b, 1), kv, :].rearrange("p o w -> p (o w)"),
                                       start=True, stop=True)
                    mm.then_inc(pv_done, 1)
                if (s - LO) % NG == 0 and live(LO):
                    par, seq = ((s - LO) // NG) % 2, seq0 + (s - LO) // NG
                    wait(pe, normed, seq + 1)
                    for c in range(KC):
                        mm = pe.transpose(TOB[:, c * S:(c + 1) * S], heads_out[:, par, c * P:(c + 1) * P],
                                          env.ident[:, :])
                    mm.then_inc(heads_turned, 1)
                if (s - LW) % NG == 0 and live(LW):
                    par, seq = ((s - LW) // NG) % 2, seq0 + (s - LW) // NG
                    wait(pe, heads_turned_out, seq + 1)
                    wait(pe, added, seq + 1)
                    for c in range(KC):
                        mm = pe.matmul(WB[:, 0:D], heads_outT[:, par, c * S:(c + 1) * S], w_o[:, c, :],
                                       start=c == 0, stop=c == KC - 1)
                    mm.then_inc(out_up, 1)

            def norm_ahead(s):
                if s == LP - 1 and ahead:
                    ahead.pe_turn(pe, 0)

            before.pe_all(pe)
            if late:
                late.pe_turn(pe)
            run(step, pe, norm_ahead)

        @block.scalar
        def _(act):
            def step(seq0, s, live, on):
                g = seq0 * NG + s
                if live(LT):
                    wait(act, turned, g - LT + 1)
                    wait(act, pv_done, g - LT - 1)
                    act.activation(probsT[:, (s - LT) % 2, :], TB[s % 2][:, :], ACT.Copy)\
                        .then_inc(turned_out, 1)
                if (s - LH) % NG == 0 and live(LH):
                    par, seq = ((s - LH) // NG) % 2, seq0 + (s - LH) // NG
                    wait(act, heads_turned, seq + 1)
                    for c in range(KC):
                        ins = act.activation(heads_outT[:, par, c * S:(c + 1) * S], TOB[:, c * S:(c + 1) * S],
                                             ACT.Identity, bias=v_bias[:, c:c + 1])
                    ins.then_inc(heads_turned_out, 1)
                if on:
                    wait(act, max_done, g + 1)
                    wait(act, turned, g - 3)
                    for h in range(4):
                        ins = act.activation(probs[:, s % 4, h, :], masked[:, s % 4, h, :], ACT.Exp,
                                             bias=nmax[:, s % 4, h:h + 1])
                    ins.then_inc(exp_done, 1)
                    if isinstance(seq0, int):
                        before.act_deferred(act, s)

            def norm_ahead(s):
                if s == LP - 1 and ahead:
                    ahead.act_evacuate(act, 0)

            if not parts_ready:
                before.act_parts(act)
            before.act_products(act)
            run(step, act, norm_ahead)

        @block.vector
        def _(dve):
            dve.wait_ge(env.masks_made, 6)
            dve.tensor_reduce(row_mask[:, :], head_mask[:, :].rearrange("p (g j) -> p g j", j=4), X, ALU.max)
            dve.tensor_reduce(group_mask[:, :], head_mask[:, :].rearrange("p (g j) -> p j g", j=4), X, ALU.max)\
                .then_inc(mask_made, 1)
            if parts_ready:
                before.norm.dve_all(dve)
            else:
                before.dve_parts(dve, slice(0, 1))
                before.norm.dve_all(dve, lambda: before.dve_parts(dve, slice(1, None)))
            if late:
                late.dve_copy(dve)
            dve.sem_inc(added, 1)
            dve.wait_ge(env.mask_in, 16)
            if multiply:
                dve.tensor_scalar(shift[:, :, :], mask[:, :, :], 10000.0, -10000.0, ALU.mult, ALU.add)\
                    .then_inc(shift_done, 1)
                dve.wait_ge(shift_done, 1)

            def step(seq0, s, live, on):
                g = seq0 * NG + s
                if (s - LN) % NG == 0 and live(LN):
                    k = (s - LN) // NG
                    par, seq = k % 2, seq0 + k
                    o = OB[par][:, 0:heads * W].rearrange("p (h w) -> p h w", w=W)
                    wait(dve, pv_done, g - LP)
                    dve.reciprocal(rinv[:, par, :], o[:, :, hd]).then_inc(rinv_done, 1)
                    wait(dve, rinv_done, seq + 1)
                    dve.tensor_tensor(heads_out[:, par, :].rearrange("p (h d) -> p h d", d=hd), o[:, :, 0:hd],
                                      rinv[:, par, :].unsqueeze(2).to_broadcast([P, heads, hd]), ALU.mult)\
                        .then_inc(normed, 1)
                if (s - LA) % NG == 0 and live(LA):
                    seq = seq0 + (s - LA) // NG
                    if isinstance(seq, int) and seq == 0:
                        dve.wait_ge(before.bias_added, 1)
                    wait(dve, out_up, seq + 1)
                    xb = env.x[:, bass.ds(seq, 1), :].rearrange("p o d -> p (o d)")
                    dve.tensor_tensor(xb, WB[:, 0:D], xb, ALU.add).then_inc(added, 1)
                if on:
                    b = seq0 + s // NG if per_sequence else 0
                    wait(dve, scores_up, g + 1)
                    wait(dve, exp_done, g - 3)
                    dve.scalar_tensor_tensor(masked[:, s % 4, :, :],
                                             SB[s % 2][:, :].rearrange("p (h n) -> p h n", n=S), scale,
                                             mask[:, bass.ds(b, 1), :].to_broadcast([P, 4, S]),
                                             ALU.mult, ALU.mult if multiply else ALU.add)\
                        .then_inc(masked_done, 1)
                    wait(dve, masked_done, g + 1)
                    if multiply:
                        dve.tensor_tensor(masked[:, s % 4, :, :], masked[:, s % 4, :, :],
                                          shift[:, bass.ds(b, 1), :].to_broadcast([P, 4, S]), ALU.add)\
                            .then_inc(shifted, 1)
                        wait(dve, shifted, g + 1)
                    dve.tensor_reduce(nmax[:, s % 4, :], masked[:, s % 4, :, :], X, ALU.max, negate=True)\
                        .then_inc(max_done, 1)

            def norm_ahead(s):
                if s == 0:
                    dve.wait_ge(added, 1 + B // 2)
                    if ahead:
                        ahead.dve_stats(dve, 0)
                    if norm_after:
                        norm_after.dve_stats(dve)
                elif s == 1:
                    if ahead:
                        ahead.dve_normalise(dve, 0)
                    if norm_after:
                        norm_after.dve_normalise(dve)
                elif s == LP and ahead:
                    ahead.dve_split(dve, 0)

            run(step, dve, norm_ahead)


class PairWeights:

    QUERIES, KEYS, VALUES = range(3)

    def __init__(self, env, sb, a):
        n = 2 * P
        self.raw = sb("la_w_raw", [P, 2, 3, KC, n])
        self.hi = sb("la_w_hi", [P, 2, 3, KC, n], F32R)
        self.lo = sb("la_w_lo", [P, 2, 3, KC, n], F32R)
        self.loaded = [env.lasting_sem("la_w_in0"), env.lasting_sem("la_w_in1")]
        self.split_done = env.lasting_sem("la_w_split")
        self.dram = [[a["L2_xattn_" + w + str(k + 1)].rearrange("(c p) n -> p c n", p=P)
                      for w in ("wq", "wk", "wv")] for k in range(2)]

    def load(self, sp, layer, turn, par):
        for k in range(3):
            sp.dma_start(self.raw[:, par, k, :, :], self.dram[layer][k][:, :, bass.ds(turn * 2 * P, 2 * P)])\
                .then_inc(self.loaded[par], 16)

    def pool_split(self, pool, pair, par):
        for i, which in enumerate((self.KEYS, self.VALUES, self.QUERIES)):
            hi, raw = self.hi[:, par, which], self.raw[:, par, which]
            pool.tensor_copy(hi, raw).then_inc(self.split_done, 1)
            wait(pool, self.split_done, 6 * pair + 2 * i + 1)
            pool.tensor_tensor(self.lo[:, par, which], raw, f32_view(hi), ALU.subtract)\
                .then_inc(self.split_done, 1)

    def pool_split_first(self, pool):
        for pair in range(2):
            pool.wait_ge(self.loaded[pair], 48)
            self.pool_split(pool, pair, pair)


ALL, CONTEXT_ONLY, NOTHING = "all", "context only", "nothing"


def long_head_attentions(env, a):
    nc = env.nc
    H, K, PAIRS = 16, P, 8
    LAYERS = 2
    T = S + 2
    SCALE = float(K) ** -0.5
    GR = H + 2
    PREP_OF_LAYER = 5
    LT, LP, LW = 1, 2, 3
    QUERIES, KEYS, VALUES = PairWeights.QUERIES, PairWeights.KEYS, PairWeights.VALUES
    L2 = "L2_xattn_"

    def vectors(name):
        return [env.col(L2 + name + str(n + 1)) for n in range(LAYERS)]

    bq, bk, bv, bias_k, bias_v = (vectors(n) for n in ("bq", "bk", "bv", "bias_k", "bias_v"))
    with ExitStack() as stack:
        sb = env.scoped(stack)
        weights = env.pair_weights
        w_hi, w_lo, w_in, w_split = weights.hi, weights.lo, weights.loaded, weights.split_done
        wo_raw = sb("la_wo_raw", [P, 2, 2, D])
        wo_hi = sb("la_wo_hi", [P, 2, 2, D], F32R)
        wo_lo = sb("la_wo_lo", [P, 2, 2, D], F32R)
        qT = sb("la_qT", [P, 2, 2, TOK])
        kT = sb("la_kT", [P, 2, 2, B, T])
        v = sb("la_v", [P, 2, B, 2 * K])
        bq_scaled = sb("la_bq_scaled", [P, LAYERS, H])
        extra = sb("la_extra", [P, LAYERS, H, GR])
        extra_hi = sb("la_extra_hi", [P, LAYERS, H, GR], F32R)
        extra_lo = sb("la_extra_lo", [P, LAYERS, H, GR], F32R)
        extra_now = sb("la_extra_now", [P, 2, 2, 2, GR], F32R)
        wb = sb("la_wb", [P, B, GR])
        wbT = sb("la_wbT", [GR, 4, P])
        G = sb("la_G", [GR, D])
        nmax = sb("la_nmax", [P, 2, 2])
        den = sb("la_den", [P, 2, 2])
        rinv = sb("la_rinv", [P, 2, 2])
        probs = sb("la_probs", [P, 2, 2, T])
        probs_n = sb("la_probs_n", [P, 2, 2, S + 1])
        probsT = sb("la_probsT", [P, 2, 2 * S])
        o_hi = sb("la_o_hi", [P, 2, 2 * S], F32R)
        o_lo = sb("la_o_lo", [P, 2, 2 * S], F32R)
        SB, KQB, VB = env.bank[0:2], env.bank[2], env.bank[3]
        TB, OB, WB, GB = env.bank[4], env.bank[5], env.bank[6], env.bank[7]
        sem = lambda s: env.sem("la_" + s)
        wo_in = [sem("wo_in0"), sem("wo_in1")]
        wo_split = sem("wo_split")
        side = sem("side")
        prep = sem("prep")
        bq_done = sem("bq_done")
        kq_up, kq_down = sem("kq_up"), sem("kq_down")
        v_up, v_down = sem("v_up"), sem("v_down")
        scores_up = sem("scores_up")
        max_done = sem("max")
        exp_done = sem("exp")
        rinv_done = sem("rinv")
        scaled = sem("scaled")
        turned, turned_out = sem("turned"), sem("turned_out")
        pv_done = sem("pv")
        o_hi_done, o_lo_done = sem("o_hi"), sem("o_lo")
        out_up, added = sem("out_up"), sem("added")
        g_done = sem("g_done")
        wb_done = sem("wb_done")
        g_out = sem("g_out")
        bo_added = sem("bo_added")
        norm0 = TokenNorm(env, "la_n0", 1, 1e-6, env.free["L0_xattn_gamma"], env.free["L0_xattn_beta"])
        nl_up, nl_scaled, nl_added = sem("nl_up"), sem("nl_scaled"), sem("nl_added")
        act_gate, pool_gate = sem("act_gate"), sem("pool_gate")
        norms = []
        for n, ln in enumerate(("ln1", "ln2", "ln_mlp")):
            gamma, beta = (env.col(f"{L2}{ln}_{part}") for part in ("scale", "offset"))
            norms.append(Norm(env, sb, f"la_ln{n}", gamma, beta, 1e-5, SB, like=norms[0] if n else None,
                              halves=(0, 1) if n < LAYERS else (0,)))
        wy = norms[0].xn
        block = stack.enter_context(nc.Block())

        wo_dram = [a[L2 + "wo" + str(n + 1)].rearrange("(h d) n -> d h n", d=K) for n in range(LAYERS)]
        bo = [env.free[L2 + "bo" + str(n + 1)] for n in range(LAYERS)]

        def run(layer, step, engine, after=None):
            for b in range(B):
                step(layer, 0, 0, b, lambda lag, b=b: b >= lag, True, ALL)
            with engine.Fori(0, 3) as it:
                for k in range(2):
                    for b in range(B):
                        step(layer, it * 2 + 1 + k, (1 + k) % 2, b, lambda lag: True, True, ALL)
            for b in range(B):
                step(layer, PAIRS - 1, (PAIRS - 1) % 2, b, lambda lag: True, True,
                     CONTEXT_ONLY if layer < LAYERS - 1 else NOTHING)
                if after:
                    after(b)

        def drain(layer, step, b):
            step(layer, PAIRS, 0, b, lambda lag: b < lag, False, NOTHING)

        def last_of(turn, b, lag):
            return isinstance(turn, int) and (turn == PAIRS or turn == PAIRS - 1 and b >= lag)

        @block.sync
        def _(sp):
            def load(layer, turn, par):
                pair = layer * PAIRS + turn
                if not isinstance(pair, int) or pair >= 2:
                    wait(sp, w_split, 6 * (pair - 1))
                    weights.load(sp, layer, turn, par)
                wait(sp, wo_split, 2 * (pair - 1))
                sp.dma_start(wo_raw[:, par, :, :], wo_dram[layer][:, bass.ds(turn * 2, 2), :])\
                    .then_inc(wo_in[par], 16)

            for layer in range(LAYERS):
                for turn in range(2):
                    load(layer, turn, turn)
                with sp.Fori(1, PAIRS // 2) as it:
                    for par in range(2):
                        load(layer, it * 2 + par, par)

        @block.gpsimd
        def _(pool):
            def split_qkv(layer, turn, par, half_turn):
                pair = layer * PAIRS + turn
                wait(pool, w_in[par], 48 * (half_turn + layer * PAIRS // 2 + 1))
                wait(pool, kq_up, 8 * (pair - 1))
                wait(pool, v_up, 8 * (pair - 1))
                pool.sem_inc(pool_gate, 1)
                weights.pool_split(pool, pair, par)

            def split_o(layer, turn, par, half_turn):
                pair = layer * PAIRS + turn
                wait(pool, wo_in[par], 16 * (half_turn + layer * PAIRS // 2 + 1))
                wait(pool, out_up, 8 * (pair - 1))
                wait(pool, g_done, pair - 1)
                pool.sem_inc(pool_gate, 1)
                pool.tensor_copy(wo_hi[:, par], wo_raw[:, par]).then_inc(wo_split, 1)
                wait(pool, wo_split, 2 * pair + 1)
                pool.tensor_tensor(wo_lo[:, par], wo_raw[:, par], f32_view(wo_hi[:, par]), ALU.subtract)\
                    .then_inc(wo_split, 1)
                for k, part in enumerate((extra_hi, extra_lo)):
                    pool.tensor_copy(extra_now[:, par, k, :, :],
                                     f32_view(part[:, layer, bass.ds(turn * 2, 2), :]))
                wait(pool, scores_up, 8 * (pair - 1))
                pool.sem_inc(pool_gate, 1)
                pool.tensor_copy(kT[:, par, :, :, S:T],
                                 bias_k[layer][:, bass.ds(turn * 2, 2)].unsqueeze(2).unsqueeze(3)
                                 .to_broadcast([P, 2, B, 2])).then_inc(side, 1)

            def left_factors():
                for n in range(LAYERS):
                    count = n * PREP_OF_LAYER
                    pool.memset(extra[:, n, :, :], 0.0).then_inc(prep, 1)
                    pool.wait_ge(prep, count + 1)
                    flat_extra = extra[:, n, :, :].rearrange("p h g -> p (h g)")
                    pool.tensor_tensor(flat_extra[:, 0:(GR + 1) * (H - 1) + 1:GR + 1], bias_v[n], bv[n],
                                       ALU.subtract).then_inc(prep, 1)
                    pool.tensor_copy(extra[:, n, :, H], bv[n]).then_inc(prep, 1)
                    pool.wait_ge(prep, count + 3)
                    pool.tensor_copy(extra_hi[:, n, :, :], extra[:, n, :, :]).then_inc(prep, 1)
                    pool.wait_ge(prep, count + 4)
                    pool.tensor_tensor(extra_lo[:, n, :, :], extra[:, n, :, :], f32_view(extra_hi[:, n, :, :]),
                                       ALU.subtract).then_inc(prep, 1)
                pool.wait_ge(prep, PREP_OF_LAYER * LAYERS)

            for layer in range(LAYERS):
                if layer == 0:
                    norm0.pool_rstd(pool)
                    left_factors()
                else:
                    split_qkv(layer, 0, 0, 0)
                split_o(layer, 0, 0, 0)
                if layer > 0:
                    split_qkv(layer, 1, 1, 0)
                norms[layer].pool_all(pool)
                pool.wait_ge(norms[layer].normed, B)
                pool.tensor_tensor(env.x[:, :, :], env.x[:, :, :],
                                   bo[layer][:, :].unsqueeze(1).to_broadcast([P, B, D]), ALU.add)\
                    .then_inc(bo_added, 1)
                split_o(layer, 1, 1, 0)
                with pool.Fori(1, PAIRS // 2) as it:
                    for par in range(2):
                        split_qkv(layer, it * 2 + par, par, it)
                        split_o(layer, it * 2 + par, par, it)
            norms[LAYERS].pool_all(pool)

        @block.tensor
        def _(pe):
            def project_kq(layer, turn, par, b, first):
                pair = layer * PAIRS + turn
                if b in (0, 4):
                    wait(pe, w_split, 6 * pair + (2 if b == 0 else 6))
                which, half, head = (KEYS if b < 4 else QUERIES), (b % 4) // 2, b % 2
                a_hi, a_lo = (env.ctx_hi, env.ctx_lo) if which == KEYS else (env.h_hi, env.h_lo)
                cols = slice(half * HALF, (half + 1) * HALF)
                bank = KQB
                if which == QUERIES and first:
                    pe.wait_ge(norms[layer].h_ready, KC * (half + 1))
                    bank = (KQB, VB)[b % 2]
                    pe.wait_ge(v_down, 8 * pair + 8)
                    wait(pe, kq_down, 8 * pair + max(b - 1, 4))
                else:
                    wait(pe, kq_down, 8 * pair + b)
                split_product(pe, bank[:, :],
                              [(w_hi[:, par, which, c, head * K:(head + 1) * K],
                                w_lo[:, par, which, c, head * K:(head + 1) * K]) for c in range(KC)],
                              [(a_hi[:, c, cols], a_lo[:, c, cols]) for c in range(KC)], True, True)\
                    .then_inc(kq_up, 1)

            def project_v(layer, turn, par, b):
                pair = layer * PAIRS + turn
                cols = slice(b * S, (b + 1) * S)
                if b == 0:
                    wait(pe, w_split, 6 * pair + 4)
                wait(pe, v_down, 8 * pair + b)
                split_product(pe, VB[:, 0:2 * K],
                              [(env.ctx_hi[:, c, cols], env.ctx_lo[:, c, cols]) for c in range(KC)],
                              [(w_hi[:, par, VALUES, c, :], w_lo[:, par, VALUES, c, :]) for c in range(KC)], True, True)\
                    .then_inc(v_up, 1)

            def step(layer, turn, par, b, live, attend, ahead):
                pair = layer * PAIRS + turn
                g = pair * 8 + b
                if attend:
                    if b == 0:
                        wait(pe, side, pair + 1)
                        wait(pe, kq_down, 8 * (pair + 1))
                    wait(pe, max_done, g - 1)
                    wait(pe, exp_done, g - 1)
                    for h in range(2):
                        mm = pe.matmul(SB[b % 2][:, h * T:(h + 1) * T], qT[:, par, h, b * S:(b + 1) * S],
                                       kT[:, par, h, b, :], start=True, stop=True)
                    mm.then_inc(scores_up, 1)
                if ahead is ALL:
                    project_kq(layer, turn + 1, 1 - par, b, False)
                    project_v(layer, turn + 1, 1 - par, b)
                elif ahead is CONTEXT_ONLY:
                    if b < 4:
                        project_kq(layer + 1, 0, 0, b, True)
                    project_v(layer + 1, 0, 0, b)
                if live(LT):
                    wait(pe, scaled, g - LT + 1)
                    wait(pe, turned_out, g - LT)
                    for h in range(2):
                        mm = pe.transpose(TB[:, h * S:(h + 1) * S], probs_n[:, (b - LT) % 2, h, 0:S],
                                          env.ident[:, :])
                    if last_of(turn, b, LT):
                        wait(pe, wb_done, g - LT + 2)
                        mm = pe.transpose(TB[0:GR, 2 * S:3 * S], wb[:, (b - LT) % B, :], env.ident[:, :])
                    mm.then_inc(turned, 1)
                if live(LP):
                    own = par if b >= LP else 1 - par
                    if b == LP:
                        wait(pe, v_down, 8 * (pair + 1))
                    wait(pe, turned_out, g - LP + 1)
                    wait(pe, o_lo_done, g - LP)
                    for h in range(2):
                        mm = pe.matmul(OB[:, h * S:(h + 1) * S], v[:, own, (b - LP) % B, h * K:(h + 1) * K],
                                       probsT[:, (b - LP) % 2, h * S:(h + 1) * S], start=True, stop=True)
                    mm.then_inc(pv_done, 1)
                if live(LW):
                    own = par if b >= LW else 1 - par
                    wait(pe, o_lo_done, g - LW + 1)
                    wait(pe, added, g - LW)
                    last = last_of(turn, b, LW)
                    o = (slice(None), (b - LW) % 2)
                    mm = split_product(
                        pe, WB[:, 0:D],
                        [(o_hi[o + (slice(h * S, (h + 1) * S),)], o_lo[o + (slice(h * S, (h + 1) * S),)])
                         for h in range(2)],
                        [(wo_hi[:, own, h, :], wo_lo[:, own, h, :]) for h in range(2)], True, not last)
                    if last:
                        if b == LW:
                            pe.wait_ge(g_out, layer + 1)
                        mm = pe.matmul(WB[:, 0:D], wbT[:, (b - LW) % 4, :], G[:, :], start=False, stop=True)
                    mm.then_inc(out_up, 1)
                if attend and b == 0:
                    first, last = (isinstance(turn, int) and turn == t for t in (0, PAIRS - 1))
                    wait(pe, wo_split, 2 * (pair + 1))
                    for h in range(2):
                        lo, hi = extra_now[:, par, 1, h, :], extra_now[:, par, 0, h, :]
                        pe.matmul(GB[0:GR, 0:D], lo, wo_hi[:, par, h, :], start=first and h == 0, stop=False,
                                  skip_group_check=True)
                        pe.matmul(GB[0:GR, 0:D], hi, wo_lo[:, par, h, :], start=False, stop=False,
                                  skip_group_check=True)
                        mm = pe.matmul(GB[0:GR, 0:D], hi, wo_hi[:, par, h, :], start=False,
                                       stop=last and h == 1, skip_group_check=True)
                    mm.then_inc(g_done, 1)

            def non_local(half):
                for b in range(half * 4, half * 4 + 4):
                    if half == 1:
                        pe.wait_ge(norm0.done, 1)
                        pe.wait_ge(nl_scaled, b - 3)
                    pe.matmul(env.bank[4 + b % 4][:, 0:D], env.qT1[:, b, 0:P], env.x[:, b, :], start=True,
                              stop=True).then_inc(nl_up, 1)

            non_local(0)
            for b in range(4):
                project_kq(0, 0, 0, b, True)
                project_v(0, 0, 0, b)
            non_local(1)
            norms[0].pe_turn(pe, 0)
            for b in range(4, B):
                project_v(0, 0, 0, b)
            norms[0].pe_turn(pe, 1)
            for layer in range(LAYERS):
                for b in range(4, B):
                    project_kq(layer, 0, 0, b, True)
                run(layer, step, pe)
                drain(layer, step, 0)
                norms[layer + 1].pe_turn(pe, 0)
                drain(layer, step, 1)
                drain(layer, step, 2)
                if layer < LAYERS - 1:
                    norms[layer + 1].pe_turn(pe, 1)

        @block.scalar
        def _(act):
            def project_kq(layer, turn, par, b, first=False):
                pair = layer * PAIRS + turn
                which, half, head = (KEYS if b < 4 else QUERIES), (b % 4) // 2, b % 2
                wait(act, kq_up, 8 * pair + b + 1)
                wait(act, scores_up, 8 * (pair - 1))
                act.sem_inc(act_gate, 1)
                at = bass.ds(turn * 2 + head, 1)
                if which == KEYS:
                    act.activation(kT[:, par, head, half * 4:half * 4 + 4, 0:S],
                                   KQB[:, :].rearrange("p (b t) -> p b t", t=S), ACT.Identity,
                                   bias=bk[layer][:, at]).then_inc(kq_down, 1)
                else:
                    bank = (KQB, VB)[b % 2] if first else KQB
                    act.activation(qT[:, par, head, half * HALF:(half + 1) * HALF], bank[:, :], ACT.Identity,
                                   bias=bq_scaled[:, layer, at], scale=SCALE).then_inc(kq_down, 1)

            def project_v(layer, turn, par, b):
                pair = layer * PAIRS + turn
                wait(act, v_up, 8 * pair + b + 1)
                wait(act, pv_done, 8 * (pair - 2) + b + 1)
                act.activation(v[:, par, b, :], VB[:, 0:2 * K], ACT.Copy).then_inc(v_down, 1)

            def step(layer, turn, par, b, live, attend, ahead):
                pair = layer * PAIRS + turn
                g = pair * 8 + b
                if attend:
                    wait(act, max_done, g + 1)
                    wait(act, scaled, g - 1)
                    for h in range(2):
                        ins = act.activation(probs[:, b % 2, h, 0:S + 1], SB[b % 2][:, h * T:h * T + S + 1],
                                             ACT.Exp, bias=nmax[:, b % 2, h:h + 1],
                                             accum_out=den[:, b % 2, h:h + 1])
                    ins.then_inc(exp_done, 1)
                if ahead is ALL:
                    project_kq(layer, turn + 1, 1 - par, b)
                    project_v(layer, turn + 1, 1 - par, b)
                elif ahead is CONTEXT_ONLY:
                    if b < 4:
                        project_kq(layer + 1, 0, 0, b)
                    project_v(layer + 1, 0, 0, b)
                if last_of(turn, b, 0) and b == 1 and attend:
                    act.wait_ge(g_done, PAIRS * (layer + 1))
                    act.activation(G[:, :], GB[0:GR, 0:D], ACT.Copy).then_inc(g_out, 1)
                if live(LP):
                    wait(act, pv_done, g - LP + 1)
                    wait(act, out_up, g - LP - 1)
                    act.activation(o_hi[:, b % 2, :], OB[:, 0:2 * S], ACT.Copy).then_inc(o_hi_done, 1)

            def non_local(half):
                for b in range(half * 4, half * 4 + 4):
                    act.wait_ge(nl_up, b + 1)
                    act.activation(wy[:, b, :], env.bank[4 + b % 4][:, 0:D], ACT.Identity,
                                   scale=env.bn_scale[:, 0:1], bias=env.bn_shift[:, b:b + 1])\
                        .then_inc(nl_scaled, 1)

            non_local(0)
            for b in range(4):
                project_kq(0, 0, 0, b)
                project_v(0, 0, 0, b)
            non_local(1)
            norms[0].act_evacuate(act, 0)
            for b in range(4, B):
                project_v(0, 0, 0, b)
            norms[0].act_evacuate(act, 1)
            act.wait_ge(bq_done, 1)
            for layer in range(LAYERS):
                for b in range(4, B):
                    project_kq(layer, 0, 0, b, first=True)
                run(layer, step, act)
                drain(layer, step, 0)
                norms[layer + 1].act_evacuate(act, 0)
                drain(layer, step, 1)
                drain(layer, step, 2)
                if layer < LAYERS - 1:
                    norms[layer + 1].act_evacuate(act, 1)

        @block.vector
        def _(dve):
            norm0.dve_stats(dve)
            for n in range(LAYERS):
                ins = dve.tensor_scalar(bq_scaled[:, n, :], bq[n], SCALE, None, ALU.mult)
            ins.then_inc(bq_done, 1)
            dve.memset(wb[:, :, H:H + 1], 1.0)
            dve.memset(wb[:, :, H + 1:GR], 0.0).then_inc(wb_done, 1)

            def add_non_local(half):
                for b in range(half * 4, half * 4 + 4):
                    dve.wait_ge(nl_scaled, b + 1)
                    if half == 1:
                        dve.wait_ge(norm0.done, 1)
                    dve.tensor_tensor(env.x[:, b, :], env.x[:, b, :], wy[:, b, :], ALU.add).then_inc(nl_added, 1)
                dve.wait_ge(nl_added, 4 * half + 4)

            add_non_local(0)
            norms[0].dve_stats(dve, 0)
            norm0.dve_normalise(dve)
            norms[0].dve_normalise(dve, 0)
            add_non_local(1)
            norms[0].dve_stats(dve, 1)
            norms[0].dve_split(dve, 0)
            norms[0].dve_normalise(dve, 1)
            norms[0].dve_split(dve, 1)

            def step(layer, turn, par, b, live, attend, ahead):
                pair = layer * PAIRS + turn
                g = pair * 8 + b
                if attend:
                    wait(dve, scores_up, g + 1)
                    wait(dve, exp_done, g - 1)
                    dve.tensor_reduce(nmax[:, b % 2, :],
                                      SB[b % 2][:, 0:2 * T].rearrange("p (h t) -> p h t", t=T)[:, :, 0:S + 1],
                                      X, ALU.max, negate=True).then_inc(max_done, 1)
                if live(LT):
                    wait(dve, turned, g - LT + 1)
                    wait(dve, pv_done, g - LT - 1)
                    if last_of(turn, b, LT):
                        dve.tensor_copy(wbT[:, (b - LT) % 4, :], TB[0:GR, 2 * S:3 * S])
                    dve.tensor_copy(probsT[:, (b - LT) % 2, :], TB[:, 0:2 * S]).then_inc(turned_out, 1)
                if attend:
                    wait(dve, exp_done, g + 1)
                    dve.reciprocal(rinv[:, b % 2, :], den[:, b % 2, :]).then_inc(rinv_done, 1)
                    wait(dve, rinv_done, g + 1)
                    wait(dve, turned, g - 1)
                    wait(dve, wb_done, g)
                    for h in range(2):
                        ins = dve.tensor_scalar(probs_n[:, b % 2, h, :], probs[:, b % 2, h, 0:S + 1],
                                                rinv[:, b % 2, h:h + 1], None, ALU.mult)
                    ins.then_inc(scaled, 1)
                    wait(dve, scaled, g + 1)
                    dve.tensor_copy(wb[:, b, bass.ds(turn * 2, 2)], probs_n[:, b % 2, :, S]).then_inc(wb_done, 1)
                if live(LP):
                    wait(dve, o_hi_done, g - LP + 1)
                    wait(dve, out_up, g - LP - 1)
                    dve.tensor_tensor(o_lo[:, b % 2, :], OB[:, 0:2 * S], f32_view(o_hi[:, b % 2, :]),
                                      ALU.subtract).then_inc(o_lo_done, 1)
                if live(LW):
                    if b == LW and isinstance(turn, int) and turn == 0:
                        dve.wait_ge(bo_added, layer + 1)
                    wait(dve, out_up, g - LW + 1)
                    xb = env.x[:, (b - LW) % B, :]
                    dve.tensor_tensor(xb, WB[:, 0:D], xb, ALU.add).then_inc(added, 1)

            for layer in range(LAYERS):
                norm = norms[layer + 1]

                def norm_ahead(b):
                    if b == 6:
                        dve.wait_ge(added, PAIRS * B * (layer + 1) - 4)
                        norm.dve_stats(dve, 0)
                    elif b == 7:
                        norm.dve_normalise(dve, 0)

                run(layer, step, dve, norm_ahead)
                drain(layer, step, 0)
                drain(layer, step, 1)
                norm.dve_split(dve, 0)
                drain(layer, step, 2)
                if layer < LAYERS - 1:
                    dve.wait_ge(added, PAIRS * B * (layer + 1))
                    norm.dve_stats(dve, 1)
                    norm.dve_normalise(dve, 1)
                    norm.dve_split(dve, 1)


def feed_forward(env, name, gamma, beta, w1, w2, b1, b2, func, w_in=None, load_next=None, ahead=None,
                 out=None):
    nc = env.nc
    F = w1.shape[2]
    FC = F // P
    with ExitStack() as stack:
        sb = env.scoped(stack)
        w1_hi, w1_lo = sb(name + "_w1_hi", [P, KC, F], F32R), sb(name + "_w1_lo", [P, KC, F], F32R)
        w2_hi, w2_lo = sb(name + "_w2_hi", [P, FC, D], F32R), sb(name + "_w2_lo", [P, FC, D], F32R)
        with ExitStack() as first:
            norm = Norm(env, env.scoped(first), name + "_ln", gamma, beta, 1e-5, env.bank[6:8], halves=(1,))
        act_hi = sb(name + "_act_hi", [P, NHALF, FC, HALF], F32R)
        act_lo = sb(name + "_act_lo", [P, NHALF, FC, HALF], F32R)
        if ahead:
            ahead = Norm(env, sb, name + "_ahead", ahead[0], ahead[1], 1e-5, env.bank[0:2], like=norm,
                         halves=(0,))
        act_full = sb(name + "_act", [P, 2, HALF])
        w_hi_done, w_lo_done = env.sem(name + "_w_hi"), env.sem(name + "_w_lo")
        w2_hi_done = env.sem(name + "_w2_hi_done")
        b2_added = env.sem(name + "_b2")
        up, acted = env.sem(name + "_up"), env.sem(name + "_acted")
        hi_done, lo_done = env.sem(name + "_hi"), env.sem(name + "_lo")
        out_up, added = env.sem(name + "_out_up"), env.sem(name + "_added")
        stored = env.sem(name + "_stored")
        NJ = FC * NHALF
        AHEAD = 2
        block = stack.enter_context(nc.Block())

        @block.gpsimd
        def _(pool):
            if w_in:
                pool.wait_ge(*w_in)
            count = 0
            for f in range(FC):
                cols = slice(f * P, (f + 1) * P)
                pool.tensor_copy(w1_hi[:, :, cols], w1[:, :, cols]).then_inc(w_hi_done, 1)
                count += 1
                pool.wait_ge(w_hi_done, count)
                pool.tensor_tensor(w1_lo[:, :, cols], w1[:, :, cols], f32_view(w1_hi[:, :, cols]), ALU.subtract)\
                    .then_inc(w_lo_done, 1)
                if f == 1:
                    norm.pool_all(pool)
            for f in range(FC):
                pool.wait_ge(w2_hi_done, f + 1)
                pool.tensor_tensor(w2_lo[:, f, :], w2[:, f, :], f32_view(w2_hi[:, f, :]), ALU.subtract)\
                    .then_inc(w_lo_done, 1)
            if ahead:
                ahead.pool_all(pool)

        @block.tensor
        def _(pe):
            for half in range(NHALF):
                norm.pe_wait(pe, half)
                cols = slice(half * HALF, (half + 1) * HALF)
                for f in range(FC):
                    j = half * FC + f
                    if j == AHEAD:
                        norm.pe_all(pe)
                    fs = slice(f * P, (f + 1) * P)
                    pe.wait_ge(w_lo_done, f + 1)
                    wait(pe, acted, j - 3)
                    split_product(pe, env.bank[j % 4][:, :],
                                  [(w1_hi[:, c, fs], w1_lo[:, c, fs]) for c in range(KC)],
                                  [(env.h_hi[:, c, cols], env.h_lo[:, c, cols]) for c in range(KC)], True, True)\
                        .then_inc(up, 1)
            pe.wait_ge(w_lo_done, 2 * FC)
            for b in range(B):
                half, k = divmod(b, 4)
                pe.wait_ge(lo_done, FC * (half + 1))
                wait(pe, added, b - 3)
                cols = slice(k * S, (k + 1) * S)
                split_product(pe, env.bank[4 + b % 4][:, 0:D],
                              [(act_hi[:, half, f, cols], act_lo[:, half, f, cols]) for f in range(FC)],
                              [(w2_hi[:, f, :], w2_lo[:, f, :]) for f in range(FC)], True, True)\
                    .then_inc(out_up, 1)
                if ahead and b == 6:
                    ahead.pe_all(pe)

        @block.scalar
        def _(act):
            if w_in:
                act.wait_ge(*w_in)
            for j in range(NJ):
                f = j % FC
                if j == AHEAD:
                    norm.act_all(act)
                if j < FC:
                    act.activation(w2_hi[:, j, :], w2[:, j, :], ACT.Copy).then_inc(w2_hi_done, 1)
                act.wait_ge(up, j + 1)
                wait(act, lo_done, j - 1)
                act.activation(act_full[:, j % 2, :], env.bank[j % 4][:, :], func, bias=b1[:, f:f + 1])\
                    .then_inc(acted, 1)
            if ahead:
                ahead.act_all(act)

        @block.vector
        def _(dve):
            norm.dve_all(dve)
            dve.tensor_tensor(env.x[:, :, :], env.x[:, :, :],
                              b2[:, :].unsqueeze(1).to_broadcast([P, B, D]), ALU.add).then_inc(b2_added, 1)
            for j in range(NJ):
                half, f = divmod(j, FC)
                dve.wait_ge(acted, j + 1)
                dve.tensor_copy(act_hi[:, half, f, :], act_full[:, j % 2, :]).then_inc(hi_done, 1)
                dve.wait_ge(hi_done, j + 1)
                dve.tensor_tensor(act_lo[:, half, f, :], act_full[:, j % 2, :],
                                  f32_view(act_hi[:, half, f, :]), ALU.subtract).then_inc(lo_done, 1)
            dve.wait_ge(b2_added, 1)
            for b in range(B):
                dve.wait_ge(out_up, b + 1)
                dve.tensor_tensor(env.x[:, b, :], env.bank[4 + b % 4][:, 0:D], env.x[:, b, :], ALU.add)\
                    .then_inc(added, 1)
                if ahead and b == 3:
                    dve.wait_ge(added, 4)
                    ahead.dve_stats(dve, 0)
                    ahead.dve_normalise(dve, 0)
            if ahead:
                ahead.dve_split(dve, 0)

        @block.sync
        def _(sp):
            if load_next:
                load_next(sp)
            if out is not None:
                for b in range(B):
                    sp.wait_ge(added, b + 1)
                    sp.dma_start(out[b], env.x[:, b, :]).then_inc(stored, 16)
                sp.wait_ge(stored, 16 * B)


def build(nc, a, out, until=99):
    ctx = ExitStack()
    with ctx:
        env = make_env(nc, ctx)
        sb = env.scoped(ctx)
        env.x = sb("x", [P, B, D])
        env.ident = sb("ident", [P, P])
        env.nhalf = sb("nhalf", [P, B])
        at, used = place_rows()
        env.cols = [sb(f"cols{t}", [P, n]) for t, n in enumerate(used)]

        def col(name, first=0, n=None):
            t, r, rows = at[name]
            return env.cols[t][:, r + first:r + first + (rows if n is None else n)]

        env.col = col
        env.free = {name: sb("free_" + name, [P, D]) for name in FREE_VECTORS}
        env.ctx_hi, env.ctx_lo = sb("ctx_hi", [P, KC, TOK], F32R), sb("ctx_lo", [P, KC, TOK], F32R)
        env.h_hi, env.h_lo = sb("h_hi", [P, KC, TOK], F32R), sb("h_lo", [P, KC, TOK], F32R)
        env.norm_stats = (sb("norm_stats", [P, B, 6]), sb("norm_mv", [P, B, 2]), sb("norm_ve", [P, B]),
                          sb("norm_rstd", [P, B]))
        env.bn_scale, env.bn_shift = sb("bn_scale", [P, 1]), sb("bn_shift", [P, B])
        env.head_mask8, env.head_mask16 = sb("head_mask8", [P, 16]), sb("head_mask16", [P, 8])
        env.x_in, env.w0_in, env.mask_in = (env.lasting_sem(n) for n in ("x_in", "w0_in", "mask_in"))
        env.free_in, env.ff2_in, env.l3_in = (env.lasting_sem(n) for n in ("free_in", "ff2_in", "l3_in"))
        env.masks_made = env.lasting_sem("masks_made")
        with ExitStack() as late:
            lsb = env.scoped(late)

            def weights(shapes):
                return {name: lsb(name, [P, k, n]) for name, k, n in shapes}

            L = env.w_ff2 = weights((("L2_xattn_w_fc1", 2, 1024), ("L2_xattn_w_fc2", 8, 256)))

            between = late.enter_context(ExitStack())
            env.qT1 = env.scoped(between)("qT1", [P, B, P + 1])
            env.pair_weights = PairWeights(env, env.scoped(between), a)
            with ExitStack() as l0:
                zsb = env.scoped(l0)
                env.w_q0, env.w_o0 = zsb("w_q0", [P, KC, D]), zsb("w_o0", [P, KC, D])
                env.w_k0, env.w_v0 = zsb("w_k0", [P, KC, 64]), zsb("w_v0", [P, KC, 64])
                env.mask0 = zsb("mask0", [P, B, S])
                env.rows = [zsb(f"rows{t}", [P, P]) for t in range(len(used))]
                layer0(env, a)
            if until >= 2:
                long_head_attentions(env, a)
                free_semaphores(env)
            between.close()
            L3 = weights((("L3_xattn_w_qkv", 2, 768), ("L3_xattn_w_ao", 2, 256),
                          ("L3_xattn_w_q", 2, 256), ("L3_xattn_w_kv", 2, 512),
                          ("L3_xattn_w_co", 2, 256), ("L3_xattn_w1", 2, 1024), ("L3_xattn_w2", 8, 256)))
            env.mask_self, env.mask_cross = lsb("mask_self", [P, 1, S]), lsb("mask_cross", [P, B, S])

            def load_layer3(sp):
                load_weights(env, sp, a, L3, env.l3_in)
                sp.dma_start(env.mask_self[:, 0, :], a["mask_1x1xSxS2_fc1"][0, 0]).then_inc(env.l3_in, 16)
                sp.dma_start(env.mask_cross[:, :, :], a["mask_Bx1xSxS2_ff1"].rearrange("b o q s -> q (b o) s"))\
                    .then_inc(env.l3_in, 16)

            if until >= 4:
                feed_forward(env, "ff2", env.col("L2_xattn_ln_mlp_scale"), env.col("L2_xattn_ln_mlp_offset"),
                             L["L2_xattn_w_fc1"], L["L2_xattn_w_fc2"], env.col("L2_xattn_b_fc1"),
                             env.free["L2_xattn_b_fc2"], ACT.Gelu, w_in=(env.ff2_in, 32),
                             load_next=load_layer3,
                             ahead=(env.col("L3_xattn_ln1_s"), env.col("L3_xattn_ln1_b")) if until >= 5 else None)
            if until >= 5:
                layer3_attention(env, "sa", "ln1", "ln2", L3["L3_xattn_w_qkv"], None, "b_qkv", None,
                                 env.free["L3_xattn_b_ao"], L3["L3_xattn_w_ao"], env.mask_self, False)
            if until >= 6:
                layer3_attention(env, "ca", "ln2", "ln3", L3["L3_xattn_w_q"], L3["L3_xattn_w_kv"], "b_q", "b_kv",
                                 env.free["L3_xattn_b_co"], L3["L3_xattn_w_co"], env.mask_cross, True)
            if until >= 7:
                feed_forward(env, "ff3", env.col("L3_xattn_ln3_s"), env.col("L3_xattn_ln3_b"),
                             L3["L3_xattn_w1"], L3["L3_xattn_w2"], env.col("L3_xattn_b1"),
                             env.free["L3_xattn_b2"], ACT.Gelu_apprx_tanh, out=out)
            else:
                dump(env, out)


def wait(engine, sem, value):
    if not isinstance(value, int) or value > 0:
        engine.wait_ge(sem, value)


def dump(env, out):
    stored = env.sem("stored")
    with env.nc.Block() as block:
        @block.sync
        def _(sp):
            sp.dma_start(out.rearrange("b s d -> s b d"), env.x[:, :, :]).then_inc(stored, 16)
            sp.wait_ge(stored, 16)


def layer0(env, a):
    with ExitStack() as stack:
        sb = env.scoped(stack)
        q_all, k_all = sb("q_all0", [P, KC, TOK]), sb("k_all0", [P, KC, TOK])
        v_all = sb("v_all0", [P, B, KV_HEADS, HD0 + 1])
        norm = Norm(env, sb, "p0_ln", None, None, None, env.bank[6:8])
        wv_parts = sb("wv0_hi", [P, KC, 64], F32R), sb("wv0_lo", [P, KC, 64], F32R)
        parts = stack.enter_context(ExitStack())
        psb = env.scoped(parts)

        def parts_of(raw, name, n, by_pool):
            hi, lo = psb(name + "_hi", [P, KC, n], F32R), psb(name + "_lo", [P, KC, n], F32R)
            return Weights(raw, hi[:, :, :], lo[:, :, :], by_pool)

        wk_rep = psb("wk0_rep", [P, KC, 8, GROUP, HD0])
        wq = parts_of(env.w_q0[:, :, :], "wq0", D, False)
        wk = parts_of(wk_rep[:, :, :, :, :].rearrange("p c g j d -> p c (g j d)"), "wk0", D, True)
        wv = Weights(env.w_v0[:, :, :], wv_parts[0][:, :, :], wv_parts[1][:, :, :], False)
        spread = env.sem("wk0_spread")

        def repeat_keys(pool):
            for c in range(KC):
                pool.tensor_copy(wk_rep[:, c, :, :, :],
                                 env.w_k0[:, c, :].rearrange("p (g d) -> p g d", d=HD0).unsqueeze(2)
                                 .to_broadcast([P, 8, GROUP, HD0])).then_inc(spread, 1)
            pool.wait_ge(spread, KC)

        k = feature_products(env, wk, False, k_all, env.col("bk_of_heads"))
        q = feature_products(env, wq, True, q_all, env.col("L0_xattn_bq"))
        values = token_products(env, wv, False, v_all, KV_HEADS, HD0)
        early, jobs = k + values[:4], q + values[4:]
        before = Projection(env, "p0", norm, [wv, wq, wk], early, jobs, [],
                            len(early) + KC, env.free["L0_xattn_bo"], waits_act=[(env.w0_in, 64)],
                            waits_pool=[(env.w0_in, 64)],
                            pool_first=repeat_keys, ones=v_all[:, :, :, HD0:HD0 + 1])
        setup(env, a, before)
        parts.close()
        short_head_attention(env, "a0", 32, HD0, KV_HEADS, float(HD0) ** -0.5, env.mask0, True, False,
                             env.head_mask8, q_all, k_all, v_all, env.w_o0, env.col("bv_of_heads"), before,
                             late=a, parts_ready=True,
                             pool_after=env.pair_weights.pool_split_first,
                             norm_after=TokenNorm(env, "n0", 0, 1e-6, env.free["L0_xattn_gamma"],
                                                  env.free["L0_xattn_beta"]))


def layer3_attention(env, name, ln, next_ln, w_q, w_kv, b_q, b_kv, b_out, w_out, mask, per_sequence):
    heads, hd = 16, 16
    L3 = "L3_xattn_"
    with ExitStack() as stack:
        sb = env.scoped(stack)
        q_all, k_all = sb(name + "_q", [P, KC, TOK]), sb(name + "_k", [P, KC, TOK])
        v_all = sb(name + "_v", [P, B, heads, hd + 1])
        norm = Norm(env, sb, name + "_ln", env.col(L3 + ln + "_s"), env.col(L3 + ln + "_b"), 1e-5, env.bank[6:8],
                    halves=(1,))
        parts = stack.enter_context(ExitStack())
        psb = env.scoped(parts)

        def parts_of(raw, first, part, by_pool, alloc=psb):
            hi = alloc(f"{name}_w{part}_hi", [P, KC, D], F32R)
            lo = alloc(f"{name}_w{part}_lo", [P, KC, D], F32R)
            return Weights(raw[:, :, first * D:(first + 1) * D], hi[:, :, :], lo[:, :, :], by_pool)

        own = w_kv is None
        if own:
            wv = parts_of(w_q, 2, "v", False, sb)
            wq, wk = parts_of(w_q, 0, "q", False), parts_of(w_q, 1, "k", True)
            bq, bk, bv = (env.col(L3 + b_q, 2 * k, 2) for k in range(3))
        else:
            wv = parts_of(w_kv, 1, "v", True, sb)
            wq, wk = parts_of(w_q, 0, "q", False), parts_of(w_kv, 0, "k", False)
            bq = env.col(L3 + b_q)
            bk, bv = (env.col(L3 + b_kv, 2 * k, 2) for k in range(2))
        q = feature_products(env, wq, True, q_all, bq)
        k = feature_products(env, wk, own, k_all, bk)
        values = token_products(env, wv, own, v_all, heads, hd)
        if own:
            early, jobs, deferred = [], q[:KC] + k[:KC] + q[KC:] + k[KC:], values
            ready_half = 2 * KC
        else:
            early, jobs, deferred = k + values[:4], q, values[4:]
            ready_half = len(early) + KC
        parts.close()
        before = Projection(env, name + "_p", norm,
                            [wq, wk, wv] if own else [wk, wv, wq], early, jobs, deferred, ready_half, b_out, waits_act=[(env.l3_in, 16 * 9)],
                            waits_pool=[(env.l3_in, 16 * 9)], ones=v_all[:, :, :, hd:hd + 1])
        short_head_attention(env, name, heads, hd, heads, float(hd) ** -0.5, mask, per_sequence, True,
                             env.head_mask16, q_all, k_all, v_all, w_out, bv, before,
                             ahead=(env.col(L3 + next_ln + "_s"), env.col(L3 + next_ln + "_b")))


_OUT = (B, S, D)


def kernel(**inputs):
    import numpy as _np
    import concourse.bacc as _bacc
    from concourse import mybir as _mybir
    from concourse.bass_utils import run_bass_kernel_spmd as _run

    nc = _bacc.Bacc("TRN2", target_bir_lowering=False, num_devices=1)
    arrays, args = {}, {}
    for name, value in inputs.items():
        value = _np.ascontiguousarray(value)
        arrays[f"in_{name}"] = value
        args[name] = nc.dram_tensor(f"in_{name}", value.shape, _mybir.dt.from_np(value.dtype),
                                    kind="ExternalInput").ap()
    out = nc.dram_tensor("out_0", _OUT, F32, kind="ExternalOutput").ap()
    build(nc, args, out)
    r = _run(nc, [arrays], core_ids=[0])
    return r.results[0]["out_0"]
```
